# Optimizing a Trainium2 kernel written in Bass

```python
import numpy as np
import jax
import jax.numpy as jnp

def _softmax(x, axis=-1):
    return jax.nn.softmax(x, axis=axis)

def _gelu(x):
    return jax.nn.gelu(x, approximate=True)

def _silu(x):
    return jax.nn.silu(x)

def _sigmoid(x):
    return jax.nn.sigmoid(x)

def _layernorm(x, axis=-1, eps=1e-05):
    m = jnp.mean(x, axis=axis, keepdims=True)
    v = jnp.var(x, axis=axis, keepdims=True)
    return (x - m) / jnp.sqrt(v + eps)

def _scatter_add(tgt, idx, src, axis=0):
    return tgt.at[idx].add(src)

def _segment_sum(src, seg, n):
    return jax.ops.segment_sum(src, seg, n)
kernel_name = 'mk_adj_preln_d2_adj_r2_b9fc50'

def setup_inputs(seed: int=0):
    np.random.seed(seed)
    _w = jnp.asarray

    def _rec_inputs():
        import jax
        import jax.numpy as jnp
        _gk = jax.random.key(seed)
        x = -0.0005207 + 1.001 * jax.random.normal(jax.random.fold_in(_gk, 1), (8, 1024, 128), jnp.float32)
        _a = jax.random.bernoulli(jax.random.fold_in(_gk, 2), 0.00390625, (8, 1024, 1024))
        _a = jnp.logical_or(_a, jnp.swapaxes(_a, -1, -2))
        _a = jnp.logical_or(_a, jnp.eye(1024, dtype=bool))
        _af = _a.astype(jnp.float32)
        adj = _af
        return (x, adj)
    x, adj = _rec_inputs()

    def _L0_gnn_setup():
        import jax, jax.numpy as jnp
        import numpy as np
        DIM = 128
        HEADS = 8
        BS = 8
        N = 512
        NEG = -1000000000.0
        key = jax.random.key(seed)
        ks = jax.random.split(key, 8)
        feats = jax.random.normal(ks[0], (BS, N, DIM), dtype=jnp.float32)
        adj_mat = (jax.random.uniform(ks[1], (BS, N, N)) < 0.1).astype(jnp.float32)
        s = 1.0 / np.sqrt(DIM)
        fc_w = jax.random.normal(ks[2], (DIM, DIM * HEADS), dtype=jnp.float32) * s
        fc_b = jnp.zeros((DIM * HEADS,), dtype=jnp.float32)
        q_w = jax.random.normal(ks[3], (DIM, 1), dtype=jnp.float32) * s
        q_b = jnp.zeros((1,), dtype=jnp.float32)
        k_w = jax.random.normal(ks[4], (DIM, 1), dtype=jnp.float32) * s
        k_b = jnp.zeros((1,), dtype=jnp.float32)
        fp_w = jax.random.normal(ks[5], (DIM * HEADS, DIM), dtype=jnp.float32) * (1.0 / np.sqrt(DIM * HEADS))
        fp_b = jnp.zeros((DIM,), dtype=jnp.float32)
        return {'feats': feats, 'adj_mat': adj_mat, 'fc_w': fc_w, 'fc_b': fc_b, 'q_w': q_w, 'q_b': q_b, 'k_w': k_w, 'k_b': k_b, 'fp_w': fp_w, 'fp_b': fp_b}
    _L0_gnn_all = _L0_gnn_setup()
    _L0_gnn_in = {k: v for k, v in _L0_gnn_all.items() if k in ('fc_w', 'fc_b', 'q_w', 'q_b', 'k_w', 'k_b', 'fp_w', 'fp_b')}
    del _L0_gnn_all

    def _L1_gnn_setup():
        import jax, jax.numpy as jnp
        import numpy as np
        from jax import lax
        DIM = 128
        EPS = 1e-05

        def _bn(h, g, b, m, v):
            scale = g / jnp.sqrt(v + EPS)
            return h * scale[None, :, None] + (b - m * scale)[None, :, None]

        def _conv1d(h, w, pad):
            return lax.conv_general_dilated(h, w, window_strides=(1,), padding=[(pad, pad)], dimension_numbers=('NCH', 'OIH', 'NCH'))
        key = jax.random.key(seed)
        ks = jax.random.split(key, 16)
        bs, n, d = (16, 1024, DIM)
        s = 0.05
        return {'x': jax.random.normal(ks[0], (bs, n, d), jnp.float32), 'mask': jnp.ones((bs, n, n), jnp.float32), 'w_se': jax.random.normal(ks[1], (3, d), jnp.float32) * s, 'b_se': jnp.zeros((3,), jnp.float32), 'conv1_w': jax.random.normal(ks[2], (d, d, 1), jnp.float32) * s, 'bn1_g': jnp.ones((d,), jnp.float32), 'bn1_b': jnp.zeros((d,), jnp.float32), 'bn1_m': jnp.zeros((d,), jnp.float32), 'bn1_v': jnp.ones((d,), jnp.float32), 'conv2_w': jax.random.normal(ks[3], (d, d, 17), jnp.float32) * s, 'bn2_g': jnp.ones((d,), jnp.float32), 'bn2_b': jnp.zeros((d,), jnp.float32), 'bn2_m': jnp.zeros((d,), jnp.float32), 'bn2_v': jnp.ones((d,), jnp.float32), 'w_msg': jax.random.normal(ks[4], (d, d), jnp.float32) * s, 'b_msg': jnp.zeros((d,), jnp.float32), 'w_ih': jax.random.normal(ks[5], (3 * d, 2 * d), jnp.float32) * s, 'b_ih': jnp.zeros((3 * d,), jnp.float32), 'w_hh': jax.random.normal(ks[6], (3 * d, d), jnp.float32) * s, 'b_hh': jnp.zeros((3 * d,), jnp.float32)}
    _L1_gnn_all = _L1_gnn_setup()
    _L1_gnn_in = {k: v for k, v in _L1_gnn_all.items() if k in ('w_se', 'b_se', 'conv1_w', 'bn1_g', 'bn1_b', 'bn1_m', 'bn1_v', 'conv2_w', 'bn2_g', 'bn2_b', 'bn2_m', 'bn2_v', 'w_msg', 'b_msg', 'w_ih', 'b_ih', 'w_hh', 'b_hh')}
    del _L1_gnn_all
    return {'x': x, 'adj': adj, 'L0_gnn_fc_w': _L0_gnn_in['fc_w'], 'L0_gnn_fc_b': _L0_gnn_in['fc_b'], 'L0_gnn_q_w': _L0_gnn_in['q_w'], 'L0_gnn_q_b': _L0_gnn_in['q_b'], 'L0_gnn_k_w': _L0_gnn_in['k_w'], 'L0_gnn_k_b': _L0_gnn_in['k_b'], 'L0_gnn_fp_w': _L0_gnn_in['fp_w'], 'L0_gnn_fp_b': _L0_gnn_in['fp_b'], 'L1_gnn_w_se': _L1_gnn_in['w_se'], 'L1_gnn_b_se': _L1_gnn_in['b_se'], 'L1_gnn_conv1_w': _L1_gnn_in['conv1_w'], 'L1_gnn_bn1_g': _L1_gnn_in['bn1_g'], 'L1_gnn_bn1_b': _L1_gnn_in['bn1_b'], 'L1_gnn_bn1_m': _L1_gnn_in['bn1_m'], 'L1_gnn_bn1_v': _L1_gnn_in['bn1_v'], 'L1_gnn_conv2_w': _L1_gnn_in['conv2_w'], 'L1_gnn_bn2_g': _L1_gnn_in['bn2_g'], 'L1_gnn_bn2_b': _L1_gnn_in['bn2_b'], 'L1_gnn_bn2_m': _L1_gnn_in['bn2_m'], 'L1_gnn_bn2_v': _L1_gnn_in['bn2_v'], 'L1_gnn_w_msg': _L1_gnn_in['w_msg'], 'L1_gnn_b_msg': _L1_gnn_in['b_msg'], 'L1_gnn_w_ih': _L1_gnn_in['w_ih'], 'L1_gnn_b_ih': _L1_gnn_in['b_ih'], 'L1_gnn_w_hh': _L1_gnn_in['w_hh'], 'L1_gnn_b_hh': _L1_gnn_in['b_hh']}

def reference(x, adj, L0_gnn_fc_w, L0_gnn_fc_b, L0_gnn_q_w, L0_gnn_q_b, L0_gnn_k_w, L0_gnn_k_b, L0_gnn_fp_w, L0_gnn_fp_b, L1_gnn_w_se, L1_gnn_b_se, L1_gnn_conv1_w, L1_gnn_bn1_g, L1_gnn_bn1_b, L1_gnn_bn1_m, L1_gnn_bn1_v, L1_gnn_conv2_w, L1_gnn_bn2_g, L1_gnn_bn2_b, L1_gnn_bn2_m, L1_gnn_bn2_v, L1_gnn_w_msg, L1_gnn_b_msg, L1_gnn_w_ih, L1_gnn_b_ih, L1_gnn_w_hh, L1_gnn_b_hh):
    import jax
    import jax.numpy as jnp

    def _L0_gnn_ref(feats, adj_mat, fc_w, fc_b, q_w, q_b, k_w, k_b, fp_w, fp_b):
        import jax, jax.numpy as jnp
        import numpy as np
        DIM = 128
        HEADS = 8
        BS = 8
        N = 512
        NEG = -1000000000.0
        bs, n, dim = feats.shape
        feat_proj = (feats @ fc_w + fc_b).reshape(bs, n, HEADS, dim).transpose(0, 2, 1, 3)
        q = feat_proj @ q_w + q_b
        k = feat_proj @ k_w + k_b
        logits = q + jnp.swapaxes(k, -1, -2)
        masked = logits + (1.0 - adj_mat[:, None]) * NEG
        masked = jax.nn.leaky_relu(masked, negative_slope=0.01)
        attn = jax.nn.softmax(masked, axis=-1)
        out = attn @ feat_proj
        out = out.transpose(0, 2, 1, 3).reshape(bs, n, HEADS * dim)
        out = out @ fp_w + fp_b + feats
        return jax.nn.sigmoid(out)

    def _L1_gnn_ref(x, mask, w_se, b_se, conv1_w, bn1_g, bn1_b, bn1_m, bn1_v, conv2_w, bn2_g, bn2_b, bn2_m, bn2_v, w_msg, b_msg, w_ih, b_ih, w_hh, b_hh):
        import jax, jax.numpy as jnp
        import numpy as np
        from jax import lax
        DIM = 128
        EPS = 1e-05

        def _bn(h, g, b, m, v):
            scale = g / jnp.sqrt(v + EPS)
            return h * scale[None, :, None] + (b - m * scale)[None, :, None]

        def _conv1d(h, w, pad):
            return lax.conv_general_dilated(h, w, window_strides=(1,), padding=[(pad, pad)], dimension_numbers=('NCH', 'OIH', 'NCH'))
        d = x.shape[-1]
        xc = jnp.transpose(x, (0, 2, 1))
        h = _bn(_conv1d(xc, conv1_w, 0), bn1_g, bn1_b, bn1_m, bn1_v)
        h = jax.nn.relu(h)
        h = _bn(_conv1d(h, conv2_w, 8), bn2_g, bn2_b, bn2_m, bn2_v)
        x_conv = jnp.transpose(jax.nn.relu(h + xc), (0, 2, 1))
        s = x @ w_se.T + b_se
        sq = jnp.sum(s * s, axis=-1)
        dist = sq[:, :, None] + sq[:, None, :] - 2.0 * jnp.einsum('bnd,bmd->bnm', s, s)
        A = jnp.exp(-dist) * mask
        msg = jax.nn.relu(x @ w_msg.T + b_msg)
        x_nmp = jnp.einsum('bnm,bmd->bnd', A, msg)
        x_in = jnp.concatenate([x_conv, x_nmp], axis=-1)
        gi = x_in @ w_ih.T + b_ih
        gh = x @ w_hh.T + b_hh
        gi_r, gi_z, gi_n = (gi[..., :d], gi[..., d:2 * d], gi[..., 2 * d:])
        gh_r, gh_z, gh_n = (gh[..., :d], gh[..., d:2 * d], gh[..., 2 * d:])
        r = jax.nn.sigmoid(gi_r + gh_r)
        z = jax.nn.sigmoid(gi_z + gh_z)
        nn_ = jnp.tanh(gi_n + r * gh_n)
        return (1.0 - z) * nn_ + z * x
    h = jnp.maximum(_layernorm(x, axis=-1), 0.0)
    x = x + _L0_gnn_ref(h, adj, L0_gnn_fc_w, L0_gnn_fc_b, L0_gnn_q_w, L0_gnn_q_b, L0_gnn_k_w, L0_gnn_k_b, L0_gnn_fp_w, L0_gnn_fp_b)
    h = jnp.maximum(_layernorm(x, axis=-1), 0.0)
    x = x + _L1_gnn_ref(h, adj, L1_gnn_w_se, L1_gnn_b_se, L1_gnn_conv1_w, L1_gnn_bn1_g, L1_gnn_bn1_b, L1_gnn_bn1_m, L1_gnn_bn1_v, L1_gnn_conv2_w, L1_gnn_bn2_g, L1_gnn_bn2_b, L1_gnn_bn2_m, L1_gnn_bn2_v, L1_gnn_w_msg, L1_gnn_b_msg, L1_gnn_w_ih, L1_gnn_b_ih, L1_gnn_w_hh, L1_gnn_b_hh)
    return x

_drawn_inputs = setup_inputs


def setup_inputs(seed=0):
    import zlib

    import numpy as np

    out = dict(_drawn_inputs(seed))
    spreads = {'L0_gnn_fc_b': (0.0, 0.47),
     'L0_gnn_fp_b': (0.0, 0.491),
     'L1_gnn_b_se': (0.0, 0.8),
     'L1_gnn_bn1_g': (1.0, 0.6),
     'L1_gnn_bn1_b': (0.0, 0.428),
     'L1_gnn_bn1_m': (0.0, 0.398),
     'L1_gnn_bn1_v': (1.0, 0.6),
     'L1_gnn_bn2_g': (1.0, 0.6),
     'L1_gnn_bn2_b': (0.0, 0.748),
     'L1_gnn_bn2_m': (0.0, 0.62),
     'L1_gnn_bn2_v': (1.0, 0.6),
     'L1_gnn_b_msg': (0.0, 0.1),
     'L1_gnn_b_ih': (0.0, 0.319),
     'L1_gnn_b_hh': (0.0, 0.492)}
    factors = {'L0_gnn_q_w': 8.0, 'L0_gnn_k_w': 4.163}
    for name, (base, spread) in spreads.items():
        noise = np.random.default_rng([zlib.crc32(name.encode()), seed]).standard_normal(out[name].shape)
        drawn = base * np.exp(spread * noise) if base else spread * noise
        out[name] = jnp.asarray(drawn.astype(out[name].dtype))
    for name, factor in factors.items():
        out[name] = (out[name] * factor).astype(out[name].dtype)
    return out
```

```python
import math
from contextlib import ExitStack

import concourse.bass as bass
from concourse import mybir

F32 = mybir.dt.float32
BF16 = mybir.dt.bfloat16
ALU = mybir.AluOpType
ACT = mybir.ActivationFunctionType
AX = mybir.AxisListType

P = 128
RING = 12
TAPS = 17
PAD = TAPS // 2
EPS = 1e-5
SLOPE = 0.01
HALF_C = math.exp(30.0)
HALF_SPAN = (1.0 - SLOPE) / 2


def wait(eng, sem, value):
    if isinstance(value, int) and value <= 0:
        return
    eng.wait_ge(sem, value)


def wait_apart(eng, sem, value, passed):
    eng.wait_ge(sem, value)
    eng.sem_inc(passed, 1)


def build(nc, x, adj, fc_w, fc_b, q_w, q_b, k_w, k_b, fp_w, fp_b, w_se, b_se, conv1_w, bn1_g, bn1_b, bn1_m,
          bn1_v, conv2_w, bn2_g, bn2_b, bn2_m, bn2_v, w_msg, b_msg, w_ih, b_ih, w_hh, b_hh, out):
    B, N, D = x.shape
    H = fc_w.shape[1] // D
    T = N // P
    HALF = N // 2
    W = D + 1
    S = w_se.shape[0]
    LAST = B - 1
    assert D == P and H == 8 and T == 8 and HALF == 512 and B % 2 == 0
    AM_SPLIT = T // 2
    PER = (H + 1) * T

    HEAD_AT = [0, 8, 16, 24, 36, 48, 56, 64]
    KERNEL_AT = [32, 33, 34, 35, 44, 45, 46, 47]

    def frame_start(b):
        return PER * b - T

    def tile_pos(b, h):
        if isinstance(b, int) and b == 0:
            return T * h
        return frame_start(b) + HEAD_AT[h]

    def kernel_tile_pos(b, m):
        if isinstance(b, int) and b == LAST:
            return frame_start(b + 1) + m
        return frame_start(b + 1) + KERNEL_AT[m]

    def used(b, at):
        if at in KERNEL_AT[AM_SPLIT:]:
            at -= T
        elif HEAD_AT[4] <= at < HEAD_AT[4] + T:
            at += AM_SPLIT
        return frame_start(b) + at + 1

    def head_used(b, h, t):
        if isinstance(b, int) and b == 0:
            return T * h + t + 1
        return used(b, HEAD_AT[h] + t)

    def place_free(b, at):
        return used(b, at - RING)

    def tile_slot(pos0, t):
        return (pos0 + t) % RING

    def head_slot(b, h, t):
        return tile_slot(tile_pos(b if isinstance(b, int) else 1, h), t)

    def kernel_slot(b, m):
        return tile_slot(kernel_tile_pos(b if isinstance(b, int) else 0, m), 0)

    with ExitStack() as ctx:
        def sb(name, shape, dt=F32):
            return ctx.enter_context(nc.sbuf_tensor(name, shape, dt))

        def psum(name, shape):
            return ctx.enter_context(nc.psum_tensor(name, shape, F32))

        def sem(name):
            return ctx.enter_context(nc.semaphore(name))

        ring = sb("ring", [P, RING, N])
        adj_t = [sb(f"adj_t{i}", [P, T, N], BF16) for i in range(2)]
        adj_rows = sb("adj_rows", [P, T // 2, N], BF16)
        x_in = [sb(f"x_in{i}", [P, T, D]) for i in range(2)]
        h0 = sb("h0", [P, T, D])
        h0_t = [sb(f"h0_t{i}", [P, N]) for i in range(2)]
        y = sb("y", [P, T, D])
        values = [sb(f"values{i}", [P, T, W]) for i in range(2)]
        r_half = sb("r_half", [P, N])
        r_row = [sb(f"r_row{i}", [P, N]) for i in range(2)]
        k_sb = sb("k_sb", [P, T, H])
        k_low = sb("k_low", [P, T, H])
        p_half = sb("p_half", [P, T, H])
        p_col = [sb(f"p_col{i}", [P, T, H]) for i in range(2)]
        v_col = [sb(f"v_col{i}", [P, T, H]) for i in range(2)]
        r_bias = [sb(f"r_bias{i}", [P, H]) for i in range(2)]
        r_bias_raw = sb("r_bias_raw", [P, H])
        k_part = sb("k_part", [P, H])
        k_max = sb("k_max", [H, 1])
        k_diag = sb("k_diag", [H, H])
        k_shift = sb("k_shift", [P, H])
        rden = sb("rden", [P, T + 1])
        x1 = sb("x1", [P, T, D])
        h1 = sb("h1", [P, T, D])
        msg = h1
        h1_t = sb("h1_t", [P, N])
        dist_l = sb("dist_l", [P, N])
        dist_r = sb("dist_r", [P, N])
        conv_in = sb("conv_in", [P, N + 2 * PAD])
        kern = [sb(f"kern{i}", [P, N]) for i in range(2)]
        nmp_t = sb("nmp_t", [P, N])
        conv_t = sb("conv_t", [P, N])
        out_sb = conv_t[:, :].rearrange("p (t d) -> p t d", t=T)
        gate_a = sb("gate_a", [P, N])
        gate_z = sb("gate_z", [P, N])
        diff_t = h1[:, :, :].rearrange("p t d -> p (t d)")
        y_tanh = gate_a[:, :].rearrange("p (t d) -> p t d", t=T)
        ln = []
        for i in range(2):
            ln.append(dict(stats=sb(f"ln{i}_stats", [P, T, 6]), mv=sb(f"ln{i}_mv", [P, T, 2]),
                           var=sb(f"ln{i}_var", [P, T]), rstd=sb(f"ln{i}_rstd", [P, T]),
                           s_stats=sem(f"ln{i}_stats_ready"), s_mv=sem(f"ln{i}_moments_ready"),
                           s_var=sem(f"ln{i}_var_ready"), s_rstd=sem(f"ln{i}_rstd_ready"),
                           s_mid=sem(f"ln{i}_normalised"), s_out=sem(f"ln{i}_relu_ready")))

        ident = sb("ident", [P, P])
        ones = sb("ones", [P, P])
        minus_half = sb("minus_half", [P, T])
        w_val = sb("w_val", [P, H, D])
        w_query = sb("w_query", [P, H, P])
        w_key = sb("w_key", [P, H])
        b_query = sb("b_query", [P, H])
        b_key = sb("b_key", [P, H])
        b_out = sb("b_out", [P, D])
        w_dist = sb("w_dist", [P, 3 * 32])
        b_dist = sb("b_dist", [3 * 32, 2])
        conv1_t = sb("conv1_t", [P, D])
        conv2_t = sb("conv2_t", [P, TAPS, D])
        w_msg_t = sb("w_msg_t", [P, D])
        b_msg_row = sb("b_msg_row", [P, D])
        w_ih_t = sb("w_ih_t", [P, 2, 3 * D])
        w_hh_t = sb("w_hh_t", [P, 3 * D])
        bn = sb("bn", [P, 2, 4])
        bn_aff = sb("bn_aff", [P, 2, 2])
        bn_tmp = sb("bn_tmp", [P, 2, 2])
        b_gate_in = sb("b_gate_in", [P, 2, 3])
        b_gate = sb("b_gate", [P, 2])
        qk_b = sb("qk_b", [P, 2])

        room = ring[:, :, :].rearrange("p r n -> p (r n)")
        taken = 0

        def raw(cols):
            nonlocal taken
            taken += cols
            assert taken <= RING * N
            return room[:, taken - cols:taken]

        fc_raw = raw(H * D)
        fp_raw = raw(H * D).rearrange("p (h d) -> p h d", h=H)
        ih_raw = raw(3 * 2 * D).rearrange("p (g i) -> p g i", g=3)
        hh_raw = raw(3 * D).rearrange("p (g i) -> p g i", g=3)
        msg_raw = raw(D)
        conv1_raw = raw(D)
        conv2_raw = raw(D * TAPS).rearrange("p (i k) -> p i k", k=TAPS)
        se_raw = raw(D)
        fc_t = raw(H * D).rearrange("p (h i) -> p h i", h=H)
        fcb_raw = raw(H)
        qk_raw = raw(2)
        q_rep = raw(P)
        k_rep = raw(P)
        fcb_rep = raw(H * P).rearrange("p (h c) -> p h c", h=H)

        o_ps = psum("o_ps", [P, 3, 512])
        slot_a = psum("slot_a", [P, N])
        slot_b = psum("slot_b", [P, N])
        small = psum("small", [P, 512])
        kq_ps = small[:, 0:T * H].rearrange("p (t h) -> p t h", t=T)
        kt_ps = small[0:H, 64:64 + P]
        km_ps = small[:, 192:192 + H]
        bias_ps = small[:, 256:256 + 3 * H]
        bout_ps = small[:, 384:384 + D]

        def o_block(n):
            return o_ps[:, n // 3, (n % 3) * W:(n % 3 + 1) * W]

        consts_ready = sem("consts_ready")
        w_loaded = sem("w_loaded")
        w_reps_ready = sem("w_reps_ready")
        setup_filled = sem("setup_filled")
        setup_copied = sem("setup_copied")
        bias_ready = sem("bias_ready")
        bn_step = sem("bn_step")
        passed = {e: sem(f"{e}_waits_passed") for e in ("sync", "pool", "vector")}
        x_loaded = sem("x_loaded")
        adj_cast = sem("adj_cast")
        adj_turned = sem("adj_turned")
        h0_turned = sem("h0_turned")
        h0_t_ready = sem("h0_t_ready")
        k_scored = sem("k_scored")
        k_ready = sem("k_ready")
        k_part_ready = sem("k_part_ready")
        k_part_turned = sem("k_part_turned")
        k_max_ready = sem("k_max_ready")
        k_diag_ready = sem("k_diag_ready")
        k_max_spread = sem("k_max_spread")
        k_shift_ready = sem("k_shift_ready")
        r_bias_raw_ready = sem("r_bias_raw_ready")
        k_low_ready = sem("k_low_ready")
        p_half_ready = sem("p_half_ready")
        pv_ready = sem("pv_ready")
        q_spread = sem("q_spread")
        q_clamped = sem("q_clamped")
        r_half_ready = sem("r_half_ready")
        r_ready = sem("r_ready")
        z_ready = sem("z_ready")
        values_ready = sem("values_ready")
        tile_filled = sem("tile_filled")
        tile_used = sem("tile_used")
        rden_ready = sem("rden_ready")
        head_added = sem("head_added")
        y_ready = sem("y_ready")
        y_tanh_ready = sem("y_tanh_ready")
        x1_half_ready = sem("x1_half_ready")
        x1_ready = sem("x1_ready")
        h1_turned = sem("h1_turned")
        h1_t_ready = sem("h1_t_ready")
        s_product = sem("s_product")
        s_read = sem("s_read")
        dist_ready = sem("dist_ready")
        conv1_product = sem("conv1_product")
        conv_in_ready = sem("conv_in_ready")
        msg_product = sem("msg_product")
        msg_added = sem("msg_added")
        msg_ready = sem("msg_ready")
        dist_product = sem("dist_product")
        kern_ready = sem("kern_ready")
        nmp_ready = sem("nmp_ready")
        conv2_product = sem("conv2_product")
        conv2_added = sem("conv2_added")
        conv_ready = sem("conv_ready")
        gate_r_product = sem("gate_r_product")
        gate_z_product = sem("gate_z_product")
        gate_h_product = sem("gate_h_product")
        gate_n_product = sem("gate_n_product")
        r_tanh_ready = sem("r_tanh_ready")
        z_tanh_ready = sem("z_tanh_ready")
        gate_r_ready = sem("gate_r_ready")
        gate_h_added = sem("gate_h_added")
        gate_n_added = sem("gate_n_added")
        n_ready = sem("n_ready")
        diff_ready = sem("diff_ready")
        z_diff_ready = sem("z_diff_ready")
        gru_ready = sem("gru_ready")
        gru_turned = sem("gru_turned")
        out_ready = sem("out_ready")
        out_stored = sem("out_stored")

        def blocks(dram, b):
            return dram[b].rearrange("(t p) d -> p t d", p=P)

        def block(buf, t):
            return buf[:, t * P:(t + 1) * P]

        def half(buf, i):
            return buf[:, i * HALF:(i + 1) * HALF]

        def frames(eng, frame):
            frame(0, 0, False, True)
            frame(1, 1, True, True)
            with eng.Fori(0, (B - 4) // 2) as pair:
                b = pair * 2 + 2
                frame(b, 0, True, True)
                frame(b + 1, 1, True, True)
            frame(LAST - 1, 0, True, True)
            frame(LAST, 1, True, False)

        def steps(b, prev, next_):
            for h in range(H):
                following = (b, h + 1) if h + 1 < H else (b + 1, 0)
                yield h, (following if h + 1 < H or next_ else None)

        (J_FC, J_IH, J_HH, J_TAPS0, J_TAPS1, J_TAPS2, J_VAL, J_QUERY, J_SMALL) = range(9)
        SETUP_JOBS = 9
        job_slot = [slot_a, slot_b, slot_a, slot_b, slot_a, slot_b, slot_a, slot_b, small]
        N_LOADS = 28

        blk = ctx.enter_context(nc.Block())

        @blk.sync
        def _(sp):
            def load(dst, src):
                sp.dma_start(dst, src).then_inc(w_loaded, 16)

            def col(v):
                return v.rearrange("(p a) -> p a", a=1)

            sp.dma_start(x_in[0][:, :, :], blocks(x, 0)).then_inc(x_loaded, 16)
            load(fc_raw, fc_w)
            load(fp_raw, fp_w.rearrange("(h k) d -> k h d", k=D))
            load(ih_raw, w_ih.rearrange("(g p) i -> p g i", p=P))
            load(hh_raw, w_hh.rearrange("(g p) i -> p g i", p=P))
            load(msg_raw, w_msg)
            load(conv1_raw, conv1_w.rearrange("o i k -> o (i k)"))
            load(conv2_raw, conv2_w)
            load(se_raw[0:S, :], w_se)
            load(qk_raw[:, 0:1], q_w)
            load(qk_raw[:, 1:2], k_w)
            for i, vec in enumerate((bn1_g, bn1_b, bn1_m, bn1_v, bn2_g, bn2_b, bn2_m, bn2_v)):
                load(bn[:, i // 4, i % 4:i % 4 + 1], col(vec))
            load(qk_b[:, 0:1], q_b.rearrange("(a n) -> a n", a=1).to_broadcast([P, 1]))
            load(qk_b[:, 1:2], k_b.rearrange("(a n) -> a n", a=1).to_broadcast([P, 1]))
            load(b_out[:, :], fp_b.rearrange("(a n) -> a n", a=1).to_broadcast([P, D]))
            load(b_msg_row[:, :], b_msg.rearrange("(a n) -> a n", a=1).to_broadcast([P, D]))
            with nc.allow_non_contiguous_dma(reason="bias vectors of a few hundred numbers, once"):
                load(fcb_raw, fc_b.rearrange("(h k) -> k h", k=D))
                load(b_gate_in[:, 0, :], b_ih.rearrange("(g p) -> p g", p=P))
                load(b_gate_in[:, 1, :], b_hh.rearrange("(g p) -> p g", p=P))
                sp.wait_ge(consts_ready, 8)
                for q in range(3):
                    load(b_dist[32 * q:32 * q + S, 0:1], b_se.rearrange("(p a) -> p a", a=1))

            def turn_adj(b, parity, first_wait):
                for i in range(2):
                    first_wait(i)
                    for t in range(T // 2):
                        n0 = (i * T // 2 + t) * P
                        sp.dma_start_transpose(adj_t[parity][:, :, n0:n0 + P],
                                               adj_rows[:, t, :]).then_inc(adj_turned, 16)

            turn_adj(0, 0, lambda i: sp.wait_ge(adj_cast, 16 * (i + 1)))

            def frame(b, parity, prev, next_):
                if next_:
                    nb, other = b + 1, 1 - parity
                    wait(sp, x1_ready, b)
                    sp.dma_start(x_in[other][:, :, :], blocks(x, nb)).then_inc(x_loaded, 16)
                    if prev:
                        wait_apart(sp, tile_filled, kernel_tile_pos(b - 1, T - 1) + 1, passed["sync"])
                    turn_adj(nb, other, lambda i: wait_apart(sp, adj_cast, 32 * nb + 16 * (i + 1), passed["sync"]))
                if prev:
                    sp.wait_ge(out_ready, b)
                    sp.dma_start(blocks(out, b - 1), out_sb).then_inc(out_stored, 16)

            frames(sp, frame)
            sp.wait_ge(out_ready, B)
            sp.dma_start(blocks(out, LAST), out_sb).then_inc(out_stored, 16)
            sp.wait_ge(out_stored, 16 * B)

        @blk.gpsimd
        def _(pool):
            def load_adj(b, i):
                rows = adj[b].rearrange("(s t p) m -> s p t m", p=P, s=2)
                wait(pool, adj_turned, 16 * T * b + 8 * T * i)
                pool.dma_start(adj_rows[:, :, :], rows[i]).then_inc(adj_cast, 16)

            pool.memset(ident[:, :], 0.0).then_inc(consts_ready, 1)
            pool.memset(b_dist[:, :], 0.0).then_inc(consts_ready, 1)
            pool.memset(ones[:, :], 1.0).then_inc(consts_ready, 1)
            pool.memset(minus_half[:, :], -0.5).then_inc(consts_ready, 1)
            pool.memset(w_dist[:, :], 0.0).then_inc(consts_ready, 1)
            pool.memset(conv_in[:, :], 0.0).then_inc(consts_ready, 1)
            pool.memset(dist_l[:, :], 0.0).then_inc(consts_ready, 1)
            pool.memset(dist_r[:, :], 0.0).then_inc(consts_ready, 1)
            pool.wait_ge(consts_ready, 8)
            pool.affine_select(out=ident[:, :], in_=ident[:, :], compare_op=ALU.not_equal, fill=1.0, base=0,
                               pattern=[[-1, P]], channel_multiplier=1).then_inc(consts_ready, 1)
            pool.wait_ge(consts_ready, 9)
            pool.memset(dist_l[32:32 + S, :], -1.0).then_inc(consts_ready, 1)
            pool.wait_ge(consts_ready, 10)
            pool.memset(dist_r[64:64 + S, :], 1.0).then_inc(consts_ready, 1)
            pool.wait_ge(consts_ready, 11)
            load_adj(0, 0)
            load_adj(0, 1)

            pool.wait_ge(bn_step, 1)
            pool.tensor_tensor(bn_tmp[:, :, 1], bn_tmp[:, :, 0], minus_half[:, 0:2], ALU.pow).then_inc(bn_step, 1)

            def rstd(layer, b):
                s = ln[layer]
                wait_apart(pool, s["s_mv"], b + 1, passed["pool"])
                pool.tensor_scalar(s["var"][:, :], s["mv"][:, :, 1], EPS, None, ALU.add).then_inc(s["s_var"], 1)
                pool.wait_ge(s["s_var"], b + 1)
                pool.tensor_tensor(s["rstd"][:, :], s["var"][:, :], minus_half[:, :],
                                   ALU.pow).then_inc(s["s_rstd"], 1)

            def start_y(b):
                pool.wait_ge(ln[0]["s_out"], b + 1)
                wait(pool, y_tanh_ready, b)
                pool.tensor_tensor(y[:, :, :], h0[:, :, :], b_out[:, None, :].to_broadcast([P, T, D]),
                                   ALU.add).then_inc(y_ready, 1)

            rstd(0, 0)
            pool.wait_ge(bias_ready, 5)

            def frame(b, parity, prev, next_):
                start_y(b)
                if next_:
                    load_adj(b + 1, 0)
                if prev:
                    rstd(1, b - 1)
                if next_:
                    rstd(0, b + 1)
                    load_adj(b + 1, 1)

            frames(pool, frame)
            rstd(1, LAST)

        @blk.tensor
        def _(pe):
            def job(j, needs=0):
                if max(j - 1, needs) > 0:
                    pe.wait_ge(setup_copied, max(j - 1, needs))
                return job_slot[j]

            pe.wait_ge(consts_ready, 11)
            pe.wait_ge(w_loaded, 16 * N_LOADS)
            s = job(J_FC)
            for h in range(H):
                last = pe.transpose(block(s, h), block(fc_raw, h), ident[:, :])
            last.then_inc(setup_filled, 1)
            s = job(J_IH)
            for g in range(3):
                for i in range(2):
                    pe.transpose(block(s, 3 * i + g), block(ih_raw[:, g, :], i), ident[:, :])
            pe.transpose(block(s, 6), msg_raw, ident[:, :])
            pe.transpose(block(s, 7), conv1_raw, ident[:, :]).then_inc(setup_filled, 1)
            s = job(J_HH)
            for g in range(3):
                pe.transpose(block(s, g), hh_raw[:, g, :], ident[:, :])
            pe.transpose(s[:, 3 * P:3 * P + S], se_raw[0:S, :], ident[0:S, 0:S]).then_inc(setup_filled, 1)
            for j, k0 in ((J_TAPS0, 0), (J_TAPS1, 8), (J_TAPS2, 16)):
                s = job(j)
                for k in range(k0, min(k0 + 8, TAPS)):
                    last = pe.transpose(block(s, k - k0), conv2_raw[:, :, k], ident[:, :])
                last.then_inc(setup_filled, 1)
            s = job(J_VAL)
            for h in range(H):
                last = pe.matmul(block(s, h), fc_t[:, h, :], fp_raw[:, h, :], start=True, stop=True)
            last.then_inc(setup_filled, 1)
            pe.wait_ge(w_reps_ready, 3)
            s = job(J_QUERY)
            for h in range(H):
                last = pe.matmul(block(s, h), fc_t[:, h, :], q_rep, start=True, stop=True)
            last.then_inc(setup_filled, 1)
            for h in range(H):
                pe.matmul(bias_ps[:, h:h + 1], fc_t[:, h, :], qk_raw[:, 1:2], start=True, stop=True)
            pe.matmul(bias_ps[:, H:2 * H], q_rep, fcb_raw, start=True, stop=True)
            pe.matmul(bias_ps[:, 2 * H:3 * H], k_rep, fcb_raw, start=True, stop=True)
            for h in range(H):
                last = pe.matmul(bout_ps, fcb_rep[:, h, :], fp_raw[:, h, :], start=(h == 0), stop=(h == H - 1))
            last.then_inc(setup_filled, 1)

            def turn_h0(b, after):
                pe.wait_ge(ln[0]["s_out"], b + 1)
                wait(pe, *after)
                for t in range(T):
                    last = pe.transpose(block(slot_b, t), h0[:, t, :], ident[:, :])
                last.then_inc(h0_turned, 1)

            def key_scores(b, parity):
                pe.wait_ge(h0_t_ready, b + 1)
                wait(pe, k_shift_ready, b)
                for t in range(T):
                    last = pe.matmul(kq_ps[:, t, :], block(h0_t[parity], t), w_key[:, :], start=True, stop=True)
                last.then_inc(k_scored, 1)

            def turn_key_max(b):
                pe.wait_ge(k_part_ready, b + 1)
                pe.transpose(kt_ps, k_part[:, :], ident[:, :]).then_inc(k_part_turned, 1)

            def spread_key_max(b):
                pe.wait_ge(k_diag_ready, b + 1)
                pe.matmul(km_ps, ones[0:H, :], k_diag[:, :], start=True, stop=True).then_inc(k_max_spread, 1)

            def query_rows(b, parity, h, after):
                wait(pe, q_clamped, H * b + h)
                for a in after:
                    wait(pe, *a)
                for i in range(2):
                    last = pe.matmul(half(slot_a, i), w_query[:, h, :], half(h0_t[parity], i), start=True, stop=True)
                last.then_inc(q_spread, 1)

            def head_values(b, parity, h, after):
                wait(pe, values_ready, H * b + h)
                for a in after:
                    wait(pe, *a)
                for t in range(T):
                    last = pe.matmul(block(slot_b, t), block(h0_t[parity], t), w_val[:, h, :], start=True, stop=True)
                last.then_inc(z_ready, 1)

            def attend(b, h):
                pos = tile_pos(b, h)
                pe.wait_ge(values_ready, H * b + h + 1)
                wait(pe, head_added, H * b + h)
                for t in range(T):
                    pe.wait_ge(tile_filled, pos + t + 1)
                    scores = ring[:, head_slot(b, h, t), :]
                    for n in range(T):
                        last = pe.matmul(o_block(n), block(scores, n), values[h % 2][:, t, :],
                                         start=(t == 0 and n % 3 == 0), stop=(t == T - 1),
                                         skip_group_check=True)
                    last.then_inc(tile_used, 1)

            def turn_h1(b, after):
                pe.wait_ge(ln[1]["s_out"], b + 1)
                wait(pe, *after)
                for t in range(T):
                    last = pe.transpose(block(slot_a, t), h1[:, t, :], ident[:, :])
                last.then_inc(h1_turned, 1)

            def features(b, after_a, after_b):
                pe.wait_ge(h1_t_ready, b + 1)
                wait(pe, *after_a)
                for i in range(2):
                    last = pe.matmul(half(slot_a, i)[0:96, :], w_dist[:, :], half(h1_t, i), start=True, stop=True)
                last.then_inc(s_product, 1)
                wait(pe, *after_b)
                for i in range(2):
                    last = pe.matmul(half(slot_b, i), conv1_t[:, :], half(h1_t, i), start=True, stop=True)
                last.then_inc(conv1_product, 1)
                pe.wait_ge(s_read, b + 1)
                for t in range(T):
                    last = pe.matmul(block(slot_a, t), block(h1_t, t), w_msg_t[:, :], start=True, stop=True)
                last.then_inc(msg_product, 1)

            def distances(b, m, slot, after):
                wait(pe, *after)
                if m == 0:
                    pe.wait_ge(dist_ready, b + 1)
                rows = 2 * 32 + S
                for i in range(2):
                    last = pe.matmul(half(slot, i), block(dist_l, m)[0:rows, :], half(dist_r, i)[0:rows, :],
                                     start=True, stop=True)
                last.then_inc(dist_product, 1)

            def pass_messages(b, m):
                pe.wait_ge(tile_filled, kernel_tile_pos(b, m) + 1)
                if m == 0:
                    pe.wait_ge(msg_ready, b + 1)
                tile = ring[:, kernel_slot(b, m), :]
                for i in range(2):
                    last = pe.matmul(half(slot_a, i), msg[:, m, :], half(tile, i), start=(m == 0), stop=(m == T - 1),
                                     skip_group_check=True)
                last.then_inc(tile_used, 1)

            def messages_and_distances(b, after_a, after_b):
                wait(pe, *after_a)
                for m in range(AM_SPLIT):
                    pass_messages(b, m)
                    distances(b, AM_SPLIT + m, slot_b, after_b if m == 0 else (kern_ready, T * b + AM_SPLIT + m))
                for m in range(AM_SPLIT, T):
                    pass_messages(b, m)

            def convolve(b, i, after):
                wait(pe, *after)
                if i == 0:
                    pe.wait_ge(conv_in_ready, b + 1)
                for k in range(TAPS):
                    last = pe.matmul(half(slot_a, i), conv2_t[:, k, :], conv_in[:, i * HALF + k:i * HALF + k + HALF],
                                     start=(k == 0), stop=(k == TAPS - 1))
                last.then_inc(conv2_product, 1)

            def gate(slot, terms, done):
                for i in range(2):
                    for n, (w, v) in enumerate(terms):
                        last = pe.matmul(half(slot, i), w, half(v, i), start=(n == 0), stop=(n == len(terms) - 1))
                last.then_inc(done, 1)

            def gates(b, after_a, after_b):
                def from_in(g):
                    return [(w_ih_t[:, 0, g * D:(g + 1) * D], conv_t), (w_ih_t[:, 1, g * D:(g + 1) * D], nmp_t)]

                def from_hidden(g):
                    return [(w_hh_t[:, g * D:(g + 1) * D], h1_t)]

                pe.wait_ge(conv_ready, 2 * b + 2)
                pe.wait_ge(nmp_ready, b + 1)
                wait(pe, *after_a)
                gate(slot_a, from_in(0) + from_hidden(0), gate_r_product)
                wait(pe, *after_b)
                gate(slot_b, from_hidden(2), gate_h_product)
                pe.wait_ge(r_tanh_ready, b + 1)
                gate(slot_a, from_in(1) + from_hidden(1), gate_z_product)
                pe.wait_ge(gate_h_added, b + 1)
                gate(slot_b, from_in(2), gate_n_product)

            def turn_out(b, after):
                pe.wait_ge(gru_ready, b + 1)
                wait(pe, *after)
                for t in range(T):
                    last = pe.transpose(block(slot_a, t), block(gate_z, t), ident[:, :])
                last.then_inc(gru_turned, 1)

            pe.wait_ge(bias_ready, 5)
            turn_h0(0, (setup_copied, SETUP_JOBS))
            key_scores(0, 0)
            turn_key_max(0)
            spread_key_max(0)
            query_rows(0, 0, 0, ())
            head_values(0, 0, 0, ((h0_t_ready, 1),))

            def frame(b, parity, prev, next_):
                L = b - 1
                held_a = [(out_ready, b - 1), (h1_t_ready, b), (msg_added, b), (kern_ready, T * L + 3),
                          (nmp_ready, b), (conv2_added, 2 * L + 1), (conv2_added, 2 * L + 2), (z_tanh_ready, b)]
                held_b = [None, None, (conv_in_ready, b), (kern_ready, T * L + 4), None, None, None, (gate_n_added, b)]
                for h, following in steps(b, prev, next_):
                    if following:
                        fb, fh = following
                        fp = parity if fh else 1 - parity
                        query_rows(fb, fp, fh, [held_a[h]] if prev else [])
                        after_b = [held_b[h]] if prev and held_b[h] else []
                        if h == 4 and next_:
                            after_b = [(h0_t_ready, b + 2)]
                        head_values(fb, fp, fh, after_b)
                    attend(b, h)
                    n_query = H * b + h + 2
                    a_free, b_free = (q_clamped, n_query), (values_ready, n_query)
                    if prev:
                        if h == 0:
                            turn_h1(L, a_free)
                        elif h == 1:
                            features(L, a_free, b_free)
                        elif h == 2:
                            distances(L, 0, slot_a, a_free)
                            distances(L, 1, slot_b, b_free)
                            distances(L, 2, slot_a, (kern_ready, T * L + 1))
                            distances(L, 3, slot_b, (kern_ready, T * L + 2))
                        elif h == 3:
                            messages_and_distances(L, a_free, b_free)
                        elif h in (4, 5):
                            convolve(L, h - 4, a_free)
                        elif h == 6:
                            gates(L, a_free, b_free)
                        elif h == 7:
                            turn_out(L, a_free if next_ else (z_tanh_ready, b))
                    if next_:
                        if h == 3:
                            turn_h0(b + 1, (kern_ready, T * b) if prev else b_free)
                        elif h == 4:
                            key_scores(b + 1, 1 - parity)
                        elif h == 5:
                            turn_key_max(b + 1)
                        elif h == 6:
                            spread_key_max(b + 1)

            frames(pe, frame)
            L = LAST
            turn_h1(L, (out_ready, L))
            features(L, (h1_t_ready, B), (gate_n_added, L))
            distances(L, 0, slot_a, (msg_added, B))
            distances(L, 1, slot_b, (conv_in_ready, B))
            distances(L, 2, slot_a, (kern_ready, T * L + 1))
            distances(L, 3, slot_b, (kern_ready, T * L + 2))
            messages_and_distances(L, (kern_ready, T * L + 3), (kern_ready, T * L + 4))
            convolve(L, 0, (nmp_ready, B))
            convolve(L, 1, (conv2_added, 2 * L + 1))
            gates(L, (conv2_added, 2 * L + 2), (kern_ready, T * B))
            turn_out(L, (z_tanh_ready, B))

        @blk.scalar
        def _(act):
            def copy(dst, src):
                return act.activation(dst, src, ACT.Copy)

            act.wait_ge(setup_filled, J_FC + 1)
            copy(fc_t.rearrange("p h i -> p (h i)"), slot_a[:, :]).then_inc(setup_copied, 1)
            act.wait_ge(setup_filled, J_IH + 1)
            copy(w_ih_t[:, :, :].rearrange("p i n -> p (i n)"), slot_b[:, 0:6 * P])
            copy(w_msg_t[:, :], block(slot_b, 6))
            copy(conv1_t[:, :], block(slot_b, 7)).then_inc(setup_copied, 1)
            act.wait_ge(setup_filled, J_HH + 1)
            act.wait_ge(consts_ready, 11)
            copy(w_hh_t[:, :], slot_a[:, 0:3 * P])
            for q in range(3):
                last = copy(w_dist[:, 32 * q:32 * q + S], slot_a[:, 3 * P:3 * P + S])
            last.then_inc(setup_copied, 1)
            for j, k0, slot in ((J_TAPS0, 0, slot_b), (J_TAPS1, 8, slot_a), (J_TAPS2, 16, slot_b)):
                act.wait_ge(setup_filled, j + 1)
                n = min(8, TAPS - k0)
                copy(conv2_t[:, k0:k0 + n, :].rearrange("p k o -> p (k o)"), slot[:, 0:n * P]).then_inc(setup_copied, 1)
            act.wait_ge(setup_filled, J_VAL + 1)
            copy(w_val[:, :, :].rearrange("p h d -> p (h d)"), slot_a[:, :]).then_inc(setup_copied, 1)
            act.wait_ge(setup_filled, J_QUERY + 1)
            copy(w_query[:, :, :].rearrange("p h c -> p (h c)"), slot_b[:, :]).then_inc(setup_copied, 1)
            act.wait_ge(setup_filled, J_SMALL + 1)
            copy(w_key[:, :], bias_ps[:, 0:H]).then_inc(setup_copied, 1)

            def copy_h0_t(b, parity):
                act.wait_ge(h0_turned, b + 1)
                copy(h0_t[parity][:, :], slot_b[:, :]).then_inc(h0_t_ready, 1)

            def key_weights(b, parity):
                act.wait_ge(k_low_ready, b + 1)
                act.activation(p_half[:, :, :], k_low[:, :, :], ACT.Exp, scale=HALF_SPAN).then_inc(p_half_ready, 1)
                act.activation(v_col[parity][:, :, :], k_low[:, :, :], ACT.Exp, scale=SLOPE)
                act.wait_ge(p_half_ready, b + 1)
                act.activation(p_col[parity][:, :, :], p_half[:, :, :], ACT.Square, scale=HALF_C).then_inc(pv_ready, 1)

            def query_weights(b, parity, h):
                act.wait_ge(q_spread, H * b + h + 1)
                if h == 0:
                    act.wait_ge(k_low_ready, b + 1)
                wait(act, r_ready, H * b + h)
                act.activation(r_half[:, :], slot_a[:, :], ACT.Relu, bias=r_bias[parity][:, h:h + 1],
                               scale=HALF_SPAN).then_inc(q_clamped, 1)
                act.wait_ge(q_clamped, H * b + h + 1)
                act.activation(r_half[:, :], r_half[:, :], ACT.Exp, scale=-1.0).then_inc(r_half_ready, 1)
                act.wait_ge(r_half_ready, H * b + h + 1)
                if not (isinstance(b, int) and b == 0 and h < 2):
                    pos = tile_pos(b, h - 2) + T if h >= 2 else tile_pos(b, 0) - 2 * T + (h + 1) * T
                    act.wait_ge(tile_filled, pos)
                act.activation(r_row[h % 2][:, :], r_half[:, :], ACT.Square, scale=HALF_C).then_inc(r_ready, 1)

            def tanh_y(b):
                act.wait_ge(head_added, H * b + H)
                wait(act, gru_ready, b)
                act.activation(y_tanh, y[:, :, :], ACT.Tanh, scale=0.5).then_inc(y_tanh_ready, 1)

            def copy_h1_t(b):
                act.wait_ge(h1_turned, b + 1)
                wait(act, gru_ready, b)
                copy(h1_t[:, :], slot_a[:, :]).then_inc(h1_t_ready, 1)

            def features(b):
                act.wait_ge(s_product, b + 1)
                wait(act, dist_product, T * b)
                act.activation(dist_l[0:S, :], slot_a[0:S, :], ACT.Identity, bias=b_dist[0:S, 1:2], scale=2.0)
                act.activation(dist_r[0:S, :], slot_a[0:S, :], ACT.Identity, bias=b_dist[0:S, 0:1])
                act.activation(dist_r[32:32 + S, :], slot_a[32:32 + S, :], ACT.Square, bias=b_dist[32:32 + S, 0:1])
                act.activation(dist_l[64:64 + S, :], slot_a[64:64 + S, :], ACT.Identity,
                               bias=b_dist[64:64 + S, 0:1]).then_inc(s_read, 1)
                act.wait_ge(conv1_product, b + 1)
                wait(act, conv2_product, 2 * b)
                act.activation(conv_in[:, PAD:PAD + N], slot_b[:, :], ACT.Relu, bias=bn_aff[:, 0, 1:2],
                               scale=bn_aff[:, 0, 0:1]).then_inc(conv_in_ready, 1)

            def kernel_block(b, m, slot):
                act.wait_ge(dist_product, T * b + m + 1)
                if m >= 2:
                    act.wait_ge(tile_filled, kernel_tile_pos(b, m - 2) + 1)
                elif not (isinstance(b, int) and b == 0):
                    act.wait_ge(tile_filled, kernel_tile_pos(b - 1, T - 2 + m) + 1)
                act.activation(kern[m % 2][:, :], slot[:, :], ACT.Exp).then_inc(kern_ready, 1)

            def copy_nmp(b, last_batch=False):
                act.wait_ge(tile_used, kernel_tile_pos(b, T - 1) + 1 if last_batch else used(b + 1, KERNEL_AT[-1]))
                wait(act, gate_n_product, b)
                copy(nmp_t[:, :], slot_a[:, :]).then_inc(nmp_ready, 1)

            def conv_relu(b, i):
                act.wait_ge(conv2_added, 2 * b + i + 1)
                act.activation(half(conv_t, i), half(conv_t, i), ACT.Relu, bias=bn_aff[:, 1, 1:2]).then_inc(conv_ready, 1)

            def gate_tanhs(b):
                act.wait_ge(gate_r_product, b + 1)
                act.activation(gate_a[:, :], slot_a[:, :], ACT.Tanh, bias=b_gate[:, 0:1], scale=0.5)\
                   .then_inc(r_tanh_ready, 1)
                act.wait_ge(gate_z_product, b + 1)
                wait(act, gru_turned, b)
                act.activation(gate_z[:, :], slot_a[:, :], ACT.Tanh, bias=b_gate[:, 1:2], scale=0.5)\
                   .then_inc(z_tanh_ready, 1)
                act.wait_ge(gate_n_added, b + 1)
                act.activation(gate_a[:, :], gate_a[:, :], ACT.Tanh, bias=b_gate_in[:, 0, 2:3]).then_inc(n_ready, 1)

            act.wait_ge(bias_ready, 5)
            copy_h0_t(0, 0)
            key_weights(0, 0)
            query_weights(0, 0, 0)

            def frame(b, parity, prev, next_):
                L = b - 1
                for h, following in steps(b, prev, next_):
                    if h == 0 and prev:
                        tanh_y(L)
                    if following:
                        fb, fh = following
                        query_weights(fb, parity if fh else 1 - parity, fh)
                    if prev:
                        if h == 0:
                            copy_h1_t(L)
                        elif h == 1:
                            features(L)
                        elif h == 2:
                            for m in range(AM_SPLIT):
                                kernel_block(L, m, (slot_a, slot_b)[m % 2])
                        elif h == 3:
                            for m in range(AM_SPLIT, T):
                                kernel_block(L, m, slot_b)
                            copy_nmp(L)
                        elif h in (4, 5):
                            conv_relu(L, h - 4)
                        elif h == 6:
                            gate_tanhs(L)
                    if next_ and h == 3:
                        copy_h0_t(b + 1, 1 - parity)
                    if next_ and h == 6:
                        key_weights(b + 1, 1 - parity)

            frames(act, frame)
            L = LAST
            tanh_y(L)
            copy_h1_t(L)
            features(L)
            for m in range(T):
                kernel_block(L, m, slot_b if m >= AM_SPLIT else (slot_a, slot_b)[m % 2])
            copy_nmp(L, True)
            conv_relu(L, 0)
            conv_relu(L, 1)
            gate_tanhs(L)

        @blk.vector
        def _(dve):
            dve.wait_ge(consts_ready, 11)
            dve.wait_ge(w_loaded, 16 * N_LOADS)
            dve.tensor_scalar(q_rep, ones[:, :], qk_raw[:, 0:1], None, ALU.mult).then_inc(w_reps_ready, 1)
            dve.tensor_scalar(k_rep, ones[:, :], qk_raw[:, 1:2], None, ALU.mult).then_inc(w_reps_ready, 1)
            for h in range(H):
                last = dve.tensor_scalar(fcb_rep[:, h, :], ones[:, :], fcb_raw[:, h:h + 1], None, ALU.mult)
            last.then_inc(w_reps_ready, 1)
            dve.tensor_scalar(bn_tmp[:, :, 0], bn[:, :, 3], EPS, None, ALU.add).then_inc(bn_step, 1)
            dve.wait_ge(bn_step, 2)
            dve.tensor_tensor(bn_aff[:, :, 0], bn[:, :, 0], bn_tmp[:, :, 1], ALU.mult).then_inc(bn_step, 1)
            dve.wait_ge(bn_step, 3)
            dve.tensor_tensor(bn_tmp[:, :, 0], bn[:, :, 2], bn_aff[:, :, 0], ALU.mult).then_inc(bn_step, 1)
            dve.wait_ge(bn_step, 4)
            dve.tensor_tensor(bn_aff[:, :, 1], bn[:, :, 1], bn_tmp[:, :, 0], ALU.subtract).then_inc(bias_ready, 1)
            dve.tensor_tensor(b_gate[:, :], b_gate_in[:, 0, 0:2], b_gate_in[:, 1, 0:2], ALU.add).then_inc(bn_step, 1)
            dve.wait_ge(bn_step, 5)
            dve.tensor_scalar(b_gate[:, :], b_gate[:, :], 0.5, None, ALU.mult).then_inc(bias_ready, 1)
            dve.tensor_scalar(b_dist[:, 1:2], b_dist[:, 0:1], 2.0, None, ALU.mult).then_inc(bias_ready, 1)

            def layer_norm(layer, b, src, dst):
                s = ln[layer]
                for t in range(T):
                    last = dve.bn_stats(s["stats"][:, t, :], src[:, t, :])
                last.then_inc(s["s_stats"], 1)
                wait_apart(dve, s["s_stats"], b + 1, passed["vector"])
                for t in range(T):
                    last = dve.bn_aggr(s["mv"][:, t, :], s["stats"][:, t, :])
                last.then_inc(s["s_mv"], 1)
                dve.wait_ge(s["s_rstd"], b + 1)
                for t in range(T):
                    last = dve.tensor_scalar(dst[:, t, :], src[:, t, :], s["mv"][:, t, 0:1], s["rstd"][:, t:t + 1],
                                             ALU.subtract, ALU.mult)
                last.then_inc(s["s_mid"], 1)
                dve.wait_ge(s["s_mid"], b + 1)
                dve.tensor_scalar(dst[:, :, :], dst[:, :, :], 0.0, None, ALU.max).then_inc(s["s_out"], 1)

            def first_norm(b, parity):
                dve.wait_ge(x_loaded, 16 * (b + 1))
                wait(dve, y_ready, b)
                layer_norm(0, b, x_in[parity], h0)

            def keys(b):
                dve.wait_ge(k_scored, b + 1)
                wait(dve, pv_ready, b)
                dve.tensor_tensor(k_sb[:, :, :], kq_ps, b_key[:, None, :].to_broadcast([P, T, H]), ALU.add)\
                   .then_inc(k_ready, 1)
                dve.wait_ge(k_ready, b + 1)
                dve.tensor_reduce(k_part[:, :], k_sb[:, :, :].rearrange("p t h -> p h t"), AX.X, ALU.max)\
                   .then_inc(k_part_ready, 1)

            def key_max(b):
                dve.wait_ge(k_part_turned, b + 1)
                dve.tensor_reduce(k_max[:, :], kt_ps, AX.X, ALU.max).then_inc(k_max_ready, 1)
                dve.wait_ge(k_max_ready, b + 1)
                dve.tensor_scalar(k_diag[:, :], ident[0:H, 0:H], k_max[:, 0:1], None, ALU.mult).then_inc(k_diag_ready, 1)

            def key_shift(b, parity):
                dve.wait_ge(k_max_spread, b + 1)
                dve.tensor_copy(k_shift[:, :], km_ps).then_inc(k_shift_ready, 1)
                dve.wait_ge(k_shift_ready, b + 1)
                dve.tensor_tensor(r_bias_raw[:, :], k_shift[:, :], b_query[:, :], ALU.add).then_inc(r_bias_raw_ready, 1)
                dve.wait_ge(r_bias_raw_ready, b + 1)
                dve.tensor_scalar(r_bias[parity][:, :], r_bias_raw[:, :], HALF_SPAN, None, ALU.mult)
                dve.tensor_tensor(k_low[:, :, :], k_sb[:, :, :], k_shift[:, None, :].to_broadcast([P, T, H]),
                                  ALU.subtract).then_inc(k_low_ready, 1)

            def scale_values(b, parity, h):
                dve.wait_ge(z_ready, H * b + h + 1)
                if h == 0:
                    dve.wait_ge(pv_ready, b + 1)
                weights = v_col[parity][:, :, h:h + 1]
                dve.tensor_copy(values[h % 2][:, :, D:W], weights)
                dve.tensor_tensor(values[h % 2][:, :, 0:D], slot_b[:, :].rearrange("p (t d) -> p t d", t=T),
                                  weights.to_broadcast([P, T, D]), ALU.mult).then_inc(values_ready, 1)

            def score_tiles(b, parity, h):
                if h == 0:
                    dve.wait_ge(adj_turned, 16 * T * (b + 1))
                dve.wait_ge(r_ready, H * b + h + 1)
                for t in range(T):
                    if isinstance(b, int) and b == 0:
                        wait(dve, tile_used, T * h + t + 1 - RING)
                    else:
                        dve.wait_ge(tile_used, place_free(b, HEAD_AT[h] + t))
                    dve.scalar_tensor_tensor(out=ring[:, head_slot(b, h, t), :], in0=r_row[h % 2][:, :],
                                             scalar=p_col[parity][:, t, h:h + 1], in1=adj_t[parity][:, t, :],
                                             op0=ALU.max, op1=ALU.mult).then_inc(tile_filled, 1)

            def add_head(b, h):
                dve.wait_ge(tile_used, head_used(b, h, T - 1))
                if h == 0:
                    dve.wait_ge(y_ready, b + 1)
                else:
                    dve.wait_ge(head_added, H * b + h)
                dve.reciprocal(rden[:, 0:6].rearrange("p (c n) -> p c n", c=2),
                               o_ps[:, 0:2, 0:3 * W].rearrange("p c (n w) -> p c n w", w=W)[:, :, :, D])
                dve.reciprocal(rden[:, 6:8], o_ps[:, 2, 0:2 * W].rearrange("p (n w) -> p n w", w=W)[:, :, D])\
                   .then_inc(rden_ready, 1)
                dve.wait_ge(rden_ready, H * b + h + 1)
                for n in range(T):
                    last = dve.scalar_tensor_tensor(out=y[:, n, :], in0=o_block(n)[:, 0:D], scalar=rden[:, n:n + 1],
                                                    in1=y[:, n, :], op0=ALU.mult, op1=ALU.add)
                last.then_inc(head_added, 1)

            def first_output(b, parity):
                dve.wait_ge(y_tanh_ready, b + 1)
                wait(dve, out_ready, b)
                dve.scalar_tensor_tensor(out=x1[:, :, :], in0=y_tanh, scalar=0.5, in1=x_in[parity][:, :, :],
                                         op0=ALU.mult, op1=ALU.add).then_inc(x1_half_ready, 1)
                dve.wait_ge(x1_half_ready, b + 1)
                dve.tensor_scalar(x1[:, :, :], x1[:, :, :], 0.5, None, ALU.add).then_inc(x1_ready, 1)
                dve.wait_ge(x1_ready, b + 1)
                layer_norm(1, b, x1, h1)

            def features(b):
                dve.wait_ge(s_read, b + 1)
                dve.scalar_tensor_tensor(out=dist_l[64:64 + S, :], in0=dist_l[64:64 + S, :], scalar=-1.0,
                                         in1=dist_l[64:64 + S, :], op0=ALU.mult, op1=ALU.mult).then_inc(dist_ready, 1)
                dve.wait_ge(msg_product, b + 1)
                dve.tensor_tensor(msg[:, :, :], slot_a[:, :].rearrange("p (t d) -> p t d", t=T),
                                  b_msg_row[:, None, :].to_broadcast([P, T, D]), ALU.add).then_inc(msg_added, 1)
                dve.wait_ge(msg_added, b + 1)
                dve.tensor_scalar(msg[:, :, :], msg[:, :, :], 0.0, None, ALU.max).then_inc(msg_ready, 1)

            def kernel_tile(b, parity, m):
                dve.wait_ge(kern_ready, T * b + m + 1)
                if isinstance(b, int) and b == LAST:
                    dve.wait_ge(tile_used, kernel_tile_pos(b, m) + 1 - RING)
                else:
                    dve.wait_ge(tile_used, place_free(b + 1, KERNEL_AT[m]))
                dve.tensor_tensor(ring[:, kernel_slot(b, m), :], kern[m % 2][:, :], adj_t[parity][:, m, :],
                                  ALU.mult).then_inc(tile_filled, 1)

            def conv_add(b, i):
                dve.wait_ge(conv2_product, 2 * b + i + 1)
                if i == 0:
                    wait(dve, out_stored, 16 * b)
                dve.scalar_tensor_tensor(out=half(conv_t, i), in0=half(slot_a, i), scalar=bn_aff[:, 1, 0:1],
                                         in1=half(h1_t, i), op0=ALU.mult, op1=ALU.add).then_inc(conv2_added, 1)

            def gru(b):
                dve.wait_ge(r_tanh_ready, b + 1)
                dve.tensor_scalar(gate_a[:, :], gate_a[:, :], 0.5, 0.5, ALU.mult, ALU.add).then_inc(gate_r_ready, 1)
                dve.wait_ge(gate_r_ready, b + 1)
                dve.wait_ge(gate_h_product, b + 1)
                dve.scalar_tensor_tensor(out=gate_a[:, :], in0=slot_b[:, :], scalar=b_gate_in[:, 1, 2:3],
                                         in1=gate_a[:, :], op0=ALU.add, op1=ALU.mult).then_inc(gate_h_added, 1)
                dve.wait_ge(gate_h_added, b + 1)
                dve.wait_ge(gate_n_product, b + 1)
                dve.tensor_tensor(gate_a[:, :], slot_b[:, :], gate_a[:, :], ALU.add).then_inc(gate_n_added, 1)
                dve.wait_ge(n_ready, b + 1)
                dve.tensor_tensor(diff_t, h1_t[:, :], gate_a[:, :], ALU.subtract).then_inc(diff_ready, 1)
                dve.wait_ge(diff_ready, b + 1)
                dve.scalar_tensor_tensor(out=gate_z[:, :], in0=gate_z[:, :], scalar=1.0, in1=diff_t,
                                         op0=ALU.add, op1=ALU.mult).then_inc(z_diff_ready, 1)
                dve.wait_ge(z_diff_ready, b + 1)
                dve.scalar_tensor_tensor(out=gate_z[:, :], in0=gate_z[:, :], scalar=0.5, in1=gate_a[:, :],
                                         op0=ALU.mult, op1=ALU.add).then_inc(gru_ready, 1)

            def add_out(b):
                dve.wait_ge(gru_turned, b + 1)
                dve.tensor_tensor(out_sb, slot_a[:, :].rearrange("p (t d) -> p t d", t=T), x1[:, :, :],
                                  ALU.add).then_inc(out_ready, 1)

            first_norm(0, 0)
            dve.wait_ge(setup_copied, SETUP_JOBS)
            dve.tensor_scalar(b_query[:, :], bias_ps[:, H:2 * H], qk_b[:, 0:1], None, ALU.add)
            dve.tensor_scalar(b_key[:, :], bias_ps[:, 2 * H:3 * H], qk_b[:, 1:2], None, ALU.add).then_inc(bias_ready, 1)
            dve.tensor_tensor(b_out[:, :], bout_ps, b_out[:, :], ALU.add).then_inc(bias_ready, 1)
            dve.wait_ge(bias_ready, 5)
            keys(0)
            key_max(0)
            key_shift(0, 0)
            scale_values(0, 0, 0)
            score_tiles(0, 0, 0)

            def frame(b, parity, prev, next_):
                L = b - 1
                for h, following in steps(b, prev, next_):
                    if following:
                        fb, fh = following
                        fp = parity if fh else 1 - parity
                        scale_values(fb, fp, fh)
                        score_tiles(fb, fp, fh)
                    if h == 0 and prev:
                        first_output(L, 1 - parity)
                    add_head(b, h)
                    if prev:
                        if h == 1:
                            features(L)
                        elif h == 2:
                            for m in range(AM_SPLIT):
                                kernel_tile(L, 1 - parity, m)
                        elif h == 3:
                            for m in range(AM_SPLIT, T):
                                kernel_tile(L, 1 - parity, m)
                        elif h in (4, 5):
                            conv_add(L, h - 4)
                        elif h == 6:
                            gru(L)
                        elif h == 7:
                            add_out(L)
                    if next_:
                        if h == 2:
                            first_norm(b + 1, 1 - parity)
                        elif h == 4:
                            keys(b + 1)
                        elif h == 5:
                            key_max(b + 1)
                        elif h == 6:
                            key_shift(b + 1, 1 - parity)

            frames(dve, frame)
            L = LAST
            first_output(L, 1)
            features(L)
            for m in range(T):
                kernel_tile(L, 1, m)
            conv_add(L, 0)
            conv_add(L, 1)
            gru(L)
            add_out(L)


_INS = ["x", "adj", "L0_gnn_fc_w", "L0_gnn_fc_b", "L0_gnn_q_w", "L0_gnn_q_b", "L0_gnn_k_w", "L0_gnn_k_b",
        "L0_gnn_fp_w", "L0_gnn_fp_b", "L1_gnn_w_se", "L1_gnn_b_se", "L1_gnn_conv1_w", "L1_gnn_bn1_g",
        "L1_gnn_bn1_b", "L1_gnn_bn1_m", "L1_gnn_bn1_v", "L1_gnn_conv2_w", "L1_gnn_bn2_g", "L1_gnn_bn2_b",
        "L1_gnn_bn2_m", "L1_gnn_bn2_v", "L1_gnn_w_msg", "L1_gnn_b_msg", "L1_gnn_w_ih", "L1_gnn_b_ih",
        "L1_gnn_w_hh", "L1_gnn_b_hh"]


def kernel(**inputs):
    import numpy as _np
    import concourse.bacc as _bacc
    from concourse import mybir as _mybir
    from concourse.bass_utils import run_bass_kernel_spmd as _run

    nc = _bacc.Bacc("TRN2", target_bir_lowering=False, num_devices=1)
    arrays, args = {}, []
    for name in _INS:
        a = _np.ascontiguousarray(inputs[name])
        arrays[f"in_{name}_dram"] = a
        args.append(nc.dram_tensor(f"in_{name}_dram", a.shape, _mybir.dt.from_np(a.dtype), kind="ExternalInput").ap())
    shape = arrays["in_x_dram"].shape
    args.append(nc.dram_tensor("out_0_dram", shape, _mybir.dt.float32, kind="ExternalOutput").ap())
    build(nc, *args)
    r = _run(nc, [arrays], core_ids=[0])
    return r.results[0]["out_0_dram"]
```

```python
import math
from contextlib import ExitStack

import concourse.bass as bass
from concourse import mybir

F32 = mybir.dt.float32
F32R = mybir.dt.float32r
BF16 = mybir.dt.bfloat16
ALU = mybir.AluOpType
ACT = mybir.ActivationFunctionType
AX = mybir.AxisListType

P = 128
R_ROWS = 2
KERNS = 4
RING = 12
TAPS = 17
PAD = TAPS // 2
EPS = 1e-5
SLOPE = 0.01
HALF_C = math.exp(30.0)
HALF_SPAN = (1.0 - SLOPE) / 2


def wait(eng, sem, value):
    if isinstance(value, int) and value <= 0:
        return
    eng.wait_ge(sem, value)


def wait_apart(eng, sem, value, passed):
    eng.wait_ge(sem, value)
    eng.sem_inc(passed, 1)


def build(nc, x, adj, fc_w, fc_b, q_w, q_b, k_w, k_b, fp_w, fp_b, w_se, b_se, conv1_w, bn1_g, bn1_b, bn1_m,
          bn1_v, conv2_w, bn2_g, bn2_b, bn2_m, bn2_v, w_msg, b_msg, w_ih, b_ih, w_hh, b_hh, out, r_dram):
    B, N, D = x.shape
    H = fc_w.shape[1] // D
    T = N // P
    HALF = N // 2
    W = D + 1
    S = w_se.shape[0]
    LAST = B - 1
    assert D == P and H == 8 and T == 8 and HALF == 512 and B % 2 == 0
    AM_SPLIT = T // 2
    ROWS_PROD, ROWS_SQ_N, ROWS_SQ_M = (0, 4), (32, 2), (64, 2)
    DIST_ROWS = 64 + 2 * S
    assert 4 * S <= 32
    PER = (H + 1) * T

    HEAD_AT = [0, 8, 16, 24, 32, 44, 56, 64]
    KERNEL_AT = [40, 41, 42, 43, 52, 53, 54, 55]
    BETWEEN = 5

    def frame_start(b):
        return PER * b - T

    def tile_pos(b, h):
        if isinstance(b, int) and b == 0:
            return T * h
        return frame_start(b) + HEAD_AT[h]

    def kernel_tile_pos(b, m):
        if isinstance(b, int) and b == LAST:
            return frame_start(b + 1) + m
        return frame_start(b + 1) + KERNEL_AT[m]

    def used(b, at):
        if at in KERNEL_AT[AM_SPLIT:]:
            at -= T
        elif HEAD_AT[BETWEEN] <= at < HEAD_AT[BETWEEN] + T:
            at += AM_SPLIT
        return frame_start(b) + at + 1

    def head_used(b, h, t):
        if isinstance(b, int) and b == 0:
            return T * h + t + 1
        return used(b, HEAD_AT[h] + t)

    def place_free(b, at):
        return used(b, at - RING)

    def tile_slot(pos0, t):
        return (pos0 + t) % RING

    def head_slot(b, h, t):
        return tile_slot(tile_pos(b if isinstance(b, int) else 1, h), t)

    def kernel_slot(b, m):
        return tile_slot(kernel_tile_pos(b if isinstance(b, int) else 0, m), 0)

    with ExitStack() as ctx:
        def sb(name, shape, dt=F32):
            return ctx.enter_context(nc.sbuf_tensor(name, shape, dt))

        def psum(name, shape):
            return ctx.enter_context(nc.psum_tensor(name, shape, F32))

        def sem(name):
            return ctx.enter_context(nc.semaphore(name))

        ring = sb("ring", [P, RING, N])
        adj_t = [sb(f"adj_t{i}", [P, T, N], BF16) for i in range(2)]
        adj_rows = sb("adj_rows", [P, T // 2, N], BF16)
        x_in = [sb(f"x_in{i}", [P, T, D]) for i in range(2)]
        h0 = sb("h0", [P, T, D])
        h0_t = [sb(f"h0_t{i}", [P, N]) for i in range(2)]
        y = sb("y", [P, T, D])
        values = [sb(f"values{i}", [P, T, W]) for i in range(2)]
        r_row = [sb(f"r_row{i}", [P, N]) for i in range(R_ROWS)]
        kq_sb = sb("kq_sb", [P, T, 2 * H])
        k_low = sb("k_low", [P, T, H])
        q_high = sb("q_high", [P, H, T])
        r_half = sb("r_half", [P, H, T])
        r_col = sb("r_col", [P, H, T])
        r_turned_sb = sb("r_turned_sb", [H * T, P])
        p_half = sb("p_half", [P, T, H])
        p_col = [sb(f"p_col{i}", [P, T, H]) for i in range(2)]
        v_col = [sb(f"v_col{i}", [P, T, H]) for i in range(2)]
        k_part = sb("k_part", [P, H])
        k_max = sb("k_max", [H, 1])
        k_diag = sb("k_diag", [H, H])
        k_shift = sb("k_shift", [P, H])
        rden = sb("rden", [P, T + 1])
        x1 = sb("x1", [P, T, D])
        h1 = sb("h1", [P, T, D])
        msg = h1
        h1_t = sb("h1_t", [P, N])
        dist_l = sb("dist_l", [P, N], F32R)
        dist_r = sb("dist_r", [P, N], F32R)
        conv_in = sb("conv_in", [P, N + 2 * PAD])
        kern = [sb(f"kern{i}", [P, N]) for i in range(KERNS - 1)]
        nmp_t = sb("nmp_t", [P, N])
        conv_t = sb("conv_t", [P, N])
        out_sb = conv_t[:, :].rearrange("p (t d) -> p t d", t=T)
        gate_a = sb("gate_a", [P, N])
        z_gate = sb("z_gate", [P, N])
        kern.append(z_gate)
        diff_t = h1[:, :, :].rearrange("p t d -> p (t d)")
        y_tanh = gate_a[:, :].rearrange("p (t d) -> p t d", t=T)
        ln = []
        for i in range(2):
            ln.append(dict(stats=sb(f"ln{i}_stats", [P, T, 6]), mv=sb(f"ln{i}_mv", [P, T, 2]),
                           var=sb(f"ln{i}_var", [P, T]), rstd=sb(f"ln{i}_rstd", [P, T]),
                           s_stats=sem(f"ln{i}_stats_ready"), s_mv=sem(f"ln{i}_moments_ready"),
                           s_var=sem(f"ln{i}_var_ready"), s_rstd=sem(f"ln{i}_rstd_ready"),
                           s_mid=sem(f"ln{i}_normalised"), s_out=sem(f"ln{i}_relu_ready")))

        ident = sb("ident", [P, P])
        ones = sb("ones", [P, P])
        minus_half = sb("minus_half", [P, T])
        w_val = sb("w_val", [P, H, D])
        w_kq = sb("w_kq", [P, 2 * H])
        b_kq = sb("b_kq", [P, 2 * H])
        b_out = sb("b_out", [P, D])
        w_dist = sb("w_dist", [P, 3 * 32])
        b_dist = sb("b_dist", [3 * 32, 2])
        dist_scale = sb("dist_scale", [3 * 32, 2])
        lo_rows = sb("lo_rows", [P, 4])
        minus_lo = sb("minus_lo", [P, 2])
        conv1_t = sb("conv1_t", [P, D])
        conv2_t = sb("conv2_t", [P, TAPS, D])
        w_msg_t = sb("w_msg_t", [P, D])
        b_msg_row = sb("b_msg_row", [P, D])
        w_ih_t = sb("w_ih_t", [P, 2, 3 * D])
        w_hh_t = sb("w_hh_t", [P, 3 * D])
        bn = sb("bn", [P, 2, 4])
        bn_aff = sb("bn_aff", [P, 2, 2])
        bn_tmp = sb("bn_tmp", [P, 2, 2])
        b_gate_in = sb("b_gate_in", [P, 2, 3])
        b_gate = sb("b_gate", [P, 2])
        qk_b = sb("qk_b", [P, 2])

        room = ring[:, :, :].rearrange("p r n -> p (r n)")
        taken = 0

        def raw(cols):
            nonlocal taken
            taken += cols
            assert taken <= RING * N
            return room[:, taken - cols:taken]

        fc_raw = raw(H * D)
        fp_raw = raw(H * D).rearrange("p (h d) -> p h d", h=H)
        ih_raw = raw(3 * 2 * D).rearrange("p (g i) -> p g i", g=3)
        hh_raw = raw(3 * D).rearrange("p (g i) -> p g i", g=3)
        msg_raw = raw(D)
        conv1_raw = raw(D)
        conv2_raw = raw(D * TAPS).rearrange("p (i k) -> p i k", k=TAPS)
        se_raw = raw(D)
        fc_t = raw(H * D).rearrange("p (h i) -> p h i", h=H)
        fcb_raw = raw(H)
        qk_raw = raw(2)
        q_rep = raw(P)
        k_rep = raw(P)
        fcb_rep = raw(H * P).rearrange("p (h c) -> p h c", h=H)

        o_ps = psum("o_ps", [P, 3, 512])
        slot_a = psum("slot_a", [P, N])
        slot_b = psum("slot_b", [P, N])
        small = psum("small", [P, 512])
        kq_ps = small[:, 0:T * 2 * H].rearrange("p (t h) -> p t h", t=T)
        kt_ps = small[0:H, 128:128 + P]
        km_ps = small[:, 256:256 + H]
        bias_ps = small[:, 320:320 + 4 * H]
        rt_ps = small[0:H * T, 384:384 + P]
        bout_ps = small[:, 384:384 + D]

        BANKS = [(0, 3), (3, 6), (6, 8)]

        def o_block(n):
            return o_ps[:, n // 3, (n % 3) * W:(n % 3 + 1) * W]

        consts_ready = sem("consts_ready")
        w_loaded = sem("w_loaded")
        w_reps_ready = sem("w_reps_ready")
        setup_filled = sem("setup_filled")
        setup_copied = sem("setup_copied")
        bias_ready = sem("bias_ready")
        bn_step = sem("bn_step")
        passed = {e: sem(f"{e}_waits_passed") for e in ("sync", "pool", "vector")}
        x_loaded = sem("x_loaded")
        adj_cast = sem("adj_cast")
        adj_turned = sem("adj_turned")
        h0_turned = sem("h0_turned")
        h0_t_ready = sem("h0_t_ready")
        k_scored = sem("k_scored")
        k_ready = sem("k_ready")
        k_part_ready = sem("k_part_ready")
        k_part_turned = sem("k_part_turned")
        k_max_ready = sem("k_max_ready")
        k_diag_ready = sem("k_diag_ready")
        k_max_spread = sem("k_max_spread")
        k_shift_ready = sem("k_shift_ready")
        q_shifted = sem("q_shifted")
        kq_shifted = sem("kq_shifted")
        p_half_ready = sem("p_half_ready")
        pv_ready = sem("pv_ready")
        r_half_ready = sem("r_half_ready")
        r_col_ready = sem("r_col_ready")
        r_turned = sem("r_turned")
        r_turned_read = sem("r_turned_read")
        r_stored = sem("r_stored")
        r_loaded = [sem(f"r_loaded{i}") for i in range(R_ROWS)]
        z_ready = sem("z_ready")
        values_ready = sem("values_ready")
        tile_filled = sem("tile_filled")
        tile_used = sem("tile_used")
        rden_ready = sem("rden_ready")
        bank_done = sem("bank_done")
        head_added = sem("head_added")
        y_ready = sem("y_ready")
        y_tanh_ready = sem("y_tanh_ready")
        x1_half_ready = sem("x1_half_ready")
        x1_ready = sem("x1_ready")
        h1_turned = sem("h1_turned")
        h1_t_ready = sem("h1_t_ready")
        s_product = sem("s_product")
        s_read = sem("s_read")
        s_hi_ready = sem("s_hi_ready")
        dist_ready = sem("dist_ready")
        conv1_product = sem("conv1_product")
        conv_in_ready = sem("conv_in_ready")
        msg_product = sem("msg_product")
        msg_added = sem("msg_added")
        msg_ready = sem("msg_ready")
        dist_product = sem("dist_product")
        kern_ready = sem("kern_ready")
        nmp_ready = sem("nmp_ready")
        conv2_product = sem("conv2_product")
        conv2_added = sem("conv2_added")
        conv_ready = sem("conv_ready")
        gate_r_product = sem("gate_r_product")
        gate_z_product = sem("gate_z_product")
        gate_h_product = sem("gate_h_product")
        gate_n_product = sem("gate_n_product")
        r_tanh_ready = sem("r_tanh_ready")
        z_tanh_ready = sem("z_tanh_ready")
        gate_r_ready = sem("gate_r_ready")
        gate_h_added = sem("gate_h_added")
        gate_n_added = sem("gate_n_added")
        n_ready = sem("n_ready")
        diff_ready = sem("diff_ready")
        z_diff_ready = sem("z_diff_ready")
        gru_ready = sem("gru_ready")
        gru_turned = sem("gru_turned")
        out_ready = sem("out_ready")
        out_stored = sem("out_stored")

        def blocks(dram, b):
            return dram[b].rearrange("(t p) d -> p t d", p=P)

        def block(buf, t):
            return buf[:, t * P:(t + 1) * P]

        def half(buf, i):
            return buf[:, i * HALF:(i + 1) * HALF]

        def frames(eng, frame):
            frame(0, 0, False, True)
            frame(1, 1, True, True)
            with eng.Fori(0, (B - 4) // 2) as pair:
                b = pair * 2 + 2
                frame(b, 0, True, True)
                frame(b + 1, 1, True, True)
            frame(LAST - 1, 0, True, True)
            frame(LAST, 1, True, False)

        def steps(b, prev, next_):
            for h in range(H):
                following = (b, h + 1) if h + 1 < H else (b + 1, 0)
                yield h, (following if h + 1 < H or next_ else None)

        (J_FC, J_IH, J_HH, J_TAPS0, J_TAPS1, J_TAPS2, J_VAL, J_SMALL) = range(8)
        SETUP_JOBS = 8
        job_slot = [slot_a, slot_b, slot_a, slot_b, slot_a, slot_b, slot_a, small]
        N_LOADS = 37
        N_CONSTS = 12

        blk = ctx.enter_context(nc.Block())

        @blk.sync
        def _(sp):
            def load(dst, src):
                sp.dma_start(dst, src).then_inc(w_loaded, 16)

            def col(v):
                return v.rearrange("(p a) -> p a", a=1)

            sp.dma_start(x_in[0][:, :, :], blocks(x, 0)).then_inc(x_loaded, 16)
            load(fc_raw, fc_w)
            load(fp_raw, fp_w.rearrange("(h k) d -> k h d", k=D))
            load(ih_raw, w_ih.rearrange("(g p) i -> p g i", p=P))
            load(hh_raw, w_hh.rearrange("(g p) i -> p g i", p=P))
            load(msg_raw, w_msg)
            load(conv1_raw, conv1_w.rearrange("o i k -> o (i k)"))
            load(conv2_raw, conv2_w)
            load(se_raw[0:S, :], w_se)
            load(qk_raw[:, 0:1], q_w)
            load(qk_raw[:, 1:2], k_w)
            for i, vec in enumerate((bn1_g, bn1_b, bn1_m, bn1_v, bn2_g, bn2_b, bn2_m, bn2_v)):
                load(bn[:, i // 4, i % 4:i % 4 + 1], col(vec))
            load(qk_b[:, 0:1], q_b.rearrange("(a n) -> a n", a=1).to_broadcast([P, 1]))
            load(qk_b[:, 1:2], k_b.rearrange("(a n) -> a n", a=1).to_broadcast([P, 1]))
            load(b_out[:, :], fp_b.rearrange("(a n) -> a n", a=1).to_broadcast([P, D]))
            load(b_msg_row[:, :], b_msg.rearrange("(a n) -> a n", a=1).to_broadcast([P, D]))
            with nc.allow_non_contiguous_dma(reason="bias vectors of a few hundred numbers, once"):
                load(fcb_raw, fc_b.rearrange("(h k) -> k h", k=D))
                load(b_gate_in[:, 0, :], b_ih.rearrange("(g p) -> p g", p=P))
                load(b_gate_in[:, 1, :], b_hh.rearrange("(g p) -> p g", p=P))
                sp.wait_ge(consts_ready, 7)
                for side, groups in enumerate(((ROWS_PROD, ROWS_SQ_M), (ROWS_PROD, ROWS_SQ_N))):
                    for row, copies in groups:
                        for c in range(copies):
                            load(b_dist[row + c * S:row + (c + 1) * S, side:side + 1],
                                 b_se.rearrange("(p a) -> p a", a=1))

            def turn_adj(b, parity, first_wait):
                for i in range(2):
                    first_wait(i)
                    for t in range(T // 2):
                        n0 = (i * T // 2 + t) * P
                        sp.dma_start_transpose(adj_t[parity][:, :, n0:n0 + P],
                                               adj_rows[:, t, :]).then_inc(adj_turned, 16)

            turn_adj(0, 0, lambda i: sp.wait_ge(adj_cast, 16 * (i + 1)))

            def frame(b, parity, prev, next_):
                if next_:
                    nb, other = b + 1, 1 - parity
                    wait(sp, x1_ready, b)
                    sp.dma_start(x_in[other][:, :, :], blocks(x, nb)).then_inc(x_loaded, 16)
                    if prev:
                        wait_apart(sp, tile_filled, kernel_tile_pos(b - 1, T - 1) + 1, passed["sync"])
                    turn_adj(nb, other, lambda i: wait_apart(sp, adj_cast, 32 * nb + 16 * (i + 1), passed["sync"]))
                if prev:
                    sp.wait_ge(out_ready, b)
                    sp.dma_start(blocks(out, b - 1), out_sb).then_inc(out_stored, 16)

            frames(sp, frame)
            sp.wait_ge(out_ready, B)
            sp.dma_start(blocks(out, LAST), out_sb).then_inc(out_stored, 16)
            sp.wait_ge(out_stored, 16 * B)

        @blk.gpsimd
        def _(pool):
            def load_adj(b, i):
                rows = adj[b].rearrange("(s t p) m -> s p t m", p=P, s=2)
                wait(pool, adj_turned, 16 * T * b + 8 * T * i)
                pool.dma_start(adj_rows[:, :, :], rows[i]).then_inc(adj_cast, 16)

            pool.memset(ident[:, :], 0.0).then_inc(consts_ready, 1)
            pool.memset(b_dist[:, :], 0.0).then_inc(consts_ready, 1)
            pool.memset(ones[:, :], 1.0).then_inc(consts_ready, 1)
            pool.memset(minus_half[:, :], -0.5).then_inc(consts_ready, 1)
            pool.memset(w_dist[:, :], 0.0).then_inc(consts_ready, 1)
            pool.memset(conv_in[:, :], 0.0).then_inc(consts_ready, 1)
            pool.memset(dist_scale[:, :], 0.0).then_inc(consts_ready, 1)
            pool.wait_ge(consts_ready, 7)
            pool.affine_select(out=ident[:, :], in_=ident[:, :], compare_op=ALU.not_equal, fill=1.0, base=0,
                               pattern=[[-1, P]], channel_multiplier=1).then_inc(consts_ready, 1)
            pool.wait_ge(consts_ready, 8)
            pool.memset(b_dist[32:32 + 2 * S, 0:1], -1.0).then_inc(consts_ready, 1)
            pool.wait_ge(consts_ready, 9)
            pool.memset(b_dist[64:64 + 2 * S, 1:2], -1.0).then_inc(consts_ready, 1)
            pool.wait_ge(consts_ready, 10)
            pool.memset(dist_scale[0:32, 0:1], 2.0).then_inc(consts_ready, 1)
            pool.wait_ge(consts_ready, 11)
            pool.memset(dist_scale[0:32, 1:2], 1.0).then_inc(consts_ready, 1)
            pool.wait_ge(consts_ready, N_CONSTS)
            load_adj(0, 0)
            load_adj(0, 1)

            pool.wait_ge(bn_step, 1)
            pool.tensor_tensor(bn_tmp[:, :, 1], bn_tmp[:, :, 0], minus_half[:, 0:2], ALU.pow).then_inc(bn_step, 1)

            def rstd(layer, b):
                s = ln[layer]
                wait_apart(pool, s["s_mv"], b + 1, passed["pool"])
                pool.tensor_scalar(s["var"][:, :], s["mv"][:, :, 1], EPS, None, ALU.add).then_inc(s["s_var"], 1)
                pool.wait_ge(s["s_var"], b + 1)
                pool.tensor_tensor(s["rstd"][:, :], s["var"][:, :], minus_half[:, :],
                                   ALU.pow).then_inc(s["s_rstd"], 1)

            def start_y(b):
                pool.wait_ge(ln[0]["s_out"], b + 1)
                wait(pool, y_tanh_ready, b)
                pool.tensor_tensor(y[:, :, :], h0[:, :, :], b_out[:, None, :].to_broadcast([P, T, D]),
                                   ALU.add).then_inc(y_ready, 1)

            rstd(0, 0)
            pool.wait_ge(bias_ready, 5)

            def frame(b, parity, prev, next_):
                start_y(b)
                if next_:
                    load_adj(b + 1, 0)
                if prev:
                    rstd(1, b - 1)
                if next_:
                    rstd(0, b + 1)
                    load_adj(b + 1, 1)

            frames(pool, frame)
            rstd(1, LAST)

        @blk.tensor
        def _(pe):
            def job(j, needs=0):
                if max(j - 1, needs) > 0:
                    pe.wait_ge(setup_copied, max(j - 1, needs))
                return job_slot[j]

            pe.wait_ge(consts_ready, N_CONSTS)
            pe.wait_ge(w_loaded, 16 * N_LOADS)
            s = job(J_FC)
            for h in range(H):
                last = pe.transpose(block(s, h), block(fc_raw, h), ident[:, :])
            last.then_inc(setup_filled, 1)
            s = job(J_IH)
            for g in range(3):
                for i in range(2):
                    pe.transpose(block(s, 3 * i + g), block(ih_raw[:, g, :], i), ident[:, :])
            pe.transpose(block(s, 6), msg_raw, ident[:, :])
            pe.transpose(block(s, 7), conv1_raw, ident[:, :]).then_inc(setup_filled, 1)
            s = job(J_HH)
            for g in range(3):
                pe.transpose(block(s, g), hh_raw[:, g, :], ident[:, :])
            pe.transpose(s[:, 3 * P:3 * P + S], se_raw[0:S, :], ident[0:S, 0:S]).then_inc(setup_filled, 1)
            for j, k0 in ((J_TAPS0, 0), (J_TAPS1, 8), (J_TAPS2, 16)):
                s = job(j)
                for k in range(k0, min(k0 + 8, TAPS)):
                    last = pe.transpose(block(s, k - k0), conv2_raw[:, :, k], ident[:, :])
                last.then_inc(setup_filled, 1)
            s = job(J_VAL)
            for h in range(H):
                last = pe.matmul(block(s, h), fc_t[:, h, :], fp_raw[:, h, :], start=True, stop=True)
            last.then_inc(setup_filled, 1)
            pe.wait_ge(w_reps_ready, 3)
            for h in range(H):
                for i in range(2):
                    pe.matmul(bias_ps[:, i * H + h:i * H + h + 1], fc_t[:, h, :], qk_raw[:, 1 - i:2 - i], start=True, stop=True)
            pe.matmul(bias_ps[:, 2 * H:3 * H], k_rep, fcb_raw, start=True, stop=True)
            pe.matmul(bias_ps[:, 3 * H:4 * H], q_rep, fcb_raw, start=True, stop=True)
            for h in range(H):
                last = pe.matmul(bout_ps, fcb_rep[:, h, :], fp_raw[:, h, :], start=(h == 0), stop=(h == H - 1))
            last.then_inc(setup_filled, 1)

            def turn_h0(b, after):
                pe.wait_ge(ln[0]["s_out"], b + 1)
                wait(pe, *after)
                for t in range(T):
                    last = pe.transpose(block(slot_b, t), h0[:, t, :], ident[:, :])
                last.then_inc(h0_turned, 1)

            def key_scores(b, parity):
                pe.wait_ge(h0_t_ready, b + 1)
                wait(pe, r_turned_read, b)
                for t in range(T):
                    last = pe.matmul(kq_ps[:, t, :], block(h0_t[parity], t), w_kq[:, :], start=True, stop=True)
                last.then_inc(k_scored, 1)

            def turn_key_max(b):
                pe.wait_ge(k_part_ready, b + 1)
                pe.transpose(kt_ps, k_part[:, :], ident[:, :]).then_inc(k_part_turned, 1)

            def spread_key_max(b):
                pe.wait_ge(k_diag_ready, b + 1)
                pe.matmul(km_ps, ones[0:H, :], k_diag[:, :], start=True, stop=True).then_inc(k_max_spread, 1)

            def turn_r(b):
                pe.wait_ge(r_col_ready, b + 1)
                pe.matmul(rt_ps, r_col[:, :, :].rearrange("p h t -> p (h t)"), ident[:, :], start=True,
                          stop=True).then_inc(r_turned, 1)

            def head_values(b, parity, h, after):
                wait(pe, values_ready, H * b + h)
                for a in after:
                    wait(pe, *a)
                for t in range(T):
                    last = pe.matmul(block(slot_b, t), block(h0_t[parity], t), w_val[:, h, :], start=True, stop=True)
                last.then_inc(z_ready, 1)

            def attend(b, h, side):
                pos, head = tile_pos(b, h), H * b + h
                pe.wait_ge(values_ready, head + 1)
                for t in range(T):
                    for work in side.get(t, ()):
                        work()
                    pe.wait_ge(tile_filled, pos + t + 1)
                    scores = ring[:, head_slot(b, h, t), :]
                    for bank, (first, end) in enumerate(BANKS):
                        if t == 0:
                            wait(pe, head_added, len(BANKS) * (head - 1) + bank + 1)
                        for n in range(first, end):
                            last = pe.matmul(o_block(n), block(scores, n), values[h % 2][:, t, :],
                                             start=(t == 0 and n == first), stop=(t == T - 1),
                                             skip_group_check=True)
                        if t == T - 1 and bank < 2:
                            last.then_inc(bank_done, 1)
                    last.then_inc(tile_used, 1)

            def turn_h1(b, after):
                pe.wait_ge(ln[1]["s_out"], b + 1)
                wait(pe, *after)
                for t in range(T):
                    last = pe.transpose(block(slot_a, t), h1[:, t, :], ident[:, :])
                last.then_inc(h1_turned, 1)

            def kernel_features(b, after):
                pe.wait_ge(h1_t_ready, b + 1)
                wait(pe, *after)
                for i in range(2):
                    last = pe.matmul(half(slot_a, i)[0:96, :], w_dist[:, :], half(h1_t, i), start=True, stop=True)
                last.then_inc(s_product, 1)

            def conv1(b, after):
                pe.wait_ge(h1_t_ready, b + 1)
                wait(pe, *after)
                for i in range(2):
                    last = pe.matmul(half(slot_b, i), conv1_t[:, :], half(h1_t, i), start=True, stop=True)
                last.then_inc(conv1_product, 1)

            def messages(b, after):
                wait(pe, *after)
                for t in range(T):
                    last = pe.matmul(block(slot_a, t), block(h1_t, t), w_msg_t[:, :], start=True, stop=True)
                last.then_inc(msg_product, 1)

            def distances(b, m, slot, after):
                wait(pe, *after)
                if m == 0:
                    pe.wait_ge(dist_ready, b + 1)
                for i in range(2):
                    last = pe.matmul(half(slot, i), block(dist_l, m)[0:DIST_ROWS, :], half(dist_r, i)[0:DIST_ROWS, :],
                                     start=True, stop=True)
                last.then_inc(dist_product, 1)

            def pass_messages(b, m, after):
                if m == 0:
                    wait(pe, *after)
                pe.wait_ge(tile_filled, kernel_tile_pos(b, m) + 1)
                if m == 0:
                    pe.wait_ge(msg_ready, b + 1)
                tile = ring[:, kernel_slot(b, m), :]
                for i in range(2):
                    last = pe.matmul(half(slot_a, i), msg[:, m, :], half(tile, i), start=(m == 0), stop=(m == T - 1),
                                     skip_group_check=True)
                last.then_inc(tile_used, 1)

            def convolve(b, i, after):
                wait(pe, *after)
                if i == 0:
                    pe.wait_ge(conv_in_ready, b + 1)
                for k in range(TAPS):
                    last = pe.matmul(half(slot_a, i), conv2_t[:, k, :], conv_in[:, i * HALF + k:i * HALF + k + HALF],
                                     start=(k == 0), stop=(k == TAPS - 1))
                last.then_inc(conv2_product, 1)

            def gate(slot, terms, done):
                for i in range(2):
                    for n, (w, v) in enumerate(terms):
                        last = pe.matmul(half(slot, i), w, half(v, i), start=(n == 0), stop=(n == len(terms) - 1))
                last.then_inc(done, 1)

            def from_in(g):
                return [(w_ih_t[:, 0, g * D:(g + 1) * D], conv_t), (w_ih_t[:, 1, g * D:(g + 1) * D], nmp_t)]

            def from_hidden(g):
                return [(w_hh_t[:, g * D:(g + 1) * D], h1_t)]

            def gate_r(b, after):
                pe.wait_ge(conv_ready, 2 * b + 2)
                pe.wait_ge(nmp_ready, b + 1)
                wait(pe, *after)
                gate(slot_a, from_in(0) + from_hidden(0), gate_r_product)

            def gate_h(after):
                wait(pe, *after)
                gate(slot_b, from_hidden(2), gate_h_product)

            def gate_z(after):
                wait(pe, *after)
                gate(slot_a, from_in(1) + from_hidden(1), gate_z_product)

            def gate_n(after):
                wait(pe, *after)
                gate(slot_a, from_in(2), gate_n_product)

            def turn_out(b, after):
                pe.wait_ge(gru_ready, b + 1)
                wait(pe, *after)
                for t in range(T):
                    last = pe.transpose(block(slot_a, t), block(z_gate, t), ident[:, :])
                last.then_inc(gru_turned, 1)

            pe.wait_ge(bias_ready, 5)
            turn_h0(0, (setup_copied, SETUP_JOBS))
            key_scores(0, 0)
            turn_key_max(0)
            spread_key_max(0)
            turn_r(0)
            head_values(0, 0, 0, ((h0_t_ready, 1),))

            def frame(b, parity, prev, next_):
                L = b - 1
                for h, following in steps(b, prev, next_):
                    scaled = (values_ready, H * b + h + 2)
                    side = {t: [] for t in range(T)}
                    if prev:
                        if h == 2:
                            side[3] = [lambda: turn_h1(L, (out_ready, b - 1))]
                            side[6] = [lambda: kernel_features(L, (h1_t_ready, b))]
                        elif h in (3, 4):
                            for m in range(AM_SPLIT):
                                k = m + AM_SPLIT * (h - 3)
                                after = (kern_ready, T * L + k)
                                if m == 0:
                                    after = (msg_added, b) if h == 3 else (conv2_added, 2 * L + 1)
                                t = (2, 4, 5, 7)[m] if h == 3 else (1, 3, 5, 7)[m]
                                side[t] = [lambda k=k, after=after: distances(L, k, slot_a, after)]
                        elif h == 6:
                            side[1] = [lambda: gate_r(L, (conv2_added, 2 * L + 2))]
                            side[3] = [lambda: gate_h(scaled)]
                            side[5] = [lambda: gate_z((r_tanh_ready, b))]
                    if next_:
                        if h == 4:
                            side[3].append(lambda: turn_h0(b + 1, scaled))
                            side[6].append(lambda: key_scores(b + 1, 1 - parity))
                        elif h == 5:
                            side[2].append(lambda: spread_key_max(b + 1))
                    if following:
                        fb, fh = following
                        after_b = []
                        if prev and h == 3:
                            after_b = [(conv_in_ready, b)]
                        elif prev and h == 7:
                            after_b = [(gate_h_added, b)]
                        elif next_ and h == 5:
                            after_b = [(h0_t_ready, b + 2)]
                        head_values(fb, parity if fh else 1 - parity, fh, after_b)
                    attend(b, h, side)
                    if prev:
                        if h == 2:
                            conv1(L, scaled)
                            messages(L, (s_read, b))
                        elif h == 3:
                            convolve(L, 0, (kern_ready, T * L + AM_SPLIT))
                        elif h == 4:
                            for m in range(T):
                                pass_messages(L, m, (kern_ready, T * b))
                                if next_ and m == T - 3:
                                    turn_key_max(b + 1)
                        elif h == 5:
                            convolve(L, 1, (nmp_ready, b))
                        elif h == 6:
                            gate_n((z_tanh_ready, b))
                        elif h == 7:
                            turn_out(L, (gate_n_added, b))
                    elif h == 4:
                        turn_key_max(b + 1)
                    if next_ and h == 5:
                        turn_r(b + 1)

            frames(pe, frame)
            L = LAST
            turn_h1(L, (out_ready, L))
            kernel_features(L, (h1_t_ready, B))
            conv1(L, (gate_h_added, L))
            messages(L, (s_read, B))
            distances(L, 0, slot_b, (conv_in_ready, B))
            distances(L, 1, slot_a, (msg_added, B))
            distances(L, 2, slot_b, (kern_ready, T * L + 1))
            distances(L, 3, slot_a, (kern_ready, T * L + 2))
            distances(L, 4, slot_b, (kern_ready, T * L + 3))
            for m in range(T):
                pass_messages(L, m, (kern_ready, T * L + 4))
                if AM_SPLIT < m + 5 < T:
                    distances(L, m + 5, slot_b, (kern_ready, T * L + m + 5))
            convolve(L, 0, (nmp_ready, B))
            convolve(L, 1, (conv2_added, 2 * L + 1))
            gate_r(L, (conv2_added, 2 * L + 2))
            gate_h((kern_ready, T * B))
            gate_z((r_tanh_ready, B))
            gate_n((z_tanh_ready, B))
            turn_out(L, (gate_n_added, B))

        @blk.scalar
        def _(act):
            def copy(dst, src):
                return act.activation(dst, src, ACT.Copy)

            act.wait_ge(setup_filled, J_FC + 1)
            copy(fc_t.rearrange("p h i -> p (h i)"), slot_a[:, :]).then_inc(setup_copied, 1)
            act.wait_ge(setup_filled, J_IH + 1)
            copy(w_ih_t[:, :, :].rearrange("p i n -> p (i n)"), slot_b[:, 0:6 * P])
            copy(w_msg_t[:, :], block(slot_b, 6))
            copy(conv1_t[:, :], block(slot_b, 7)).then_inc(setup_copied, 1)
            act.wait_ge(setup_filled, J_HH + 1)
            act.wait_ge(consts_ready, N_CONSTS)
            copy(w_hh_t[:, :], slot_a[:, 0:3 * P])
            for row, copies in (ROWS_PROD, ROWS_SQ_N, ROWS_SQ_M):
                for c in range(copies):
                    last = copy(w_dist[:, row + c * S:row + (c + 1) * S], slot_a[:, 3 * P:3 * P + S])
            last.then_inc(setup_copied, 1)
            for j, k0, slot in ((J_TAPS0, 0, slot_b), (J_TAPS1, 8, slot_a), (J_TAPS2, 16, slot_b)):
                act.wait_ge(setup_filled, j + 1)
                n = min(8, TAPS - k0)
                copy(conv2_t[:, k0:k0 + n, :].rearrange("p k o -> p (k o)"), slot[:, 0:n * P]).then_inc(setup_copied, 1)
            act.wait_ge(setup_filled, J_VAL + 1)
            copy(w_val[:, :, :].rearrange("p h d -> p (h d)"), slot_a[:, :]).then_inc(setup_copied, 1)
            act.wait_ge(setup_filled, J_SMALL + 1)
            copy(w_kq[:, :], bias_ps[:, 0:2 * H]).then_inc(setup_copied, 1)

            def copy_h0_t(b, parity):
                act.wait_ge(h0_turned, b + 1)
                copy(h0_t[parity][:, :], slot_b[:, :]).then_inc(h0_t_ready, 1)

            def key_weights(b, parity):
                act.wait_ge(kq_shifted, b + 1)
                act.activation(p_half[:, :, :], k_low[:, :, :], ACT.Exp, scale=HALF_SPAN).then_inc(p_half_ready, 1)
                act.activation(v_col[parity][:, :, :], k_low[:, :, :], ACT.Exp, scale=SLOPE)
                act.wait_ge(p_half_ready, b + 1)
                act.activation(p_col[parity][:, :, :], p_half[:, :, :], ACT.Square, scale=HALF_C).then_inc(pv_ready, 1)

            def query_weights(b):
                act.activation(r_half[:, :, :], q_high[:, :, :], ACT.Exp, scale=-HALF_SPAN).then_inc(r_half_ready, 1)
                act.wait_ge(r_half_ready, b + 1)
                wait(act, r_turned, b)
                act.activation(r_col[:, :, :], r_half[:, :, :], ACT.Square, scale=HALF_C).then_inc(r_col_ready, 1)

            def copy_r(b):
                act.wait_ge(r_turned, b + 1)
                wait(act, r_stored, 16 * b)
                copy(r_turned_sb[:, :], rt_ps).then_inc(r_turned_read, 1)

            def store_r(b):
                act.wait_ge(r_turned_read, b + 1)
                for i in range(R_ROWS):
                    wait(act, r_loaded[i], 16 * (H // R_ROWS) * b)
                act.dma_start(r_dram.rearrange("h (t n) -> (h t) n", t=T), r_turned_sb[:, :]).then_inc(r_stored, 16)

            def spread_r(b, h):
                if h == 0:
                    act.wait_ge(r_stored, 16 * (b + 1))
                if h >= R_ROWS:
                    act.wait_ge(tile_filled, tile_pos(b, h - R_ROWS) + T)
                elif not (isinstance(b, int) and b == 0):
                    act.wait_ge(tile_filled, tile_pos(b - 1, h + H - R_ROWS) + T)
                act.dma_start(r_row[h % R_ROWS][:, :], r_dram[h:h + 1, :].to_broadcast([P, N]))\
                    .then_inc(r_loaded[h % R_ROWS], 16)

            def tanh_y(b):
                act.wait_ge(head_added, len(BANKS) * (H * b + H))
                wait(act, gru_ready, b)
                act.activation(y_tanh, y[:, :, :], ACT.Tanh, scale=0.5).then_inc(y_tanh_ready, 1)

            def copy_h1_t(b):
                act.wait_ge(h1_turned, b + 1)
                wait(act, gru_ready, b)
                copy(h1_t[:, :], slot_a[:, :]).then_inc(h1_t_ready, 1)

            def features(b):
                act.wait_ge(s_product, b + 1)
                if not (isinstance(b, int) and b == 0):
                    act.wait_ge(tile_filled, kernel_tile_pos(b - 1, T - KERNS + 1) + 1)
                for side, rows, func in ((0, (0, 64), ACT.Identity), (0, (64, DIST_ROWS), ACT.Square),
                                         (1, (0, 32), ACT.Identity), (1, (32, 64), ACT.Square),
                                         (1, (64, DIST_ROWS), ACT.Identity)):
                    r0, r1 = rows
                    scale = dist_scale[r0:r1, side:side + 1] if func == ACT.Identity else 1.0
                    last = act.activation(kern[side][r0:r1, :], slot_a[r0:r1, :], func,
                                          bias=b_dist[r0:r1, side:side + 1], scale=scale)
                last.then_inc(s_read, 1)
                act.wait_ge(conv1_product, b + 1)
                wait(act, conv2_product, 2 * b)
                act.activation(conv_in[:, PAD:PAD + N], slot_b[:, :], ACT.Relu, bias=bn_aff[:, 0, 1:2],
                               scale=bn_aff[:, 0, 0:1]).then_inc(conv_in_ready, 1)
                act.wait_ge(s_read, b + 1)
                wait(act, dist_product, T * b)
                copy(dist_l[0:DIST_ROWS, :], kern[0][0:DIST_ROWS, :])
                copy(dist_r[0:DIST_ROWS, :], kern[1][0:DIST_ROWS, :]).then_inc(s_hi_ready, 1)

            def kernel_block(b, m, slot):
                act.wait_ge(dist_product, T * b + m + 1)
                if m == KERNS - 1:
                    wait(act, gru_turned, b)
                if m >= KERNS:
                    act.wait_ge(tile_filled, kernel_tile_pos(b, m - KERNS) + 1)
                elif not (isinstance(b, int) and b == 0):
                    act.wait_ge(tile_filled, kernel_tile_pos(b - 1, T - KERNS + m) + 1)
                act.activation(kern[m % KERNS][:, :], slot[:, :], ACT.Exp).then_inc(kern_ready, 1)

            def copy_nmp(b, last_batch=False):
                act.wait_ge(tile_used, kernel_tile_pos(b, T - 1) + 1 if last_batch else used(b + 1, KERNEL_AT[-1]))
                wait(act, gate_n_product, b)
                copy(nmp_t[:, :], slot_a[:, :]).then_inc(nmp_ready, 1)

            def conv_relu(b, i):
                act.wait_ge(conv2_added, 2 * b + i + 1)
                act.activation(half(conv_t, i), half(conv_t, i), ACT.Relu, bias=bn_aff[:, 1, 1:2]).then_inc(conv_ready, 1)

            def gate_tanhs(b):
                act.wait_ge(gate_r_product, b + 1)
                act.activation(gate_a[:, :], slot_a[:, :], ACT.Tanh, bias=b_gate[:, 0:1], scale=0.5)\
                   .then_inc(r_tanh_ready, 1)
                act.wait_ge(gate_z_product, b + 1)
                wait(act, gru_turned, b)
                act.activation(z_gate[:, :], slot_a[:, :], ACT.Tanh, bias=b_gate[:, 1:2], scale=0.5)\
                   .then_inc(z_tanh_ready, 1)

            def new_state(b):
                act.wait_ge(gate_n_added, b + 1)
                act.activation(gate_a[:, :], gate_a[:, :], ACT.Tanh, bias=b_gate_in[:, 0, 2:3]).then_inc(n_ready, 1)

            act.wait_ge(bias_ready, 5)
            copy_h0_t(0, 0)
            key_weights(0, 0)
            query_weights(0)
            copy_r(0)
            store_r(0)
            for h in range(R_ROWS):
                spread_r(0, h)

            def frame(b, parity, prev, next_):
                L = b - 1
                for h, following in steps(b, prev, next_):
                    if prev:
                        if h == 0:
                            tanh_y(L)
                        elif h == 4:
                            conv_relu(L, 0)
                        elif h == 7:
                            new_state(L)
                    if h + R_ROWS < H:
                        spread_r(b, h + R_ROWS)
                    elif next_:
                        spread_r(b + 1, h + R_ROWS - H)
                    if next_ and h == 5:
                        key_weights(b + 1, 1 - parity)
                        query_weights(b + 1)
                        copy_r(b + 1)
                        store_r(b + 1)
                    if prev:
                        if h == 2:
                            copy_h1_t(L)
                            features(L)
                        elif h == 3:
                            kernel_block(L, 0, slot_a)
                            kernel_block(L, 1, slot_a)
                            kernel_block(L, 2, slot_a)
                            kernel_block(L, 3, slot_a)
                        elif h == 4:
                            kernel_block(L, AM_SPLIT, slot_a)
                    if next_ and h == 4:
                        copy_h0_t(b + 1, 1 - parity)
                    if prev:
                        if h == 4:
                            for m in range(AM_SPLIT + 1, T):
                                kernel_block(L, m, slot_a)
                            copy_nmp(L)
                        elif h == 5:
                            conv_relu(L, 1)
                        elif h == 6:
                            gate_tanhs(L)

            frames(act, frame)
            L = LAST
            tanh_y(L)
            copy_h1_t(L)
            features(L)
            for m in range(T):
                kernel_block(L, m, slot_a if m in (1, 3) else slot_b)
            copy_nmp(L, True)
            conv_relu(L, 0)
            conv_relu(L, 1)
            gate_tanhs(L)
            new_state(L)

        @blk.vector
        def _(dve):
            dve.wait_ge(consts_ready, N_CONSTS)
            dve.wait_ge(w_loaded, 16 * N_LOADS)
            dve.tensor_scalar(q_rep, ones[:, :], qk_raw[:, 0:1], None, ALU.mult).then_inc(w_reps_ready, 1)
            dve.tensor_scalar(k_rep, ones[:, :], qk_raw[:, 1:2], None, ALU.mult).then_inc(w_reps_ready, 1)
            for h in range(H):
                last = dve.tensor_scalar(fcb_rep[:, h, :], ones[:, :], fcb_raw[:, h:h + 1], None, ALU.mult)
            last.then_inc(w_reps_ready, 1)
            dve.tensor_scalar(bn_tmp[:, :, 0], bn[:, :, 3], EPS, None, ALU.add).then_inc(bn_step, 1)
            dve.wait_ge(bn_step, 2)
            dve.tensor_tensor(bn_aff[:, :, 0], bn[:, :, 0], bn_tmp[:, :, 1], ALU.mult).then_inc(bn_step, 1)
            dve.wait_ge(bn_step, 3)
            dve.tensor_tensor(bn_tmp[:, :, 0], bn[:, :, 2], bn_aff[:, :, 0], ALU.mult).then_inc(bn_step, 1)
            dve.wait_ge(bn_step, 4)
            dve.tensor_tensor(bn_aff[:, :, 1], bn[:, :, 1], bn_tmp[:, :, 0], ALU.subtract).then_inc(bias_ready, 1)
            dve.tensor_tensor(b_gate[:, :], b_gate_in[:, 0, 0:2], b_gate_in[:, 1, 0:2], ALU.add).then_inc(bn_step, 1)
            dve.wait_ge(bn_step, 5)
            dve.tensor_scalar(b_gate[:, :], b_gate[:, :], 0.5, None, ALU.mult).then_inc(bias_ready, 1)
            dve.tensor_scalar(b_dist[0:32, 0:1], b_dist[0:32, 0:1], 2.0, None, ALU.mult).then_inc(bias_ready, 1)
            for i, rows in enumerate(((S, 3 * S), (64 + S, 64 + 2 * S), (2 * S, 4 * S), (32 + S, 32 + 2 * S))):
                last = dve.tensor_reduce(lo_rows[:, i:i + 1], ident[:, rows[0]:rows[1]], AX.X, ALU.add)
            last.then_inc(bn_step, 1)
            dve.wait_ge(bn_step, 6)
            for i in range(2):
                last = dve.tensor_tensor(minus_lo[:, i:i + 1], lo_rows[:, 2 * i:2 * i + 1],
                                         lo_rows[:, 2 * i + 1:2 * i + 2], ALU.add)
            last.then_inc(bn_step, 1)
            dve.wait_ge(bn_step, 7)
            dve.tensor_scalar(minus_lo[:, :], minus_lo[:, :], -1.0, None, ALU.mult).then_inc(bn_step, 1)
            dve.wait_ge(bn_step, 8)

            def moments(layer, b, src):
                s = ln[layer]
                for t in range(T):
                    last = dve.bn_stats(s["stats"][:, t, :], src[:, t, :])
                last.then_inc(s["s_stats"], 1)
                wait_apart(dve, s["s_stats"], b + 1, passed["vector"])
                for t in range(T):
                    last = dve.bn_aggr(s["mv"][:, t, :], s["stats"][:, t, :])
                last.then_inc(s["s_mv"], 1)

            def normalise(layer, b, src, dst):
                s = ln[layer]
                dve.wait_ge(s["s_rstd"], b + 1)
                for t in range(T):
                    last = dve.tensor_scalar(dst[:, t, :], src[:, t, :], s["mv"][:, t, 0:1], s["rstd"][:, t:t + 1],
                                             ALU.subtract, ALU.mult)
                last.then_inc(s["s_mid"], 1)
                dve.wait_ge(s["s_mid"], b + 1)
                dve.tensor_scalar(dst[:, :, :], dst[:, :, :], 0.0, None, ALU.max).then_inc(s["s_out"], 1)

            def first_norm(b, parity):
                dve.wait_ge(x_loaded, 16 * (b + 1))
                wait(dve, y_ready, b)
                moments(0, b, x_in[parity])
                normalise(0, b, x_in[parity], h0)

            def keys(b):
                dve.wait_ge(k_scored, b + 1)
                wait(dve, pv_ready, b)
                dve.tensor_tensor(kq_sb[:, :, :], kq_ps, b_kq[:, None, :].to_broadcast([P, T, 2 * H]), ALU.add)\
                   .then_inc(k_ready, 1)
                dve.wait_ge(k_ready, b + 1)
                dve.tensor_reduce(k_part[:, :], kq_sb[:, :, 0:H].rearrange("p t h -> p h t"), AX.X, ALU.max)\
                   .then_inc(k_part_ready, 1)

            def key_max(b):
                dve.wait_ge(k_part_turned, b + 1)
                dve.tensor_reduce(k_max[:, :], kt_ps, AX.X, ALU.max).then_inc(k_max_ready, 1)
                dve.wait_ge(k_max_ready, b + 1)
                dve.tensor_scalar(k_diag[:, :], ident[0:H, 0:H], k_max[:, 0:1], None, ALU.mult).then_inc(k_diag_ready, 1)

            def key_shift(b):
                dve.wait_ge(k_max_spread, b + 1)
                dve.tensor_copy(k_shift[:, :], km_ps).then_inc(k_shift_ready, 1)
                dve.wait_ge(k_shift_ready, b + 1)
                wait(dve, r_half_ready, b)
                dve.tensor_tensor(q_high[:, :, :].rearrange("p h t -> p t h"), kq_sb[:, :, H:2 * H],
                                  k_shift[:, None, :].to_broadcast([P, T, H]), ALU.add).then_inc(q_shifted, 1)
                dve.tensor_tensor(k_low[:, :, :], kq_sb[:, :, 0:H], k_shift[:, None, :].to_broadcast([P, T, H]),
                                  ALU.subtract)
                dve.wait_ge(q_shifted, b + 1)
                dve.tensor_scalar(q_high[:, :, :], q_high[:, :, :], 0.0, None, ALU.max).then_inc(kq_shifted, 1)

            def scale_values(b, parity, h):
                dve.wait_ge(z_ready, H * b + h + 1)
                if h == 0:
                    dve.wait_ge(pv_ready, b + 1)
                weights = v_col[parity][:, :, h:h + 1]
                dve.tensor_copy(values[h % 2][:, :, D:W], weights)
                dve.tensor_tensor(values[h % 2][:, :, 0:D], slot_b[:, :].rearrange("p (t d) -> p t d", t=T),
                                  weights.to_broadcast([P, T, D]), ALU.mult).then_inc(values_ready, 1)

            def score_tiles(b, parity, h):
                if h == 0:
                    dve.wait_ge(adj_turned, 16 * T * (b + 1))
                dve.wait_ge(r_loaded[h % R_ROWS], 16 * (H // R_ROWS * b + h // R_ROWS + 1))
                for t in range(T):
                    if isinstance(b, int) and b == 0:
                        wait(dve, tile_used, T * h + t + 1 - RING)
                    else:
                        dve.wait_ge(tile_used, place_free(b, HEAD_AT[h] + t))
                    dve.scalar_tensor_tensor(out=ring[:, head_slot(b, h, t), :], in0=r_row[h % R_ROWS][:, :],
                                             scalar=p_col[parity][:, t, h:h + 1], in1=adj_t[parity][:, t, :],
                                             op0=ALU.max, op1=ALU.mult).then_inc(tile_filled, 1)

            def add_head(b, h):
                head = H * b + h
                for bank, (first, end) in enumerate(BANKS):
                    if bank < 2:
                        dve.wait_ge(bank_done, 2 * head + bank + 1)
                    else:
                        dve.wait_ge(tile_used, head_used(b, h, T - 1))
                    if bank == 0:
                        if h == 0:
                            dve.wait_ge(y_ready, b + 1)
                        else:
                            dve.wait_ge(head_added, len(BANKS) * head)
                    sums = o_ps[:, bank, 0:(end - first) * W].rearrange("p (n w) -> p n w", w=W)[:, :, D]
                    dve.reciprocal(rden[:, first:end], sums).then_inc(rden_ready, 1)
                    dve.wait_ge(rden_ready, len(BANKS) * head + bank + 1)
                    for n in range(first, end):
                        last = dve.scalar_tensor_tensor(out=y[:, n, :], in0=o_block(n)[:, 0:D],
                                                        scalar=rden[:, n:n + 1], in1=y[:, n, :], op0=ALU.mult,
                                                        op1=ALU.add)
                    last.then_inc(head_added, 1)

            def first_output(b, parity):
                dve.wait_ge(y_tanh_ready, b + 1)
                wait(dve, out_ready, b)
                dve.scalar_tensor_tensor(out=x1[:, :, :], in0=y_tanh, scalar=0.5, in1=x_in[parity][:, :, :],
                                         op0=ALU.mult, op1=ALU.add).then_inc(x1_half_ready, 1)
                dve.wait_ge(x1_half_ready, b + 1)
                dve.tensor_scalar(x1[:, :, :], x1[:, :, :], 0.5, None, ALU.add).then_inc(x1_ready, 1)
                dve.wait_ge(x1_ready, b + 1)
                moments(1, b, x1)

            def split_features(b):
                dve.wait_ge(s_hi_ready, b + 1)
                for i, buf in enumerate((dist_l, dist_r)):
                    last = dve.scalar_tensor_tensor(out=buf[0:DIST_ROWS, :], in0=buf[0:DIST_ROWS, :].bitcast(F32),
                                                    scalar=minus_lo[0:DIST_ROWS, i:i + 1],
                                                    in1=kern[i][0:DIST_ROWS, :], op0=ALU.mult, op1=ALU.add)
                last.then_inc(dist_ready, 1)

            def messages(b):
                dve.wait_ge(msg_product, b + 1)
                dve.tensor_tensor(msg[:, :, :], slot_a[:, :].rearrange("p (t d) -> p t d", t=T),
                                  b_msg_row[:, None, :].to_broadcast([P, T, D]), ALU.add).then_inc(msg_added, 1)
                dve.wait_ge(msg_added, b + 1)
                dve.tensor_scalar(msg[:, :, :], msg[:, :, :], 0.0, None, ALU.max).then_inc(msg_ready, 1)

            def kernel_tile(b, parity, m):
                dve.wait_ge(kern_ready, T * b + m + 1)
                if isinstance(b, int) and b == LAST:
                    dve.wait_ge(tile_used, kernel_tile_pos(b, m) + 1 - RING)
                else:
                    dve.wait_ge(tile_used, place_free(b + 1, KERNEL_AT[m]))
                dve.tensor_tensor(ring[:, kernel_slot(b, m), :], kern[m % KERNS][:, :], adj_t[parity][:, m, :],
                                  ALU.mult).then_inc(tile_filled, 1)

            def conv_add(b, i):
                dve.wait_ge(conv2_product, 2 * b + i + 1)
                if i == 0:
                    wait(dve, out_stored, 16 * b)
                dve.scalar_tensor_tensor(out=half(conv_t, i), in0=half(slot_a, i), scalar=bn_aff[:, 1, 0:1],
                                         in1=half(h1_t, i), op0=ALU.mult, op1=ALU.add).then_inc(conv2_added, 1)

            def gate_hidden(b):
                dve.wait_ge(r_tanh_ready, b + 1)
                dve.tensor_scalar(gate_a[:, :], gate_a[:, :], 0.5, 0.5, ALU.mult, ALU.add).then_inc(gate_r_ready, 1)
                dve.wait_ge(gate_r_ready, b + 1)
                dve.wait_ge(gate_h_product, b + 1)
                dve.scalar_tensor_tensor(out=gate_a[:, :], in0=slot_b[:, :], scalar=b_gate_in[:, 1, 2:3],
                                         in1=gate_a[:, :], op0=ALU.add, op1=ALU.mult).then_inc(gate_h_added, 1)

            def gru(b):
                dve.wait_ge(gate_h_added, b + 1)
                dve.wait_ge(gate_n_product, b + 1)
                dve.tensor_tensor(gate_a[:, :], slot_a[:, :], gate_a[:, :], ALU.add).then_inc(gate_n_added, 1)
                dve.wait_ge(n_ready, b + 1)
                dve.tensor_tensor(diff_t, h1_t[:, :], gate_a[:, :], ALU.subtract).then_inc(diff_ready, 1)
                dve.wait_ge(diff_ready, b + 1)
                dve.scalar_tensor_tensor(out=z_gate[:, :], in0=z_gate[:, :], scalar=1.0, in1=diff_t,
                                         op0=ALU.add, op1=ALU.mult).then_inc(z_diff_ready, 1)
                dve.wait_ge(z_diff_ready, b + 1)
                dve.scalar_tensor_tensor(out=z_gate[:, :], in0=z_gate[:, :], scalar=0.5, in1=gate_a[:, :],
                                         op0=ALU.mult, op1=ALU.add).then_inc(gru_ready, 1)

            def add_out(b):
                dve.wait_ge(gru_turned, b + 1)
                dve.tensor_tensor(out_sb, slot_a[:, :].rearrange("p (t d) -> p t d", t=T), x1[:, :, :],
                                  ALU.add).then_inc(out_ready, 1)

            first_norm(0, 0)
            dve.wait_ge(setup_copied, SETUP_JOBS)
            dve.tensor_scalar(b_kq[:, 0:H], bias_ps[:, 2 * H:3 * H], qk_b[:, 1:2], None, ALU.add)
            dve.tensor_scalar(b_kq[:, H:2 * H], bias_ps[:, 3 * H:4 * H], qk_b[:, 0:1], None, ALU.add)\
                .then_inc(bias_ready, 1)
            dve.tensor_tensor(b_out[:, :], bout_ps, b_out[:, :], ALU.add).then_inc(bias_ready, 1)
            dve.wait_ge(bias_ready, 5)
            keys(0)
            key_max(0)
            key_shift(0)
            scale_values(0, 0, 0)
            score_tiles(0, 0, 0)

            def frame(b, parity, prev, next_):
                L = b - 1
                for h, following in steps(b, prev, next_):
                    if following:
                        fb, fh = following
                        fp = parity if fh else 1 - parity
                        scale_values(fb, fp, fh)
                        score_tiles(fb, fp, fh)
                    if prev and h == 6:
                        gate_hidden(L)
                    if next_ and h == 5:
                        key_shift(b + 1)
                    add_head(b, h)
                    if prev:
                        if h == 0:
                            first_output(L, 1 - parity)
                        elif h == 1:
                            normalise(1, L, x1, h1)
                        elif h == 2:
                            messages(L)
                            split_features(L)
                        elif h == 3:
                            for m in range(AM_SPLIT):
                                kernel_tile(L, 1 - parity, m)
                        elif h == 4:
                            for m in range(AM_SPLIT, T):
                                kernel_tile(L, 1 - parity, m)
                        elif h == 5:
                            conv_add(L, 1)
                        elif h == 6:
                            gru(L)
                        elif h == 7:
                            add_out(L)
                    if next_:
                        if h == 3:
                            first_norm(b + 1, 1 - parity)
                        elif h == 4:
                            keys(b + 1)
                            key_max(b + 1)
                    if prev and h == 3:
                        conv_add(L, 0)

            frames(dve, frame)
            L = LAST
            first_output(L, 1)
            normalise(1, L, x1, h1)
            split_features(L)
            messages(L)
            for m in range(T):
                kernel_tile(L, 1, m)
            conv_add(L, 0)
            conv_add(L, 1)
            gate_hidden(L)
            gru(L)
            add_out(L)


_INS = ["x", "adj", "L0_gnn_fc_w", "L0_gnn_fc_b", "L0_gnn_q_w", "L0_gnn_q_b", "L0_gnn_k_w", "L0_gnn_k_b",
        "L0_gnn_fp_w", "L0_gnn_fp_b", "L1_gnn_w_se", "L1_gnn_b_se", "L1_gnn_conv1_w", "L1_gnn_bn1_g",
        "L1_gnn_bn1_b", "L1_gnn_bn1_m", "L1_gnn_bn1_v", "L1_gnn_conv2_w", "L1_gnn_bn2_g", "L1_gnn_bn2_b",
        "L1_gnn_bn2_m", "L1_gnn_bn2_v", "L1_gnn_w_msg", "L1_gnn_b_msg", "L1_gnn_w_ih", "L1_gnn_b_ih",
        "L1_gnn_w_hh", "L1_gnn_b_hh"]


def kernel(**inputs):
    import numpy as _np
    import concourse.bacc as _bacc
    from concourse import mybir as _mybir
    from concourse.bass_utils import run_bass_kernel_spmd as _run

    nc = _bacc.Bacc("TRN2", target_bir_lowering=False, num_devices=1)
    arrays, args = {}, []
    for name in _INS:
        a = _np.ascontiguousarray(inputs[name])
        arrays[f"in_{name}_dram"] = a
        args.append(nc.dram_tensor(f"in_{name}_dram", a.shape, _mybir.dt.from_np(a.dtype), kind="ExternalInput").ap())
    shape = arrays["in_x_dram"].shape
    args.append(nc.dram_tensor("out_0_dram", shape, _mybir.dt.float32, kind="ExternalOutput").ap())
    heads = arrays["in_L0_gnn_fc_w_dram"].shape[1] // shape[2]
    args.append(nc.dram_tensor("query_weights_dram", (heads, shape[1]), _mybir.dt.float32, kind="Internal").ap())
    build(nc, *args)
    r = _run(nc, [arrays], core_ids=[0])
    return r.results[0]["out_0_dram"]
```

```python
import math
from contextlib import ExitStack

import concourse.bass as bass
from concourse import mybir

F32 = mybir.dt.float32
F32R = mybir.dt.float32r
BF16 = mybir.dt.bfloat16
ALU = mybir.AluOpType
ACT = mybir.ActivationFunctionType
AX = mybir.AxisListType

P = 128
R_ROWS = 2
KERNS = 4
RING = 9
TAPS = 17
PAD = TAPS // 2
EPS = 1e-5
SLOPE = 0.01
HALF_C = math.exp(30.0)
HALF_SPAN = (1.0 - SLOPE) / 2


def wait(eng, sem, value):
    if isinstance(value, int) and value <= 0:
        return
    eng.wait_ge(sem, value)


def wait_apart(eng, sem, value, passed):
    eng.wait_ge(sem, value)
    eng.sem_inc(passed, 1)


def build(nc, x, adj, fc_w, fc_b, q_w, q_b, k_w, k_b, fp_w, fp_b, w_se, b_se, conv1_w, bn1_g, bn1_b, bn1_m,
          bn1_v, conv2_w, bn2_g, bn2_b, bn2_m, bn2_v, w_msg, b_msg, w_ih, b_ih, w_hh, b_hh, out, r_dram):
    B, N, D = x.shape
    H = fc_w.shape[1] // D
    T = N // P
    HALF = N // 2
    W = D + 1
    S = w_se.shape[0]
    LAST = B - 1
    assert D == P and H == 8 and T == 8 and HALF == 512 and B % 2 == 0
    AM_SPLIT = T // 2
    SCALED_BY_ACT = (0, 1, 2, 7)
    ROWS_PROD, ROWS_SQ_N, ROWS_SQ_M = (0, 4), (32, 2), (64, 2)
    DIST_ROWS = 64 + 2 * S
    assert 4 * S <= 32
    PER = (H + 1) * T

    HEAD_AT = [0, 8, 16, 24, 32, 48, 56, 64]
    KERNEL_AT = list(range(40, 48))

    def frame_start(b):
        return PER * b - T

    def tile_pos(b, h):
        if isinstance(b, int) and b == 0:
            return T * h
        return frame_start(b) + HEAD_AT[h]

    def kernel_tile_pos(b, m):
        if isinstance(b, int) and b == LAST:
            return frame_start(b + 1) + m
        return frame_start(b + 1) + KERNEL_AT[m]

    def used(b, at):
        return frame_start(b) + at + 1

    def head_used(b, h, t):
        if isinstance(b, int) and b == 0:
            return T * h + t + 1
        return used(b, HEAD_AT[h] + t)

    def place_free(b, at):
        return used(b, at - RING)

    def tile_slot(pos0, t):
        return (pos0 + t) % RING

    def head_slot(b, h, t):
        return tile_slot(tile_pos(b if isinstance(b, int) else 1, h), t)

    def kernel_slot(b, m):
        return tile_slot(kernel_tile_pos(b if isinstance(b, int) else 0, m), 0)

    with ExitStack() as ctx:
        def sb(name, shape, dt=F32):
            return ctx.enter_context(nc.sbuf_tensor(name, shape, dt))

        def psum(name, shape):
            return ctx.enter_context(nc.psum_tensor(name, shape, F32))

        def sem(name):
            return ctx.enter_context(nc.semaphore(name))

        ring = sb("ring", [P, RING, N])
        adj_t = [sb(f"adj_t{i}", [P, T, N], BF16) for i in range(2)]
        adj_rows = sb("adj_rows", [P, T // 2, N], BF16)
        x_in = [sb(f"x_in{i}", [P, T, D]) for i in range(2)]
        h0 = sb("h0", [P, T, D])
        h0_t = [sb(f"h0_t{i}", [P, N]) for i in range(2)]
        y = sb("y", [P, T, D])
        values = [sb(f"values{i}", [P, T, W]) for i in range(2)]
        r_row = [sb(f"r_row{i}", [P, N]) for i in range(R_ROWS)]
        kq_sb = sb("kq_sb", [P, T, 2 * H])
        k_low = sb("k_low", [P, T, H])
        q_high = sb("q_high", [P, H, T])
        r_col = q_high
        p_col = [sb(f"p_col{i}", [P, T, H]) for i in range(2)]
        v_col = [sb(f"v_col{i}", [P, T, H]) for i in range(2)]
        k_part = sb("k_part", [P, H])
        k_max = sb("k_max", [H, 1])
        k_diag = sb("k_diag", [H, H])
        k_shift = sb("k_shift", [P, H])
        rden = sb("rden", [P, T + 1])
        x1 = sb("x1", [P, T, D])
        h1 = sb("h1", [P, T, D])
        msg = h1
        h1_t = sb("h1_t", [P, N])
        dist_l = sb("dist_l", [P, N], F32R)
        dist_r = sb("dist_r", [P, N], F32R)
        conv_hi = sb("conv_hi", [P, N + 2 * PAD], F32R)
        conv_lo = sb("conv_lo", [P, N + 2 * PAD], F32R)
        kern_all = sb("kern", [P, KERNS - 1, N])
        kern = [kern_all[:, i, :] for i in range(KERNS - 1)]
        r_turned_sb = kern[2][0:H * T, P:2 * P]
        nmp_hi, nmp_lo = dist_l, dist_r
        x_conv_hi = sb("x_conv_hi", [P, N], F32R)
        x_conv_lo = sb("x_conv_lo", [P, N], F32R)
        out_sb = h1
        gate_a = sb("gate_a", [P, N])
        x_conv = gate_a
        z_gate = sb("z_gate", [P, N])
        kern.append(z_gate)
        diff_t = h1[:, :, :].rearrange("p t d -> p (t d)")
        y_tanh = gate_a[:, :].rearrange("p (t d) -> p t d", t=T)
        ln = []
        for i in range(2):
            ln.append(dict(stats=sb(f"ln{i}_stats", [P, T, 6]), mv=sb(f"ln{i}_mv", [P, T, 2]),
                           var=sb(f"ln{i}_var", [P, T]), rstd=sb(f"ln{i}_rstd", [P, T]),
                           s_stats=sem(f"ln{i}_stats_ready"), s_mv=sem(f"ln{i}_moments_ready"),
                           s_var=sem(f"ln{i}_var_ready"), s_rstd=sem(f"ln{i}_rstd_ready"),
                           s_mid=sem(f"ln{i}_normalised"), s_out=sem(f"ln{i}_relu_ready")))

        ident = sb("ident", [P, P])
        ident_16 = sb("ident_16", [P, P], BF16)
        ones = sb("ones", [P, P])
        minus_half = sb("minus_half", [P, T])
        w_val = sb("w_val", [P, H, D])
        w_kq = sb("w_kq", [P, 2 * H])
        b_kq = sb("b_kq", [P, 2 * H])
        b_out = sb("b_out", [P, D])
        w_dist = sb("w_dist", [P, 3 * 32])
        b_dist = sb("b_dist", [3 * 32, 2])
        dist_scale = sb("dist_scale", [3 * 32, 2])
        lo_rows = sb("lo_rows", [P, 4])
        minus_lo = sb("minus_lo", [P, 2])
        conv1_t = sb("conv1_t", [P, D])
        conv2_hi = sb("conv2_hi", [P, TAPS, D], F32R)
        conv2_lo = sb("conv2_lo", [P, TAPS, D], F32R)
        w_msg_t = sb("w_msg_t", [P, D])
        b_msg_row = sb("b_msg_row", [P, D])
        w_ih_hi = sb("w_ih_hi", [P, 2, 3 * D], F32R)
        w_ih_lo = sb("w_ih_lo", [P, 2, 3 * D], F32R)
        w_hh_t = sb("w_hh_t", [P, 3 * D])
        bn = sb("bn", [P, 2, 4])
        bn_aff = sb("bn_aff", [P, 2, 2])
        bn_tmp = sb("bn_tmp", [P, 2, 2])
        b_gate_in = sb("b_gate_in", [P, 2, 3])
        b_gate = sb("b_gate", [P, 2])
        qk_b = sb("qk_b", [P, 2])

        room = ring[:, :, :].rearrange("p r n -> p (r n)")
        taken = 0

        def raw(cols):
            nonlocal taken
            taken += cols
            assert taken <= RING * N
            return room[:, taken - cols:taken]

        fc_raw = raw(H * D)
        fp_raw = raw(H * D).rearrange("p (h d) -> p h d", h=H)
        ih_raw = z_gate[:, 0:3 * 2 * D].rearrange("p (g i) -> p g i", g=3)
        hh_raw = h1_t[:, 0:3 * D].rearrange("p (g i) -> p g i", g=3)
        msg_raw, conv1_raw, se_raw = (h1_t[:, (3 + i) * D:(4 + i) * D] for i in range(3))
        conv2_raw = kern_all[:, :, :].rearrange("p k n -> p (k n)")[:, 0:D * TAPS].rearrange("p (i k) -> p i k", k=TAPS)
        fc_t = raw(H * D).rearrange("p (h i) -> p h i", h=H)
        fcb_raw = raw(H)
        qk_raw = raw(2)
        q_rep = raw(P)
        k_rep = raw(P)
        fcb_rep = raw(H * P).rearrange("p (h c) -> p h c", h=H)

        o_ps = psum("o_ps", [P, 3, 512])
        slot_a = psum("slot_a", [P, N])
        slot_b = psum("slot_b", [P, N])
        small = psum("small", [P, 512])
        kq_ps = small[:, 0:T * 2 * H].rearrange("p (t h) -> p t h", t=T)
        kt_ps = small[0:H, 128:128 + P]
        km_ps = small[:, 256:256 + H]
        bias_ps = small[:, 320:320 + 4 * H]
        rt_ps = small[0:H * T, 384:384 + P]

        bout_ps = o_ps[:, 0, 0:D]

        BANKS = [(0, 3), (3, 6), (6, 8)]

        slot_o = o_ps[:, 0:2, :].rearrange("p c n -> p (c n)")

        def o_block(n):
            return o_ps[:, n // 3, (n % 3) * W:(n % 3 + 1) * W]

        consts_ready = sem("consts_ready")
        fc_loaded = sem("fc_loaded")
        w_loaded = sem("w_loaded")
        w_rest_loaded = sem("w_rest_loaded")
        w_late_loaded = sem("w_late_loaded")
        w_reps_ready = sem("w_reps_ready")
        setup_filled = sem("setup_filled")
        setup_copied = sem("setup_copied")
        taps_hi_ready = sem("taps_hi_ready")
        w_ih_split = sem("w_ih_split")
        taps_split = sem("taps_split")
        bias_ready = sem("bias_ready")
        bias_late_ready = sem("bias_late_ready")
        bn_step = sem("bn_step")
        passed = {e: sem(f"{e}_waits_passed") for e in ("pool", "vector")}
        x_loaded = sem("x_loaded")
        adj_cast = sem("adj_cast")
        ident_16_ready = sem("ident_16_ready")
        adj_turned = sem("adj_turned")
        adj_t_ready = sem("adj_t_ready")
        h0_turned = sem("h0_turned")
        h0_t_ready = sem("h0_t_ready")
        k_scored = sem("k_scored")
        k_ready = sem("k_ready")
        k_part_ready = sem("k_part_ready")
        k_part_turned = sem("k_part_turned")
        k_max_ready = sem("k_max_ready")
        k_diag_ready = sem("k_diag_ready")
        k_max_spread = sem("k_max_spread")
        k_shift_ready = sem("k_shift_ready")
        q_shifted = sem("q_shifted")
        kq_shifted = sem("kq_shifted")
        p_half_ready = sem("p_half_ready")
        pv_ready = sem("pv_ready")
        r_half_ready = sem("r_half_ready")
        r_col_ready = sem("r_col_ready")
        r_turned = sem("r_turned")
        r_turned_read = sem("r_turned_read")
        r_stored = sem("r_stored")
        r_loaded = [sem(f"r_loaded{i}") for i in range(R_ROWS)]
        z_ready = sem("z_ready")
        values_ready = sem("values_ready")
        tile_filled = sem("tile_filled")
        tile_used = sem("tile_used")
        rden_ready = sem("rden_ready")
        bank_done = sem("bank_done")
        head_added = sem("head_added")
        y_ready = sem("y_ready")
        y_tanh_ready = sem("y_tanh_ready")
        x1_half_ready = sem("x1_half_ready")
        x1_ready = sem("x1_ready")
        h1_turned = sem("h1_turned")
        h1_t_ready = sem("h1_t_ready")
        s_product = sem("s_product")
        s_read = sem("s_read")
        s_hi_ready = sem("s_hi_ready")
        dist_ready = sem("dist_ready")
        conv1_product = sem("conv1_product")
        conv_raw_ready = sem("conv_raw_ready")
        conv_hi_ready = sem("conv_hi_ready")
        conv_lo_ready = sem("conv_lo_ready")
        msg_product = sem("msg_product")
        msg_added = sem("msg_added")
        msg_ready = sem("msg_ready")
        dist_product = sem("dist_product")
        kern_ready = sem("kern_ready")
        nmp_hi_ready = sem("nmp_hi_ready")
        nmp_ready = sem("nmp_ready")
        conv2_product = sem("conv2_product")
        conv2_shifted = sem("conv2_shifted")
        conv2_added = sem("conv2_added")
        x_conv_hi_ready = sem("x_conv_hi_ready")
        x_conv_ready = sem("x_conv_ready")
        gate_r_product = sem("gate_r_product")
        gate_z_product = sem("gate_z_product")
        gate_h_product = sem("gate_h_product")
        gate_n_product = sem("gate_n_product")
        r_tanh_ready = sem("r_tanh_ready")
        z_tanh_ready = sem("z_tanh_ready")
        gate_r_ready = sem("gate_r_ready")
        gate_h_added = sem("gate_h_added")
        gate_n_added = sem("gate_n_added")
        n_ready = sem("n_ready")
        diff_ready = sem("diff_ready")
        z_diff_ready = sem("z_diff_ready")
        gru_ready = sem("gru_ready")
        gru_turned = sem("gru_turned")
        out_ready = sem("out_ready")
        out_stored = sem("out_stored")

        ADJ_BANKS_0 = [o_ps[:, 1, :].bitcast(BF16), o_ps[:, 2, :].bitcast(BF16)]
        ADJ_BANKS = [slot_b[:, 0:HALF].bitcast(BF16), slot_b[:, HALF:N].bitcast(BF16)]
        ADJ_TAPS = (6, 9, 12, 15)

        def blocks(dram, b):
            return dram[b].rearrange("(t p) d -> p t d", p=P)

        def block(buf, t):
            return buf[:, t * P:(t + 1) * P]

        def half(buf, i):
            return buf[:, i * HALF:(i + 1) * HALF]

        def block_range(part):
            return range(T) if part is None else range(part * T // 2, (part + 1) * T // 2)

        def block_span(part):
            return slice(block_range(part)[0], block_range(part)[-1] + 1)

        def columns(buf, part):
            return buf[:, :] if part is None else half(buf, part)

        def count(b, part):
            return b + 1 + (part or 0)

        def frames(eng, frame):
            frame(0, 0, False, True)
            frame(1, 1, True, True)
            with eng.Fori(0, (B - 4) // 2) as pair:
                b = pair * 2 + 2
                frame(b, 0, True, True)
                frame(b + 1, 1, True, True)
            frame(LAST - 1, 0, True, True)
            frame(LAST, 1, True, False)

        def steps(b, prev, next_):
            for h in range(H):
                following = (b, h + 1) if h + 1 < H else (b + 1, 0)
                yield h, (following if h + 1 < H or next_ else None)

        TAP_JOBS = 3
        TAPS_PER_JOB = 8
        FIRST_COPIES, ALL_COPIES = 3, 5
        N_LOADS, N_REST_LOADS, N_LATE_LOADS = 3, 4, 29

        N_CONSTS = 11

        blk = ctx.enter_context(nc.Block())

        @blk.sync
        def _(sp):
            def load(dst, src):
                sp.dma_start(dst, src).then_inc(w_loaded, 16)

            def load_late(dst, src):
                sp.dma_start(dst, src).then_inc(w_late_loaded, 16)

            def col(v):
                return v.rearrange("(p a) -> p a", a=1)

            def row(v, cols):
                return v.rearrange("(a n) -> a n", a=1).to_broadcast([P, cols])

            def load_rest(dst, src):
                sp.dma_start(dst, src).then_inc(w_rest_loaded, 16)

            sp.dma_start(fc_raw, fc_w).then_inc(fc_loaded, 16)
            load(qk_raw[:, 0:1], k_w)
            load(qk_raw[:, 1:2], q_w)
            sp.dma_start(x_in[0][:, :, :], blocks(x, 0)).then_inc(x_loaded, 16)
            with nc.allow_non_contiguous_dma(reason="bias vectors of a few hundred numbers, once"):
                load(fcb_raw, fc_b.rearrange("(h k) -> k h", k=D))
            load_rest(qk_b[:, 0:1], row(q_b, 1))
            load_rest(qk_b[:, 1:2], row(k_b, 1))
            load_rest(fp_raw, fp_w.rearrange("(h k) d -> k h d", k=D))
            load_rest(b_out[:, :], row(fp_b, D))

            def late_loads():
                load_late(ih_raw, w_ih.rearrange("(g p) i -> p g i", p=P))
                load_late(hh_raw, w_hh.rearrange("(g p) i -> p g i", p=P))
                load_late(msg_raw, w_msg)
                load_late(conv1_raw, conv1_w.rearrange("o i k -> o (i k)"))
                load_late(conv2_raw, conv2_w)
                load_late(se_raw[0:S, :], w_se)
                for i, vec in enumerate((bn1_g, bn1_b, bn1_m, bn1_v, bn2_g, bn2_b, bn2_m, bn2_v)):
                    load_late(bn[:, i // 4, i % 4:i % 4 + 1], col(vec))
                load_late(b_msg_row[:, :], row(b_msg, D))
                with nc.allow_non_contiguous_dma(reason="bias vectors of a few hundred numbers, once"):
                    load_late(b_gate_in[:, 0, :], b_ih.rearrange("(g p) -> p g", p=P))
                    load_late(b_gate_in[:, 1, :], b_hh.rearrange("(g p) -> p g", p=P))
                    sp.wait_ge(consts_ready, 6)
                    for side, groups in enumerate(((ROWS_PROD, ROWS_SQ_M), (ROWS_PROD, ROWS_SQ_N))):
                        for row0, copies in groups:
                            for c in range(copies):
                                load_late(b_dist[row0 + c * S:row0 + (c + 1) * S, side:side + 1], col(b_se))

            sp.wait_ge(r_loaded[1], 16)
            late_loads()

            def frame(b, parity, prev, next_):
                if next_:
                    nb, other = b + 1, 1 - parity
                    wait(sp, x1_ready, b)
                    sp.dma_start(x_in[other][:, :, :], blocks(x, nb)).then_inc(x_loaded, 16)
                if prev:
                    sp.wait_ge(out_ready, b)
                    sp.dma_start(blocks(out, b - 1), out_sb[:, :, :]).then_inc(out_stored, 16)

            frames(sp, frame)
            for part in range(2):
                span = block_span(part)
                sp.wait_ge(out_ready, count(LAST, part))
                sp.dma_start(blocks(out, LAST)[:, span, :], out_sb[:, span, :]).then_inc(out_stored, 16)
            sp.wait_ge(out_stored, 16 * (B + 1))

        @blk.gpsimd
        def _(pool):
            def load_adj(b, i):
                rows = adj[b].rearrange("(s t p) m -> s p t m", p=P, s=2)
                wait(pool, adj_turned, T * b + T // 2 * i)
                pool.dma_start(adj_rows[:, :, :], rows[i]).then_inc(adj_cast, 16)

            pool.memset(ident[:, :], 0.0).then_inc(consts_ready, 1)
            pool.memset(b_dist[:, :], 0.0).then_inc(consts_ready, 1)
            pool.memset(ones[:, :], 1.0).then_inc(consts_ready, 1)
            pool.memset(minus_half[:, :], -0.5).then_inc(consts_ready, 1)
            pool.memset(w_dist[:, :], 0.0).then_inc(consts_ready, 1)
            pool.memset(dist_scale[:, :], 0.0).then_inc(consts_ready, 1)
            pool.wait_ge(consts_ready, 6)
            pool.affine_select(out=ident[:, :], in_=ident[:, :], compare_op=ALU.not_equal, fill=1.0, base=0,
                               pattern=[[-1, P]], channel_multiplier=1).then_inc(consts_ready, 1)
            pool.wait_ge(consts_ready, 7)
            pool.memset(b_dist[32:32 + 2 * S, 0:1], -1.0).then_inc(consts_ready, 1)
            pool.wait_ge(consts_ready, 8)
            pool.memset(b_dist[64:64 + 2 * S, 1:2], -1.0).then_inc(consts_ready, 1)
            pool.wait_ge(consts_ready, 9)
            pool.memset(dist_scale[0:32, 0:1], 2.0).then_inc(consts_ready, 1)
            pool.wait_ge(consts_ready, 10)
            pool.memset(dist_scale[0:32, 1:2], 1.0).then_inc(consts_ready, 1)
            pool.wait_ge(consts_ready, N_CONSTS)
            load_adj(0, 0)

            def rstd_batch_norms():
                pool.wait_ge(bn_step, 1)
                pool.tensor_tensor(bn_tmp[:, :, 1], bn_tmp[:, :, 0], minus_half[:, 0:2], ALU.pow).then_inc(bn_step, 1)

            def rstd(layer, b, part=None):
                s, span = ln[layer], block_span(part)
                wait_apart(pool, s["s_mv"], count(b, part), passed["pool"])
                pool.tensor_scalar(s["var"][:, span], s["mv"][:, span, 1], EPS, None, ALU.add).then_inc(s["s_var"], 1)
                pool.wait_ge(s["s_var"], count(b, part))
                pool.tensor_tensor(s["rstd"][:, span], s["var"][:, span], minus_half[:, span],
                                   ALU.pow).then_inc(s["s_rstd"], 1)

            def start_y(b):
                pool.wait_ge(ln[0]["s_out"], b + 1)
                wait(pool, y_tanh_ready, b)
                pool.tensor_tensor(y[:, :, :], h0[:, :, :], b_out[:, None, :].to_broadcast([P, T, D]),
                                   ALU.add).then_inc(y_ready, 1)

            rstd(0, 0)
            load_adj(0, 1)
            pool.wait_ge(bias_ready, 2)

            def frame(b, parity, prev, next_):
                start_y(b)
                if next_:
                    load_adj(b + 1, 0)
                if not prev:
                    rstd_batch_norms()
                if prev:
                    rstd(1, b - 1)
                if next_:
                    rstd(0, b + 1)
                    load_adj(b + 1, 1)

            frames(pool, frame)
            rstd(1, LAST, 0)
            rstd(1, LAST, 1)

        @blk.tensor
        def _(pe):
            pe.wait_ge(consts_ready, N_CONSTS)
            pe.wait_ge(fc_loaded, 16)
            for h in range(H):
                last = pe.transpose(block(slot_a, h), block(fc_raw, h), ident[:, :])
            last.then_inc(setup_filled, 1)
            pe.wait_ge(setup_copied, 1)
            pe.wait_ge(w_loaded, 16 * N_LOADS)
            pe.wait_ge(w_reps_ready, 3)
            kq_cols = bias_ps[:, 0:2 * H].rearrange("p (i h) -> p h i", i=2)
            for h in range(H):
                pe.matmul(kq_cols[:, h, :], fc_t[:, h, :], qk_raw, start=True, stop=True)
            pe.matmul(bias_ps[:, 2 * H:3 * H], k_rep, fcb_raw, start=True, stop=True)
            last = pe.matmul(bias_ps[:, 3 * H:4 * H], q_rep, fcb_raw, start=True, stop=True)
            last.then_inc(setup_filled, 1)

            def turn_late_weights(h):
                if h == 1:
                    pe.wait_ge(w_late_loaded, 16 * N_LATE_LOADS)
                    for g in range(3):
                        for i in range(2):
                            pe.transpose(block(slot_a, 3 * i + g), block(ih_raw[:, g, :], i), ident[:, :])
                    pe.transpose(block(slot_a, 6), msg_raw, ident[:, :])
                    last = pe.transpose(block(slot_a, 7), conv1_raw, ident[:, :])
                elif h == 2:
                    pe.wait_ge(w_ih_split, 1)
                    for g in range(3):
                        pe.transpose(block(slot_a, g), hh_raw[:, g, :], ident[:, :])
                    last = pe.transpose(slot_a[:, 3 * P:3 * P + S], se_raw[0:S, :], ident[0:S, 0:S])
                else:
                    j = h - 3
                    if j == 0:
                        pe.wait_ge(setup_copied, FIRST_COPIES + 2)
                    else:
                        pe.wait_ge(taps_split, j)
                    for k in range(TAPS_PER_JOB * j, min(TAPS_PER_JOB * (j + 1), TAPS)):
                        last = pe.transpose(block(slot_a, k - TAPS_PER_JOB * j), conv2_raw[:, :, k], ident[:, :])
                last.then_inc(setup_filled, 1)

            def turn_h0(b, after):
                pe.wait_ge(ln[0]["s_out"], b + 1)
                wait(pe, *after)
                for t in range(T):
                    last = pe.transpose(block(slot_b, t), h0[:, t, :], ident[:, :])
                last.then_inc(h0_turned, 1)

            def turn_adj(b, k, bank, after=()):
                pe.wait_ge(adj_cast, 32 * b + 16 * (k // (T // 2) + 1))
                for a in after:
                    wait(pe, *a)
                if k >= 2:
                    pe.wait_ge(adj_t_ready, T * b + k - 1)
                for m in range(T):
                    last = pe.transpose(block(bank, m), block(adj_rows[:, k % (T // 2), :], m), ident_16[:, :])
                last.then_inc(adj_turned, 1)

            def key_scores(b, parity):
                pe.wait_ge(h0_t_ready, b + 1)
                wait(pe, r_turned_read, b)
                for t in range(T):
                    last = pe.matmul(kq_ps[:, t, :], block(h0_t[parity], t), w_kq[:, :], start=True, stop=True)
                last.then_inc(k_scored, 1)

            def turn_key_max(b):
                pe.wait_ge(k_part_ready, b + 1)
                pe.transpose(kt_ps, k_part[:, :], ident[:, :]).then_inc(k_part_turned, 1)

            def spread_key_max(b):
                pe.wait_ge(k_diag_ready, b + 1)
                pe.matmul(km_ps, ones[0:H, :], k_diag[:, :], start=True, stop=True).then_inc(k_max_spread, 1)

            def turn_r(b):
                pe.wait_ge(r_col_ready, b + 1)
                pe.matmul(rt_ps, r_col[:, :, :].rearrange("p h t -> p (h t)"), ident[:, :], start=True,
                          stop=True).then_inc(r_turned, 1)

            def head_values(b, parity, h, after):
                wait(pe, values_ready, H * b + h)
                for a in after:
                    wait(pe, *a)
                for t in range(T):
                    last = pe.matmul(block(slot_b, t), block(h0_t[parity], t), w_val[:, h, :], start=True, stop=True)
                last.then_inc(z_ready, 1)

            def attend(b, h, side):
                pos, head = tile_pos(b, h), H * b + h
                pe.wait_ge(values_ready, head + 1)
                for t in range(T):
                    for work in side.get(t, ()):
                        work()
                    pe.wait_ge(tile_filled, pos + t + 1)
                    scores = ring[:, head_slot(b, h, t), :]
                    for bank, (first, end) in enumerate(BANKS):
                        if t == 0:
                            wait(pe, head_added, len(BANKS) * (head - 1) + bank + 1)
                        for n in range(first, end):
                            last = pe.matmul(o_block(n), block(scores, n), values[h % 2][:, t, :],
                                             start=(t == 0 and n == first), stop=(t == T - 1),
                                             skip_group_check=True)
                        if t == T - 1 and bank < 2:
                            last.then_inc(bank_done, 1)
                    last.then_inc(tile_used, 1)

            def turn_h1(b, after, part=None):
                pe.wait_ge(ln[1]["s_out"], count(b, part))
                wait(pe, *after)
                for t in block_range(part):
                    last = pe.transpose(block(slot_a, t), h1[:, t, :], ident[:, :])
                last.then_inc(h1_turned, 1)

            def kernel_features(b, slot, after):
                pe.wait_ge(h1_t_ready, b + 1)
                wait(pe, *after)
                for i in range(2):
                    last = pe.matmul(half(slot, i)[0:96, :], w_dist[:, :], half(h1_t, i), start=True, stop=True)
                last.then_inc(s_product, 1)

            def conv1(b, after, by_halves=False):
                pe.wait_ge(h1_t_ready, b + 1)
                wait(pe, *after)
                for i in range(2):
                    if by_halves and i == 1:
                        pe.wait_ge(h1_t_ready, count(b, 1))
                    last = pe.matmul(half(slot_b, i), conv1_t[:, :], half(h1_t, i), start=True, stop=True)
                last.then_inc(conv1_product, 1)

            def messages(b, after):
                wait(pe, *after)
                for t in range(T):
                    last = pe.matmul(block(slot_a, t), block(h1_t, t), w_msg_t[:, :], start=True, stop=True)
                last.then_inc(msg_product, 1)

            def distances(b, m, slot, after):
                wait(pe, *after)
                if m == 0:
                    pe.wait_ge(dist_ready, b + 1)
                for i in range(2):
                    last = pe.matmul(half(slot, i), block(dist_l, m)[0:DIST_ROWS, :], half(dist_r, i)[0:DIST_ROWS, :],
                                     start=True, stop=True)
                last.then_inc(dist_product, 1)

            def pass_messages(b, m, after):
                if m == 0:
                    wait(pe, *after)
                pe.wait_ge(tile_filled, kernel_tile_pos(b, m) + 1)
                if m == 0:
                    pe.wait_ge(msg_ready, b + 1)
                tile = ring[:, kernel_slot(b, m), :]
                for i in range(2):
                    last = pe.matmul(half(slot_a, i), msg[:, m, :], half(tile, i), start=(m == 0), stop=(m == T - 1),
                                     skip_group_check=True)
                last.then_inc(tile_used, 1)

            def convolve(b, i, after, bank, side={}):
                if after:
                    wait(pe, *after)
                if i == 0:
                    pe.wait_ge(conv_lo_ready, b + 1)
                for k in range(TAPS):
                    for work in side.get(k, ()):
                        work()
                    at = slice(i * HALF + k, i * HALF + k + HALF)
                    for n, (w, v) in enumerate(((conv2_hi, conv_hi), (conv2_hi, conv_lo), (conv2_lo, conv_hi))):
                        last = pe.matmul(bank, w[:, k, :], v[:, at], start=(k == 0 and n == 0),
                                         stop=(k == TAPS - 1 and n == 2))
                last.then_inc(conv2_product, 1)

            def gate(slot, terms, done, nmp=None, by_halves=False):
                for i in range(2):
                    for n, (w, v) in enumerate(terms):
                        if nmp and i == 0 and n == len(terms) - 3:
                            pe.wait_ge(*nmp)
                        last = pe.matmul(half(slot, i), w, half(v, i), start=(n == 0), stop=(n == len(terms) - 1))
                    if by_halves or i == 1:
                        last.then_inc(done, 1)

            def from_in(g):
                terms = []
                for i, (hi, lo) in enumerate(((x_conv_hi, x_conv_lo), (nmp_hi, nmp_lo))):
                    w_hi, w_lo = w_ih_hi[:, i, g * D:(g + 1) * D], w_ih_lo[:, i, g * D:(g + 1) * D]
                    terms += [(w_hi, hi), (w_hi, lo), (w_lo, hi)]
                return terms

            def from_hidden(g):
                return [(w_hh_t[:, g * D:(g + 1) * D], h1_t)]

            def gate_r(b, after, slot=slot_a):
                wait(pe, *after)
                pe.wait_ge(x_conv_ready, 2 * b + 2)
                gate(slot, from_hidden(0) + from_in(0), gate_r_product, (nmp_ready, b + 1))

            def gate_h(after):
                wait(pe, *after)
                gate(slot_b, from_hidden(2), gate_h_product)

            def gate_z(after):
                wait(pe, *after)
                gate(slot_a, from_hidden(1) + from_in(1), gate_z_product)

            def gate_n(after, slot=slot_a, by_halves=False):
                wait(pe, *after)
                gate(slot, from_in(2), gate_n_product, by_halves=by_halves)

            def turn_out(b, after, part=None):
                pe.wait_ge(gru_ready, count(b, part))
                wait(pe, *after)
                for t in block_range(part):
                    last = pe.transpose(block(slot_a, t), block(z_gate, t), ident[:, :])
                last.then_inc(gru_turned, 1)

            pe.wait_ge(ident_16_ready, 1)
            for k in range(T // 2):
                turn_adj(0, k, ADJ_BANKS_0[k % 2])
            turn_h0(0, (setup_copied, 1))
            pe.wait_ge(w_rest_loaded, 16 * N_REST_LOADS)
            for h in range(H):
                last = pe.matmul(block(slot_a, h), fc_t[:, h, :], fp_raw[:, h, :], start=True, stop=True)
            last.then_inc(setup_filled, 1)
            pe.wait_ge(setup_copied, 2)
            pe.wait_ge(bias_ready, 1)
            key_scores(0, 0)
            pe.wait_ge(setup_copied, FIRST_COPIES)
            head_values(0, 0, 0, ((h0_t_ready, 1),))
            turn_key_max(0)
            spread_key_max(0)
            turn_r(0)
            for h in range(H):
                last = pe.matmul(bout_ps, fcb_rep[:, h, :], fp_raw[:, h, :], start=(h == 0), stop=(h == H - 1))
            last.then_inc(setup_filled, 1)
            for k in range(T // 2, T):
                turn_adj(0, k, ADJ_BANKS_0[k % 2])
            pe.wait_ge(bias_ready, 2)
            pe.wait_ge(adj_t_ready, T)

            def frame(b, parity, prev, next_):
                L = b - 1
                if isinstance(b, int) and b == 1:
                    pe.wait_ge(setup_copied, ALL_COPIES)
                    pe.wait_ge(taps_split, TAP_JOBS)
                for h, following in steps(b, prev, next_):
                    scaled = (values_ready, H * b + h + 2)
                    side = {t: [] for t in range(T)}
                    if prev:
                        if h == 2:
                            side[3] = [lambda: turn_h1(L, (out_ready, b - 1))]
                            side[5] = [lambda: kernel_features(L, slot_a, (h1_t_ready, b))]
                            side[7] = [lambda: conv1(L, scaled)]
                        elif h in (3, 4):
                            for m in range(AM_SPLIT):
                                k = m + AM_SPLIT * (h - 3)
                                after = (kern_ready, T * L + k)
                                if m == 0:
                                    after = (msg_added, b) if h == 3 else (conv2_shifted, 2 * L + 1)
                                t = (2, 4, 5, 7)[m] if h == 3 else (1, 3, 5, 7)[m]
                                side[t] = [lambda k=k, after=after: distances(L, k, slot_a, after)]
                        elif h == 6:
                            side[2] = [lambda: gate_r(L, (conv2_shifted, 2 * L + 2))]
                            side[3] = [lambda: gate_h(scaled)]
                            side[5] = [lambda: gate_z((r_tanh_ready, b))]
                    if next_:
                        if h == 4:
                            side[3].append(lambda: turn_h0(b + 1, scaled))
                            side[6].append(lambda: key_scores(b + 1, 1 - parity))
                        elif h == 6 and not prev:
                            for k in range(T // 2, T):
                                side[k - 2].append(lambda k=k: turn_adj(b + 1, k, ADJ_BANKS[k % 2],
                                                                        [scaled] if k == T // 2 else []))
                        elif h == 5:
                            if not prev:
                                side[1].append(lambda: turn_key_max(b + 1))
                            side[2 if prev else 3].append(lambda: spread_key_max(b + 1))
                            for k in range(T // 2):
                                side[k + (2 if prev else 4)].append(lambda k=k: turn_adj(b + 1, k, ADJ_BANKS[k % 2],
                                                                        [scaled] if k == 0 else []))
                    if following:
                        fb, fh = following
                        after_b = []
                        if prev and h == 3:
                            after_b = [(conv_hi_ready, b)]
                        elif prev and h == 7:
                            after_b = [(gate_h_added, b)]
                        elif h == 7 and next_:
                            after_b = [(adj_t_ready, T * (b + 2))]
                        elif next_ and h == 5:
                            after_b = [(h0_t_ready, b + 2)]
                        elif next_ and h == 6 and prev:
                            after_b = [(adj_t_ready, T * (b + 2))]
                        elif next_ and h == 6:
                            after_b = [(adj_t_ready, T * (b + 1) + T // 2)]
                        head_values(fb, parity if fh else 1 - parity, fh, after_b)
                    attend(b, h, side)
                    if prev:
                        if h == 2:
                            messages(L, (s_read, b))
                        elif h == 3:
                            convolve(L, 0, (kern_ready, T * L + AM_SPLIT), half(slot_a, 0))
                        elif h == 4:
                            for m in range(T):
                                pass_messages(L, m, (kern_ready, T * b))
                                if next_ and m == T - 3:
                                    turn_key_max(b + 1)
                        elif h == 5:
                            side = {}
                            if next_:
                                for k in range(T // 2, T):
                                    side[ADJ_TAPS[k - T // 2]] = [lambda k=k: turn_adj(b + 1, k, ADJ_BANKS[k % 2])]
                            convolve(L, 1, (nmp_ready, b), half(slot_a, 1), side)
                        elif h == 6:
                            gate_n((z_tanh_ready, b))
                        elif h == 7:
                            turn_out(L, (gate_n_added, b))
                    else:
                        if 1 <= h <= 2 + TAP_JOBS:
                            turn_late_weights(h)
                    if next_ and h == 5:
                        turn_r(b + 1)

            frames(pe, frame)
            L = LAST
            for part in range(2):
                turn_h1(L, (out_ready, L), part)
            conv1(L, (gate_h_added, L), by_halves=True)
            kernel_features(L, slot_o, (head_added, len(BANKS) * H * B))
            messages(L, (h1_t_ready, count(L, 1)))
            convolve(L, 0, (), o_ps[:, 2, :])
            side = {}
            for m in range(T):
                after = (kern_ready, T * L + m) if m else (conv_hi_ready, B)
                side[2 * m] = [lambda m=m, after=after: distances(L, m, slot_b, after)]
            convolve(L, 1, (s_read, B), o_ps[:, 0, :], side)
            for m in range(T):
                pass_messages(L, m, (msg_added, B))
            gate_h((kern_ready, T * B))
            gate_r(L, (conv2_shifted, 2 * L + 2), slot_o)
            gate_z((nmp_ready, B))
            gate_n((r_tanh_ready, B), slot_o, by_halves=True)
            for part in range(2):
                turn_out(L, (z_tanh_ready, B), part)

        @blk.scalar
        def _(act):
            def copy(dst, src):
                return act.activation(dst, src, ACT.Copy)

            act.wait_ge(setup_filled, 1)
            copy(fc_t.rearrange("p h i -> p (h i)"), slot_a[:, :]).then_inc(setup_copied, 1)
            act.wait_ge(setup_filled, 2)
            copy(w_kq[:, :], bias_ps[:, 0:2 * H]).then_inc(setup_copied, 1)

            def copy_late_weights(h):
                act.wait_ge(setup_filled, 3 + h)
                if h == 2:
                    copy(w_ih_hi[:, :, :].rearrange("p i n -> p (i n)"), slot_a[:, 0:6 * P])
                    copy(w_msg_t[:, :], block(slot_a, 6))
                    last = copy(conv1_t[:, :], block(slot_a, 7))
                else:
                    act.wait_ge(consts_ready, N_CONSTS)
                    copy(w_hh_t[:, :], slot_a[:, 0:3 * P])
                    for row, copies in (ROWS_PROD, ROWS_SQ_N, ROWS_SQ_M):
                        for c in range(copies):
                            last = copy(w_dist[:, row + c * S:row + (c + 1) * S], slot_a[:, 3 * P:3 * P + S])
                last.then_inc(setup_copied, 1)

            def copy_h0_t(b, parity):
                act.wait_ge(h0_turned, b + 1)
                copy(h0_t[parity][:, :], slot_b[:, :]).then_inc(h0_t_ready, 1)

            def key_weights(b, parity):
                act.wait_ge(kq_shifted, b + 1)
                act.activation(p_col[parity][:, :, :], k_low[:, :, :], ACT.Exp, scale=HALF_SPAN)\
                   .then_inc(p_half_ready, 1)
                act.activation(v_col[parity][:, :, :], k_low[:, :, :], ACT.Exp, scale=SLOPE)
                act.wait_ge(p_half_ready, b + 1)
                act.activation(p_col[parity][:, :, :], p_col[parity][:, :, :], ACT.Square, scale=HALF_C)\
                   .then_inc(pv_ready, 1)

            def query_weights(b):
                act.activation(q_high[:, :, :], q_high[:, :, :], ACT.Exp, scale=-HALF_SPAN).then_inc(r_half_ready, 1)
                act.wait_ge(r_half_ready, b + 1)
                wait(act, r_turned, b)
                act.activation(r_col[:, :, :], q_high[:, :, :], ACT.Square, scale=HALF_C).then_inc(r_col_ready, 1)

            def copy_r(b):
                act.wait_ge(r_turned, b + 1)
                wait(act, r_stored, 16 * b)
                copy(r_turned_sb, rt_ps).then_inc(r_turned_read, 1)

            def store_r(b):
                act.wait_ge(r_turned_read, b + 1)
                for i in range(R_ROWS):
                    wait(act, r_loaded[i], 16 * (H // R_ROWS) * b)
                act.dma_start(r_dram.rearrange("h (t n) -> (h t) n", t=T), r_turned_sb).then_inc(r_stored, 16)

            def spread_r(b, h):
                if h == 0:
                    act.wait_ge(r_stored, 16 * (b + 1))
                if h >= R_ROWS:
                    act.wait_ge(tile_filled, tile_pos(b, h - R_ROWS) + T)
                elif not (isinstance(b, int) and b == 0):
                    act.wait_ge(tile_filled, tile_pos(b - 1, h + H - R_ROWS) + T)
                act.dma_start(r_row[h % R_ROWS][:, :], r_dram[h:h + 1, :].to_broadcast([P, N]))\
                    .then_inc(r_loaded[h % R_ROWS], 16)

            def copy_adj(b, parity, k, bank):
                act.wait_ge(adj_turned, T * b + k + 1)
                if k == 0 and not (isinstance(b, int) and b < 2):
                    act.wait_ge(tile_filled, kernel_tile_pos(b - 2, T - 1) + 1)
                copy(adj_t[parity][:, :, k * P:(k + 1) * P], bank.rearrange("p (m n) -> p m n", m=T))\
                    .then_inc(adj_t_ready, 1)

            def scale_values(b, parity, h):
                act.wait_ge(z_ready, H * b + h + 1)
                if h == 0:
                    act.wait_ge(pv_ready, b + 1)
                copy(values[h % 2][:, :, D:W], v_col[parity][:, :, h:h + 1])
                for t in range(T):
                    last = act.activation(values[h % 2][:, t, 0:D], block(slot_b, t), ACT.Copy,
                                          scale=v_col[parity][:, t, h:h + 1])
                last.then_inc(values_ready, 1)

            def tanh_y(b, part=None):
                act.wait_ge(head_added, len(BANKS) * (H * b + H) - (1 if part == 0 else 0))
                wait(act, gru_ready, b)
                span = block_span(part)
                act.activation(y_tanh[:, span, :], y[:, span, :], ACT.Tanh, scale=0.5).then_inc(y_tanh_ready, 1)

            def copy_h1_t(b, part=None):
                act.wait_ge(h1_turned, count(b, part))
                wait(act, gru_ready, b)
                copy(columns(h1_t, part), columns(slot_a, part)).then_inc(h1_t_ready, 1)

            def dist_features(b, slot):
                act.wait_ge(s_product, b + 1)
                if not (isinstance(b, int) and b == 0):
                    act.wait_ge(tile_filled, kernel_tile_pos(b - 1, T - KERNS + 1) + 1)
                for side, rows, func in ((0, (0, 64), ACT.Identity), (0, (64, DIST_ROWS), ACT.Square),
                                         (1, (0, 32), ACT.Identity), (1, (32, 64), ACT.Square),
                                         (1, (64, DIST_ROWS), ACT.Identity)):
                    r0, r1 = rows
                    scale = dist_scale[r0:r1, side:side + 1] if func == ACT.Identity else 1.0
                    last = act.activation(kern[side][r0:r1, :], slot[r0:r1, :], func,
                                          bias=b_dist[r0:r1, side:side + 1], scale=scale)
                last.then_inc(s_read, 1)

            def conv_input(b):
                act.wait_ge(conv1_product, b + 1)
                if not (isinstance(b, int) and b == 0):
                    act.wait_ge(tile_filled, kernel_tile_pos(b - 1, T - KERNS + 2) + 1)
                act.activation(kern[2][:, :], slot_b[:, :], ACT.Relu, bias=bn_aff[:, 0, 1:2],
                               scale=bn_aff[:, 0, 0:1]).then_inc(conv_raw_ready, 1)
                wait(act, conv2_product, 2 * b)
                act.activation(conv_hi[:, PAD:PAD + N], slot_b[:, :], ACT.Relu, bias=bn_aff[:, 0, 1:2],
                               scale=bn_aff[:, 0, 0:1]).then_inc(conv_hi_ready, 1)

            def dist_hi_parts(b):
                act.wait_ge(s_read, b + 1)
                wait(act, gate_n_product, b)
                copy(dist_l[0:DIST_ROWS, :], kern[0][0:DIST_ROWS, :])
                copy(dist_r[0:DIST_ROWS, :], kern[1][0:DIST_ROWS, :]).then_inc(s_hi_ready, 1)

            def kernel_block(b, m, slot):
                act.wait_ge(dist_product, T * b + m + 1)
                if m == 2:
                    act.wait_ge(conv_lo_ready, b + 1)
                if m == KERNS - 1:
                    wait(act, gru_turned, b)
                if m >= KERNS:
                    act.wait_ge(tile_filled, kernel_tile_pos(b, m - KERNS) + 1)
                elif not (isinstance(b, int) and b == 0):
                    act.wait_ge(tile_filled, kernel_tile_pos(b - 1, T - KERNS + m) + 1)
                act.activation(kern[m % KERNS][:, :], slot[:, :], ACT.Exp).then_inc(kern_ready, 1)

            def copy_nmp(b, last_batch=False):
                act.wait_ge(tile_used, kernel_tile_pos(b, T - 1) + 1 if last_batch else used(b + 1, KERNEL_AT[-1]))
                copy(nmp_hi[:, :], slot_a[:, :]).then_inc(nmp_hi_ready, 1)

            def conv_shift(b, i, acc):
                act.wait_ge(conv2_product, 2 * b + i + 1)
                act.activation(half(x_conv, i), acc, ACT.Identity, bias=bn_aff[:, 1, 1:2],
                               scale=bn_aff[:, 1, 0:1]).then_inc(conv2_shifted, 1)

            def conv_hi_part(b, i):
                act.wait_ge(conv2_added, 2 * b + i + 1)
                wait(act, gate_n_product, b)
                act.activation(half(x_conv_hi, i), half(x_conv, i), ACT.Relu).then_inc(x_conv_hi_ready, 1)

            def gate_tanhs(b, slot=slot_a):
                act.wait_ge(gate_r_product, b + 1)
                act.activation(gate_a[:, :], slot[:, :], ACT.Tanh, bias=b_gate[:, 0:1], scale=0.5)\
                   .then_inc(r_tanh_ready, 1)
                act.wait_ge(r_tanh_ready, b + 1)
                act.activation(gate_a[:, :], gate_a[:, :], ACT.Copy, scale=0.5, bias=0.5).then_inc(gate_r_ready, 1)
                act.wait_ge(gate_z_product, b + 1)
                wait(act, gru_turned, b)
                act.activation(z_gate[:, :], slot_a[:, :], ACT.Tanh, bias=b_gate[:, 1:2], scale=0.5)\
                   .then_inc(z_tanh_ready, 1)

            def new_state(b, part=None):
                act.wait_ge(gate_n_added, count(b, part))
                act.activation(columns(gate_a, part), columns(gate_a, part), ACT.Tanh,
                               bias=b_gate_in[:, 0, 2:3]).then_inc(n_ready, 1)

            for k in range(T // 2):
                copy_adj(0, 0, k, ADJ_BANKS_0[k % 2])
            copy_h0_t(0, 0)
            act.wait_ge(setup_filled, 3)
            copy(w_val[:, :, :].rearrange("p h d -> p (h d)"), slot_a[:, :]).then_inc(setup_copied, 1)
            key_weights(0, 0)
            query_weights(0)
            copy_r(0)
            store_r(0)
            for k in range(T // 2, T):
                if k == T - 2:
                    for h in range(R_ROWS):
                        spread_r(0, h)
                copy_adj(0, 0, k, ADJ_BANKS_0[k % 2])
            scale_values(0, 0, 0)

            def frame(b, parity, prev, next_):
                L = b - 1
                if isinstance(b, int) and b == 1:
                    act.wait_ge(bias_late_ready, 3)
                for h, following in steps(b, prev, next_):
                    if prev:
                        if h == 0:
                            tanh_y(L)
                        elif h == 4:
                            conv_hi_part(L, 0)
                        elif h == 7:
                            new_state(L)
                    if following and following[1] in SCALED_BY_ACT:
                        fb, fh = following
                        scale_values(fb, parity if fh else 1 - parity, fh)
                    if next_ and h == 5:
                        for k in range(T // 2):
                            copy_adj(b + 1, 1 - parity, k, ADJ_BANKS[k % 2])
                    if h + R_ROWS < H:
                        spread_r(b, h + R_ROWS)
                    elif next_:
                        spread_r(b + 1, h + R_ROWS - H)
                    if not prev and h in (2, 3):
                        copy_late_weights(h)
                    if next_ and h == 5:
                        key_weights(b + 1, 1 - parity)
                        query_weights(b + 1)
                    if next_ and h == (5 if prev else 6):
                        for k in range(T // 2, T):
                            copy_adj(b + 1, 1 - parity, k, ADJ_BANKS[k % 2])
                    if next_ and h == 5:
                        copy_r(b + 1)
                        store_r(b + 1)
                    if prev:
                        if h == 2:
                            copy_h1_t(L)
                            dist_features(L, slot_a)
                            conv_input(L)
                            dist_hi_parts(L)
                        elif h == 3:
                            kernel_block(L, 0, slot_a)
                            kernel_block(L, 1, slot_a)
                            kernel_block(L, 2, slot_a)
                            kernel_block(L, 3, slot_a)
                            conv_shift(L, 0, half(slot_a, 0))
                        elif h == 4:
                            kernel_block(L, AM_SPLIT, slot_a)
                    if next_ and h == 4:
                        copy_h0_t(b + 1, 1 - parity)
                    if prev:
                        if h == 4:
                            for m in range(AM_SPLIT + 1, T):
                                kernel_block(L, m, slot_a)
                            copy_nmp(L)
                        elif h == 5:
                            conv_shift(L, 1, half(slot_a, 1))
                            conv_hi_part(L, 1)
                        elif h == 6:
                            gate_tanhs(L)

            frames(act, frame)
            L = LAST
            for part in range(2):
                tanh_y(L, part)
            for part in range(2):
                copy_h1_t(L, part)
            conv_input(L)
            dist_features(L, slot_o)
            dist_hi_parts(L)
            conv_shift(L, 0, o_ps[:, 2, :])
            conv_hi_part(L, 0)
            for m in range(T):
                kernel_block(L, m, slot_b)
            conv_shift(L, 1, o_ps[:, 0, :])
            conv_hi_part(L, 1)
            copy_nmp(L, True)
            gate_tanhs(L, slot_o)
            for part in range(2):
                new_state(L, part)

        @blk.vector
        def _(dve):
            dve.wait_ge(consts_ready, N_CONSTS)
            def moments(layer, b, src, part=None):
                s = ln[layer]
                for t in block_range(part):
                    last = dve.bn_stats(s["stats"][:, t, :], src[:, t, :])
                last.then_inc(s["s_stats"], 1)
                wait_apart(dve, s["s_stats"], count(b, part), passed["vector"])
                for t in block_range(part):
                    last = dve.bn_aggr(s["mv"][:, t, :], s["stats"][:, t, :])
                last.then_inc(s["s_mv"], 1)

            def normalise(layer, b, src, dst, part=None):
                s, span = ln[layer], block_span(part)
                dve.wait_ge(s["s_rstd"], count(b, part))
                for t in block_range(part):
                    last = dve.tensor_scalar(dst[:, t, :], src[:, t, :], s["mv"][:, t, 0:1], s["rstd"][:, t:t + 1],
                                             ALU.subtract, ALU.mult)
                last.then_inc(s["s_mid"], 1)
                dve.wait_ge(s["s_mid"], count(b, part))
                dve.tensor_scalar(dst[:, span, :], dst[:, span, :], 0.0, None, ALU.max).then_inc(s["s_out"], 1)

            def first_norm(b, parity):
                dve.wait_ge(x_loaded, 16 * (b + 1))
                wait(dve, y_ready, b)
                moments(0, b, x_in[parity])
                normalise(0, b, x_in[parity], h0)

            def keys(b):
                dve.wait_ge(k_scored, b + 1)
                wait(dve, pv_ready, b)
                dve.tensor_tensor(kq_sb[:, :, :], kq_ps, b_kq[:, None, :].to_broadcast([P, T, 2 * H]), ALU.add)\
                   .then_inc(k_ready, 1)
                dve.wait_ge(k_ready, b + 1)
                dve.tensor_reduce(k_part[:, :], kq_sb[:, :, 0:H].rearrange("p t h -> p h t"), AX.X, ALU.max)\
                   .then_inc(k_part_ready, 1)

            def key_max(b):
                dve.wait_ge(k_part_turned, b + 1)
                dve.tensor_reduce(k_max[:, :], kt_ps, AX.X, ALU.max).then_inc(k_max_ready, 1)
                dve.wait_ge(k_max_ready, b + 1)
                dve.tensor_scalar(k_diag[:, :], ident[0:H, 0:H], k_max[:, 0:1], None, ALU.mult)\
                   .then_inc(k_diag_ready, 1)

            def key_shift(b):
                dve.wait_ge(k_max_spread, b + 1)
                dve.tensor_copy(k_shift[:, :], km_ps).then_inc(k_shift_ready, 1)
                dve.wait_ge(k_shift_ready, b + 1)
                wait(dve, r_turned, b)
                dve.tensor_tensor(q_high[:, :, :].rearrange("p h t -> p t h"), kq_sb[:, :, H:2 * H],
                                  k_shift[:, None, :].to_broadcast([P, T, H]), ALU.add).then_inc(q_shifted, 1)
                dve.tensor_tensor(k_low[:, :, :], kq_sb[:, :, 0:H], k_shift[:, None, :].to_broadcast([P, T, H]),
                                  ALU.subtract)
                dve.wait_ge(q_shifted, b + 1)
                dve.tensor_scalar(q_high[:, :, :], q_high[:, :, :], 0.0, None, ALU.max).then_inc(kq_shifted, 1)

            def scale_values(b, parity, h):
                dve.wait_ge(z_ready, H * b + h + 1)
                weights = v_col[parity][:, :, h:h + 1]
                dve.tensor_copy(values[h % 2][:, :, D:W], weights)
                dve.tensor_tensor(values[h % 2][:, :, 0:D], slot_b[:, :].rearrange("p (t d) -> p t d", t=T),
                                  weights.to_broadcast([P, T, D]), ALU.mult).then_inc(values_ready, 1)

            def score_tiles(b, parity, h):
                if h == 0:
                    dve.wait_ge(adj_t_ready, T * (b + 1))
                    dve.wait_ge(pv_ready, b + 1)
                dve.wait_ge(r_loaded[h % R_ROWS], 16 * (H // R_ROWS * b + h // R_ROWS + 1))
                for t in range(T):
                    if isinstance(b, int) and b == 0:
                        wait(dve, tile_used, T * h + t + 1 - RING)
                    else:
                        dve.wait_ge(tile_used, place_free(b, HEAD_AT[h] + t))
                    dve.scalar_tensor_tensor(out=ring[:, head_slot(b, h, t), :], in0=r_row[h % R_ROWS][:, :],
                                             scalar=p_col[parity][:, t, h:h + 1], in1=adj_t[parity][:, t, :],
                                             op0=ALU.max, op1=ALU.mult).then_inc(tile_filled, 1)

            def add_head(b, h):
                head = H * b + h
                for bank, (first, end) in enumerate(BANKS):
                    if bank < 2:
                        dve.wait_ge(bank_done, 2 * head + bank + 1)
                    else:
                        dve.wait_ge(tile_used, head_used(b, h, T - 1))
                    if bank == 0:
                        if h == 0:
                            dve.wait_ge(y_ready, b + 1)
                        else:
                            dve.wait_ge(head_added, len(BANKS) * head)
                    sums = o_ps[:, bank, 0:(end - first) * W].rearrange("p (n w) -> p n w", w=W)[:, :, D]
                    dve.reciprocal(rden[:, first:end], sums).then_inc(rden_ready, 1)
                    dve.wait_ge(rden_ready, len(BANKS) * head + bank + 1)
                    for n in range(first, end):
                        last = dve.scalar_tensor_tensor(out=y[:, n, :], in0=o_block(n)[:, 0:D],
                                                        scalar=rden[:, n:n + 1], in1=y[:, n, :], op0=ALU.mult,
                                                        op1=ALU.add)
                    last.then_inc(head_added, 1)

            def first_output(b, parity, part=None):
                span = block_span(part)
                dve.wait_ge(y_tanh_ready, count(b, part))
                wait(dve, out_ready, b)
                dve.scalar_tensor_tensor(out=x1[:, span, :], in0=y_tanh[:, span, :], scalar=0.5,
                                         in1=x_in[parity][:, span, :], op0=ALU.mult,
                                         op1=ALU.add).then_inc(x1_half_ready, 1)
                dve.wait_ge(x1_half_ready, count(b, part))
                dve.tensor_scalar(x1[:, span, :], x1[:, span, :], 0.5, None, ALU.add).then_inc(x1_ready, 1)
                dve.wait_ge(x1_ready, count(b, part))
                moments(1, b, x1, part)

            def split_features(b):
                dve.wait_ge(s_hi_ready, b + 1)
                for i, buf in enumerate((dist_l, dist_r)):
                    last = dve.scalar_tensor_tensor(out=buf[0:DIST_ROWS, :], in0=buf[0:DIST_ROWS, :].bitcast(F32),
                                                    scalar=minus_lo[0:DIST_ROWS, i:i + 1],
                                                    in1=kern[i][0:DIST_ROWS, :], op0=ALU.mult, op1=ALU.add)
                last.then_inc(dist_ready, 1)

            def split_conv_in(b):
                dve.wait_ge(conv_raw_ready, b + 1)
                dve.wait_ge(conv_hi_ready, b + 1)
                wait(dve, conv2_product, 2 * b)
                dve.tensor_tensor(conv_lo[:, PAD:PAD + N], kern[2][:, :], conv_hi[:, PAD:PAD + N].bitcast(F32),
                                  ALU.subtract).then_inc(conv_lo_ready, 1)

            def messages(b):
                dve.wait_ge(msg_product, b + 1)
                dve.tensor_tensor(msg[:, :, :], slot_a[:, :].rearrange("p (t d) -> p t d", t=T),
                                  b_msg_row[:, None, :].to_broadcast([P, T, D]), ALU.add).then_inc(msg_added, 1)
                dve.wait_ge(msg_added, b + 1)
                dve.tensor_scalar(msg[:, :, :], msg[:, :, :], 0.0, None, ALU.max).then_inc(msg_ready, 1)

            def kernel_tile(b, parity, m):
                dve.wait_ge(kern_ready, T * b + m + 1)
                if isinstance(b, int) and b == LAST:
                    dve.wait_ge(tile_used, kernel_tile_pos(b, m) + 1 - RING)
                else:
                    dve.wait_ge(tile_used, place_free(b + 1, KERNEL_AT[m]))
                dve.tensor_tensor(ring[:, kernel_slot(b, m), :], kern[m % KERNS][:, :], adj_t[parity][:, m, :],
                                  ALU.mult).then_inc(tile_filled, 1)

            def conv_add(b, i):
                dve.wait_ge(conv2_shifted, 2 * b + i + 1)
                dve.tensor_tensor(half(x_conv, i), half(x_conv, i), half(h1_t, i), ALU.add).then_inc(conv2_added, 1)

            def conv_lo_part(b, i):
                dve.wait_ge(x_conv_hi_ready, 2 * b + i + 1)
                dve.scalar_tensor_tensor(out=half(x_conv_lo, i), in0=half(x_conv, i), scalar=0.0,
                                         in1=half(x_conv_hi, i).bitcast(F32), op0=ALU.max,
                                         op1=ALU.subtract).then_inc(x_conv_ready, 1)

            def split_nmp(b):
                dve.wait_ge(nmp_hi_ready, b + 1)
                dve.tensor_tensor(nmp_lo[:, :], slot_a[:, :], nmp_hi[:, :].bitcast(F32),
                                  ALU.subtract).then_inc(nmp_ready, 1)

            def gate_hidden(b):
                dve.wait_ge(gate_r_ready, b + 1)
                dve.wait_ge(gate_h_product, b + 1)
                dve.scalar_tensor_tensor(out=gate_a[:, :], in0=slot_b[:, :], scalar=b_gate_in[:, 1, 2:3],
                                         in1=gate_a[:, :], op0=ALU.add, op1=ALU.mult).then_inc(gate_h_added, 1)

            def add_gate_n(b, slot=slot_a, part=None):
                dve.wait_ge(gate_h_added, b + 1)
                dve.wait_ge(gate_n_product, count(b, part))
                dve.tensor_tensor(columns(gate_a, part), columns(slot, part), columns(gate_a, part),
                                  ALU.add).then_inc(gate_n_added, 1)

            def gru(b, part=None):
                n, z, diff = columns(gate_a, part), columns(z_gate, part), columns(diff_t, part)
                dve.wait_ge(n_ready, count(b, part))
                dve.tensor_tensor(diff, columns(h1_t, part), n, ALU.subtract).then_inc(diff_ready, 1)
                dve.wait_ge(diff_ready, count(b, part))
                dve.scalar_tensor_tensor(out=z, in0=z, scalar=1.0, in1=diff, op0=ALU.add,
                                         op1=ALU.mult).then_inc(z_diff_ready, 1)
                dve.wait_ge(z_diff_ready, count(b, part))
                dve.scalar_tensor_tensor(out=z, in0=z, scalar=0.5, in1=n, op0=ALU.mult,
                                         op1=ALU.add).then_inc(gru_ready, 1)

            def add_out(b, part=None):
                span = block_span(part)
                dve.wait_ge(gru_turned, count(b, part))
                dve.tensor_tensor(out_sb[:, span, :], slot_a[:, :].rearrange("p (t d) -> p t d", t=T)[:, span, :],
                                  x1[:, span, :], ALU.add).then_inc(out_ready, 1)

            def late_biases():
                dve.wait_ge(w_late_loaded, 16 * N_LATE_LOADS)
                for part in (conv_hi, conv_lo):
                    for at in (0, PAD + N):
                        dve.tensor_scalar(part[:, at:at + PAD], ones[:, 0:PAD], 0.0, None, ALU.mult)
                dve.tensor_scalar(bn_tmp[:, :, 0], bn[:, :, 3], EPS, None, ALU.add).then_inc(bn_step, 1)
                dve.wait_ge(bn_step, 2)
                dve.tensor_tensor(bn_aff[:, :, 0], bn[:, :, 0], bn_tmp[:, :, 1], ALU.mult).then_inc(bn_step, 1)
                dve.wait_ge(bn_step, 3)
                dve.tensor_tensor(bn_tmp[:, :, 0], bn[:, :, 2], bn_aff[:, :, 0], ALU.mult).then_inc(bn_step, 1)
                dve.wait_ge(bn_step, 4)
                dve.tensor_tensor(bn_aff[:, :, 1], bn[:, :, 1], bn_tmp[:, :, 0], ALU.subtract)\
                   .then_inc(bias_late_ready, 1)
                dve.tensor_tensor(b_gate[:, :], b_gate_in[:, 0, 0:2], b_gate_in[:, 1, 0:2], ALU.add)\
                   .then_inc(bn_step, 1)
                dve.wait_ge(bn_step, 5)
                dve.tensor_scalar(b_gate[:, :], b_gate[:, :], 0.5, None, ALU.mult).then_inc(bias_late_ready, 1)
                dve.tensor_scalar(b_dist[0:32, 0:1], b_dist[0:32, 0:1], 2.0, None, ALU.mult)\
                   .then_inc(bias_late_ready, 1)
                for i, rows in enumerate(((S, 3 * S), (64 + S, 64 + 2 * S), (2 * S, 4 * S), (32 + S, 32 + 2 * S))):
                    last = dve.tensor_reduce(lo_rows[:, i:i + 1], ident[:, rows[0]:rows[1]], AX.X, ALU.add)
                last.then_inc(bn_step, 1)
                dve.wait_ge(bn_step, 6)
                for i in range(2):
                    last = dve.tensor_tensor(minus_lo[:, i:i + 1], lo_rows[:, 2 * i:2 * i + 1],
                                             lo_rows[:, 2 * i + 1:2 * i + 2], ALU.add)
                last.then_inc(bn_step, 1)
                dve.wait_ge(bn_step, 7)
                dve.tensor_scalar(minus_lo[:, :], minus_lo[:, :], -1.0, None, ALU.mult).then_inc(bn_step, 1)
                dve.wait_ge(bn_step, 8)

            def split_w_ih():
                dve.wait_ge(setup_copied, FIRST_COPIES + 1)
                dve.tensor_tensor(w_ih_lo[:, :, :].rearrange("p i n -> p (i n)"), slot_a[:, 0:6 * P],
                                  w_ih_hi[:, :, :].rearrange("p i n -> p (i n)").bitcast(F32),
                                  ALU.subtract).then_inc(w_ih_split, 1)

            def split_taps(j):
                k0, k1 = TAPS_PER_JOB * j, min(TAPS_PER_JOB * (j + 1), TAPS)
                taps = slot_a[:, 0:(k1 - k0) * P].rearrange("p (k o) -> p k o", k=k1 - k0)
                dve.wait_ge(setup_filled, FIRST_COPIES + 4 + j)
                dve.tensor_copy(conv2_hi[:, k0:k1, :], taps).then_inc(taps_hi_ready, 1)
                dve.wait_ge(taps_hi_ready, j + 1)
                dve.tensor_tensor(conv2_lo[:, k0:k1, :], taps, conv2_hi[:, k0:k1, :].bitcast(F32),
                                  ALU.subtract).then_inc(taps_split, 1)

            dve.tensor_copy(ident_16[:, :], ident[:, :]).then_inc(ident_16_ready, 1)
            dve.wait_ge(x_loaded, 16)
            moments(0, 0, x_in[0])
            dve.wait_ge(w_loaded, 16 * N_LOADS)
            dve.tensor_scalar(q_rep, ones[:, :], qk_raw[:, 1:2], None, ALU.mult).then_inc(w_reps_ready, 1)
            dve.tensor_scalar(k_rep, ones[:, :], qk_raw[:, 0:1], None, ALU.mult).then_inc(w_reps_ready, 1)
            for h in range(H):
                last = dve.tensor_scalar(fcb_rep[:, h, :], ones[:, :], fcb_raw[:, h:h + 1], None, ALU.mult)
            last.then_inc(w_reps_ready, 1)
            normalise(0, 0, x_in[0], h0)
            dve.wait_ge(setup_copied, 2)
            dve.wait_ge(w_rest_loaded, 16 * N_REST_LOADS)
            dve.tensor_scalar(b_kq[:, 0:H], bias_ps[:, 2 * H:3 * H], qk_b[:, 1:2], None, ALU.add)
            dve.tensor_scalar(b_kq[:, H:2 * H], bias_ps[:, 3 * H:4 * H], qk_b[:, 0:1], None, ALU.add)\
                .then_inc(bias_ready, 1)
            dve.wait_ge(bias_ready, 1)
            keys(0)
            key_max(0)
            key_shift(0)
            dve.wait_ge(setup_filled, FIRST_COPIES + 1)
            dve.tensor_tensor(b_out[:, :], bout_ps, b_out[:, :], ALU.add).then_inc(bias_ready, 1)
            score_tiles(0, 0, 0)

            def frame(b, parity, prev, next_):
                L = b - 1
                if isinstance(b, int) and b == 1:
                    dve.wait_ge(bias_late_ready, 3)
                    dve.wait_ge(taps_split, TAP_JOBS)
                for h, following in steps(b, prev, next_):
                    after_kernel = prev and h == 4
                    if following:
                        fb, fh = following
                        fp = parity if fh else 1 - parity
                        if fh not in SCALED_BY_ACT:
                            scale_values(fb, fp, fh)
                        if after_kernel:
                            conv_lo_part(L, 0)
                        else:
                            score_tiles(fb, fp, fh)
                    if after_kernel:
                        for m in range(1, T):
                            kernel_tile(L, 1 - parity, m)
                    if prev and h == 6:
                        gate_hidden(L)
                    if next_ and h == 5:
                        key_shift(b + 1)
                    add_head(b, h)
                    if prev:
                        if h == 0:
                            first_output(L, 1 - parity)
                        elif h == 1:
                            wait(dve, out_stored, 16 * L)
                            normalise(1, L, x1, h1)
                        elif h == 2:
                            messages(L)
                            split_features(L)
                            split_conv_in(L)
                        elif h == 3:
                            kernel_tile(L, 1 - parity, 0)
                        elif h == 5:
                            conv_add(L, 1)
                            conv_lo_part(L, 1)
                        elif h == 6:
                            add_gate_n(L)
                            gru(L)
                        elif h == 7:
                            add_out(L)
                    if next_:
                        if h == 3 and prev:
                            first_norm(b + 1, 1 - parity)
                        elif h == 2 and not prev:
                            normalise(0, b + 1, x_in[1 - parity], h0)
                        elif h == 4:
                            keys(b + 1)
                            if after_kernel:
                                score_tiles(b, parity, 5)
                            key_max(b + 1)
                    elif after_kernel:
                        score_tiles(b, parity, 5)
                    if after_kernel:
                        split_nmp(L)
                    if prev and h == 3:
                        conv_add(L, 0)
                    if not prev:
                        if h == 1:
                            late_biases()
                            split_w_ih()
                            dve.wait_ge(x_loaded, 16 * (b + 2))
                            dve.wait_ge(y_ready, b + 1)
                            moments(0, b + 1, x_in[1 - parity])
                        elif 3 <= h < 3 + TAP_JOBS:
                            split_taps(h - 3)

            frames(dve, frame)
            L = LAST
            for part in range(2):
                first_output(L, 1, part)
            dve.wait_ge(out_stored, 16 * L)
            for part in range(2):
                normalise(1, L, x1, h1, part)
            split_conv_in(L)
            messages(L)
            split_features(L)
            conv_add(L, 0)
            conv_lo_part(L, 0)
            for m in range(T):
                kernel_tile(L, 1, m)
            conv_add(L, 1)
            conv_lo_part(L, 1)
            split_nmp(L)
            gate_hidden(L)
            for part in range(2):
                add_gate_n(L, slot_o, part)
            for part in range(2):
                gru(L, part)
            for part in range(2):
                add_out(L, part)


_INS = ["x", "adj", "L0_gnn_fc_w", "L0_gnn_fc_b", "L0_gnn_q_w", "L0_gnn_q_b", "L0_gnn_k_w", "L0_gnn_k_b",
        "L0_gnn_fp_w", "L0_gnn_fp_b", "L1_gnn_w_se", "L1_gnn_b_se", "L1_gnn_conv1_w", "L1_gnn_bn1_g",
        "L1_gnn_bn1_b", "L1_gnn_bn1_m", "L1_gnn_bn1_v", "L1_gnn_conv2_w", "L1_gnn_bn2_g", "L1_gnn_bn2_b",
        "L1_gnn_bn2_m", "L1_gnn_bn2_v", "L1_gnn_w_msg", "L1_gnn_b_msg", "L1_gnn_w_ih", "L1_gnn_b_ih",
        "L1_gnn_w_hh", "L1_gnn_b_hh"]


def kernel(**inputs):
    import numpy as _np
    import concourse.bacc as _bacc
    from concourse import mybir as _mybir
    from concourse.bass_utils import run_bass_kernel_spmd as _run

    nc = _bacc.Bacc("TRN2", target_bir_lowering=False, num_devices=1)
    arrays, args = {}, []
    for name in _INS:
        a = _np.ascontiguousarray(inputs[name])
        arrays[f"in_{name}_dram"] = a
        args.append(nc.dram_tensor(f"in_{name}_dram", a.shape, _mybir.dt.from_np(a.dtype), kind="ExternalInput").ap())
    shape = arrays["in_x_dram"].shape
    args.append(nc.dram_tensor("out_0_dram", shape, _mybir.dt.float32, kind="ExternalOutput").ap())
    heads = arrays["in_L0_gnn_fc_w_dram"].shape[1] // shape[2]
    args.append(nc.dram_tensor("query_weights_dram", (heads, shape[1]), _mybir.dt.float32, kind="Internal").ap())
    build(nc, *args)
    r = _run(nc, [arrays], core_ids=[0])
    return r.results[0]["out_0_dram"]
```
